# Optimizing a Trainium2 kernel written in Bass

```python
import numpy as np
import jax
import jax.numpy as jnp

def _softmax(x, axis=-1):
    return jax.nn.softmax(x, axis=axis)

def _gelu(x):
    return jax.nn.gelu(x, approximate=True)

def _silu(x):
    return jax.nn.silu(x)

def _sigmoid(x):
    return jax.nn.sigmoid(x)

def _layernorm(x, axis=-1, eps=1e-05):
    m = jnp.mean(x, axis=axis, keepdims=True)
    v = jnp.var(x, axis=axis, keepdims=True)
    return (x - m) / jnp.sqrt(v + eps)

def _scatter_add(tgt, idx, src, axis=0):
    return tgt.at[idx].add(src)

def _segment_sum(src, seg, n):
    return jax.ops.segment_sum(src, seg, n)
kernel_name = 'mk_xattn_ffn_d2_seqx_r8_625401'

def setup_inputs(seed: int=0):
    np.random.seed(seed)
    _w = jnp.asarray

    def _rec_inputs():
        import jax
        import jax.numpy as jnp
        _rk = jax.random.key(seed)
        x = -0.0003929 + 0.9999 * jax.random.normal(jax.random.fold_in(_rk, 1), (8, 56, 256), jnp.float32)
        _lenS = 56 - jax.random.randint(jax.random.fold_in(_rk, 7), (8,), 0, max(1, 56 // 4) + 1, jnp.int32)
        _lenS2 = 1500 - jax.random.randint(jax.random.fold_in(_rk, 8), (8,), 0, max(1, 1500 // 4) + 1, jnp.int32)
        _ctx_1024P = jax.random.normal(jax.random.fold_in(_rk, 11), (8, 16, 128), jnp.float32)
        _ctx_1024c = jax.random.dirichlet(jax.random.fold_in(_rk, 511), 0.3 * jnp.ones((16,), jnp.float32), (8, 1500))
        _ctx_1024t = jnp.einsum('bsk,bkd->bsd', _ctx_1024c, _ctx_1024P)
        _ctx_1024t = _ctx_1024t * jax.lax.rsqrt(jnp.mean(jnp.square(_ctx_1024t)) + 1e-12) * 0.953939
        ctx_1024 = 0.000227908 + 0.99994 * (_ctx_1024t + 0.3 * jax.random.normal(jax.random.fold_in(_rk, 611), (8, 1500, 128), jnp.float32))
        _validS = jnp.arange(56)[None, :] < _lenS[:, None]
        _validS2 = jnp.arange(1500)[None, :] < _lenS2[:, None]
        _causal = jnp.tril(jnp.ones((56, 56), dtype=bool))
        mask_BxS2_bf1 = jnp.ones((8, 1500), dtype=bool)
        return (x, ctx_1024, mask_BxS2_bf1)
    x, ctx_1024, mask_BxS2_bf1 = _rec_inputs()

    def _L0_xattn_setup():
        import jax, jax.numpy as jnp
        import numpy as np
        EPS = 1e-05

        def rmsnorm(x, g, eps=EPS):
            var = jnp.mean(jnp.square(x), axis=-1, keepdims=True)
            return x * jax.lax.rsqrt(var + eps) * g
        key = jax.random.key(seed)
        ks = jax.random.split(key, 8)
        B, Sq, Skv = (2, 512, 64)
        dim, cdim, H, D = (256, 128, 16, 128)
        inner = H * D
        s = lambda f: 1.0 / np.sqrt(f)
        return {'hidden_states': jax.random.normal(ks[0], (B, Sq, dim), jnp.float32), 'encoder_hidden_states': jax.random.normal(ks[1], (B, Skv, cdim), jnp.float32), 'Wq': jax.random.normal(ks[2], (dim, inner), jnp.float32) * s(dim), 'Wk': jax.random.normal(ks[3], (cdim, inner), jnp.float32) * s(cdim), 'Wv': jax.random.normal(ks[4], (cdim, inner), jnp.float32) * s(cdim), 'Wo': jax.random.normal(ks[5], (inner, dim), jnp.float32) * s(inner), 'gq': jnp.ones((D,), jnp.float32), 'gk': jnp.ones((D,), jnp.float32)}
    _L0_xattn_all = _L0_xattn_setup()
    _L0_xattn_in = {k: v for k, v in _L0_xattn_all.items() if k in ('Wq', 'Wk', 'Wv', 'Wo', 'gq', 'gk')}
    del _L0_xattn_all

    def _L0_ffn_setup():
        import jax, jax.numpy as jnp
        import numpy as np
        EPS = 1e-06
        Q_B = 128.0

        def layer_norm(x):
            mean = jnp.mean(x, axis=-1, keepdims=True)
            var = jnp.var(x, axis=-1, keepdims=True)
            return (x - mean) / jnp.sqrt(var + EPS)

        def absmax_quant(x):
            gamma = jnp.max(jnp.abs(x), axis=-1, keepdims=True)
            x_hat = jnp.clip(x * Q_B / gamma, -Q_B + EPS, Q_B - EPS)
            return x_hat * gamma / Q_B

        def ternarize_weights(w):
            gamma = jnp.mean(jnp.abs(w))
            return jnp.sign(jnp.round(w / (gamma + EPS))) * gamma

        def bitlinear(x, w):
            xn = layer_norm(x)
            x_hat = xn + jax.lax.stop_gradient(absmax_quant(xn) - xn)
            w_hat = w + jax.lax.stop_gradient(ternarize_weights(w) - w)
            return jnp.einsum('bsd,od->bso', x_hat, w_hat)
        key = jax.random.key(seed)
        k1, k2, k3 = jax.random.split(key, 3)
        B, S, D = (4, 256, 256)
        x = jax.random.normal(k1, (B, S, D), dtype=jnp.float32)
        w_fc = jax.random.normal(k2, (4 * D, D), dtype=jnp.float32) / np.sqrt(D)
        w_proj = jax.random.normal(k3, (D, 4 * D), dtype=jnp.float32) / np.sqrt(4 * D)
        return {'x': x, 'w_fc': w_fc, 'w_proj': w_proj}
    _L0_ffn_all = _L0_ffn_setup()
    _L0_ffn_in = {k: v for k, v in _L0_ffn_all.items() if k in ('w_fc', 'w_proj')}
    del _L0_ffn_all

    def _L1_xattn_setup():
        import jax, jax.numpy as jnp
        import numpy as np
        N_HEADS = 16
        N_KV_HEADS = 8
        HEAD_DIM = 128
        D_TEXT = 256
        D_VISION = 128
        GROUPS = N_HEADS // N_KV_HEADS
        key = jax.random.key(seed)
        ks = jax.random.split(key, 6)
        B, T_text, T_vis = (4, 256, 72)
        text_hidden = jax.random.normal(ks[0], (B, T_text, D_TEXT), dtype=jnp.float32)
        vision_tokens = jax.random.normal(ks[1], (B, T_vis, D_VISION), dtype=jnp.float32)
        vision_mask = jnp.ones((B, T_vis), dtype=bool)
        s = 0.02
        Wq = jax.random.normal(ks[2], (D_TEXT, N_HEADS * HEAD_DIM), dtype=jnp.float32) * s
        Wk = jax.random.normal(ks[3], (D_VISION, N_KV_HEADS * HEAD_DIM), dtype=jnp.float32) * s
        Wv = jax.random.normal(ks[4], (D_VISION, N_KV_HEADS * HEAD_DIM), dtype=jnp.float32) * s
        Wo = jax.random.normal(ks[5], (N_HEADS * HEAD_DIM, D_TEXT), dtype=jnp.float32) * s
        return {'text_hidden': text_hidden, 'vision_tokens': vision_tokens, 'vision_mask': vision_mask, 'Wq': Wq, 'Wk': Wk, 'Wv': Wv, 'Wo': Wo}
    _L1_xattn_all = _L1_xattn_setup()
    _L1_xattn_in = {k: v for k, v in _L1_xattn_all.items() if k in ('Wq', 'Wk', 'Wv', 'Wo')}
    del _L1_xattn_all

    def _L1_ffn_setup():
        import jax, jax.numpy as jnp
        import numpy as np
        H = 256
        I = 176
        E = 8
        TOP_K = 2
        N_SHARED = 2
        IS = N_SHARED * I
        key = jax.random.key(seed)
        ks = jax.random.split(key, 8)
        s_h = 1.0 / np.sqrt(H)
        s_i = 1.0 / np.sqrt(I)
        s_is = 1.0 / np.sqrt(IS)
        return {'hidden_states': jax.random.normal(ks[0], (1, 256, H), jnp.float32), 'gate_w': jax.random.normal(ks[1], (E, H), jnp.float32) * s_h, 'w_gate': jax.random.normal(ks[2], (E, H, I), jnp.float32) * s_h, 'w_up': jax.random.normal(ks[3], (E, H, I), jnp.float32) * s_h, 'w_down': jax.random.normal(ks[4], (E, I, H), jnp.float32) * s_i, 'sw_gate': jax.random.normal(ks[5], (H, IS), jnp.float32) * s_h, 'sw_up': jax.random.normal(ks[6], (H, IS), jnp.float32) * s_h, 'sw_down': jax.random.normal(ks[7], (IS, H), jnp.float32) * s_is}
    _L1_ffn_all = _L1_ffn_setup()
    _L1_ffn_in = {k: v for k, v in _L1_ffn_all.items() if k in ('gate_w', 'w_gate', 'w_up', 'w_down', 'sw_gate', 'sw_up', 'sw_down')}
    del _L1_ffn_all
    return {'x': x, 'ctx_1024': ctx_1024, 'mask_BxS2_bf1': mask_BxS2_bf1, 'L0_xattn_Wq': _L0_xattn_in['Wq'], 'L0_xattn_Wk': _L0_xattn_in['Wk'], 'L0_xattn_Wv': _L0_xattn_in['Wv'], 'L0_xattn_Wo': _L0_xattn_in['Wo'], 'L0_xattn_gq': _L0_xattn_in['gq'], 'L0_xattn_gk': _L0_xattn_in['gk'], 'L0_ffn_w_fc': _L0_ffn_in['w_fc'], 'L0_ffn_w_proj': _L0_ffn_in['w_proj'], 'L1_xattn_Wq': _L1_xattn_in['Wq'], 'L1_xattn_Wk': _L1_xattn_in['Wk'], 'L1_xattn_Wv': _L1_xattn_in['Wv'], 'L1_xattn_Wo': _L1_xattn_in['Wo'], 'L1_ffn_gate_w': _L1_ffn_in['gate_w'], 'L1_ffn_w_gate': _L1_ffn_in['w_gate'], 'L1_ffn_w_up': _L1_ffn_in['w_up'], 'L1_ffn_w_down': _L1_ffn_in['w_down'], 'L1_ffn_sw_gate': _L1_ffn_in['sw_gate'], 'L1_ffn_sw_up': _L1_ffn_in['sw_up'], 'L1_ffn_sw_down': _L1_ffn_in['sw_down']}

def reference(x, ctx_1024, mask_BxS2_bf1, L0_xattn_Wq, L0_xattn_Wk, L0_xattn_Wv, L0_xattn_Wo, L0_xattn_gq, L0_xattn_gk, L0_ffn_w_fc, L0_ffn_w_proj, L1_xattn_Wq, L1_xattn_Wk, L1_xattn_Wv, L1_xattn_Wo, L1_ffn_gate_w, L1_ffn_w_gate, L1_ffn_w_up, L1_ffn_w_down, L1_ffn_sw_gate, L1_ffn_sw_up, L1_ffn_sw_down):
    import jax
    import jax.numpy as jnp

    def _L0_xattn_ref(hidden_states, encoder_hidden_states, Wq, Wk, Wv, Wo, gq, gk):
        import jax, jax.numpy as jnp
        import numpy as np
        EPS = 1e-05

        def rmsnorm(x, g, eps=EPS):
            var = jnp.mean(jnp.square(x), axis=-1, keepdims=True)
            return x * jax.lax.rsqrt(var + eps) * g
        B, Sq, _ = hidden_states.shape
        Skv = encoder_hidden_states.shape[1]
        D = gq.shape[0]
        H = Wq.shape[1] // D
        scale = 1.0 / np.sqrt(D)
        q = (hidden_states @ Wq).reshape(B, Sq, H, D)
        k = (encoder_hidden_states @ Wk).reshape(B, Skv, H, D)
        v = (encoder_hidden_states @ Wv).reshape(B, Skv, H, D)
        q = rmsnorm(q, gq)
        k = rmsnorm(k, gk)
        scores = jnp.einsum('bqhd,bkhd->bhqk', q, k) * scale
        attn = jax.nn.softmax(scores, axis=-1)
        out = jnp.einsum('bhqk,bkhd->bqhd', attn, v)
        out = out.reshape(B, Sq, H * D)
        return out @ Wo

    def _L0_ffn_ref(x, w_fc, w_proj):
        import jax, jax.numpy as jnp
        import numpy as np
        EPS = 1e-06
        Q_B = 128.0

        def layer_norm(x):
            mean = jnp.mean(x, axis=-1, keepdims=True)
            var = jnp.var(x, axis=-1, keepdims=True)
            return (x - mean) / jnp.sqrt(var + EPS)

        def absmax_quant(x):
            gamma = jnp.max(jnp.abs(x), axis=-1, keepdims=True)
            x_hat = jnp.clip(x * Q_B / gamma, -Q_B + EPS, Q_B - EPS)
            return x_hat * gamma / Q_B

        def ternarize_weights(w):
            gamma = jnp.mean(jnp.abs(w))
            return jnp.sign(jnp.round(w / (gamma + EPS))) * gamma

        def bitlinear(x, w):
            xn = layer_norm(x)
            x_hat = xn + jax.lax.stop_gradient(absmax_quant(xn) - xn)
            w_hat = w + jax.lax.stop_gradient(ternarize_weights(w) - w)
            return jnp.einsum('bsd,od->bso', x_hat, w_hat)
        h = bitlinear(x, w_fc)
        h = jax.nn.gelu(h, approximate=False)
        return bitlinear(h, w_proj)

    def _L1_xattn_ref(text_hidden, vision_tokens, vision_mask, Wq, Wk, Wv, Wo):
        import jax, jax.numpy as jnp
        import numpy as np
        N_HEADS = 16
        N_KV_HEADS = 8
        HEAD_DIM = 128
        D_TEXT = 256
        D_VISION = 128
        GROUPS = N_HEADS // N_KV_HEADS
        B, T_text, _ = text_hidden.shape
        T_vis = vision_tokens.shape[1]
        scale = jnp.float32(np.sqrt(HEAD_DIM))
        q = (text_hidden @ Wq).reshape(B, T_text, N_HEADS, HEAD_DIM).transpose(0, 2, 1, 3)
        k = (vision_tokens @ Wk).reshape(B, T_vis, N_KV_HEADS, HEAD_DIM).transpose(0, 2, 1, 3)
        v = (vision_tokens @ Wv).reshape(B, T_vis, N_KV_HEADS, HEAD_DIM).transpose(0, 2, 1, 3)
        k = jnp.repeat(k, GROUPS, axis=1)
        v = jnp.repeat(v, GROUPS, axis=1)
        scores = jnp.einsum('bhtd,bhsd->bhts', q, k) / scale
        mask = vision_mask[:, None, None, :]
        scores = jnp.where(mask, scores, -jnp.inf)
        attn = jax.nn.softmax(scores, axis=-1)
        attn = jnp.nan_to_num(attn, nan=0.0)
        out = jnp.einsum('bhts,bhsd->bhtd', attn, v)
        out = out.transpose(0, 2, 1, 3).reshape(B, T_text, N_HEADS * HEAD_DIM)
        return out @ Wo

    def _L1_ffn_ref(hidden_states, gate_w, w_gate, w_up, w_down, sw_gate, sw_up, sw_down):
        import jax, jax.numpy as jnp
        import numpy as np
        H = 256
        I = 176
        E = 8
        TOP_K = 2
        N_SHARED = 2
        IS = N_SHARED * I
        B, S, _ = hidden_states.shape
        x = hidden_states.reshape(-1, H)
        N = x.shape[0]
        logits = x @ gate_w.T
        scores = jax.nn.softmax(logits, axis=-1)
        topk_w, topk_i = jax.lax.top_k(scores, TOP_K)
        g = jnp.einsum('nh,ehi->eni', x, w_gate)
        u = jnp.einsum('nh,ehi->eni', x, w_up)
        h = jax.nn.silu(g) * u
        eo = jnp.einsum('eni,eih->enh', h, w_down)
        combine = jnp.zeros((N, E), x.dtype).at[jnp.arange(N)[:, None], topk_i].add(topk_w)
        y = jnp.einsum('ne,enh->nh', combine, eo)
        sh = jax.nn.silu(x @ sw_gate) * (x @ sw_up)
        y = y + sh @ sw_down
        return y.reshape(B, S, H)
    x = x + _L0_xattn_ref(_layernorm(x, axis=-1), ctx_1024, L0_xattn_Wq, L0_xattn_Wk, L0_xattn_Wv, L0_xattn_Wo, L0_xattn_gq, L0_xattn_gk)
    x = x + _L0_ffn_ref(_layernorm(x, axis=-1), L0_ffn_w_fc, L0_ffn_w_proj)
    x = x + _L1_xattn_ref(_layernorm(x, axis=-1), ctx_1024, mask_BxS2_bf1, L1_xattn_Wq, L1_xattn_Wk, L1_xattn_Wv, L1_xattn_Wo)
    x = x + _L1_ffn_ref(_layernorm(x, axis=-1), L1_ffn_gate_w, L1_ffn_w_gate, L1_ffn_w_up, L1_ffn_w_down, L1_ffn_sw_gate, L1_ffn_sw_up, L1_ffn_sw_down)
    return x

_drawn_inputs = setup_inputs


def setup_inputs(seed=0):
    import zlib

    import numpy as np

    out = dict(_drawn_inputs(seed))
    spreads = {'L0_xattn_gq': (1.0, 0.2), 'L0_xattn_gk': (1.0, 0.2)}
    factors = {'L1_xattn_Wq': 8.0, 'L1_xattn_Wk': 8.0}
    for name, (base, spread) in spreads.items():
        noise = np.random.default_rng([zlib.crc32(name.encode()), seed]).standard_normal(out[name].shape)
        drawn = base * np.exp(spread * noise) if base else spread * noise
        out[name] = jnp.asarray(drawn.astype(out[name].dtype))
    for name, factor in factors.items():
        out[name] = (out[name] * factor).astype(out[name].dtype)
    return out
```

```python
from contextlib import ExitStack

import concourse.bass as bass
from concourse import mybir

ALU = mybir.AluOpType
ACT = mybir.ActivationFunctionType
AX = mybir.AxisListType
F32 = mybir.dt.float32
F16 = mybir.dt.float16
U8 = mybir.dt.uint8

B, SQ, DM = 8, 56, 256
SK, CD = 1500, 128
H, HD = 16, 128
KV1 = 8
KP, KT = 125, 12
CW = CD + 1
NT, TP = 4, 112
TOK = NT * TP
KK = DM // 128
HU = 8
QU = HU * SQ
QJ = QU // TP
NU = B * H // HU
SW = KT * QU
FF = 4 * DM
FO = FF // 128
E, EI = 8, 176
IT = 88
NHT = E * EI // IT
NST = 2 * EI // IT
EXPG = 3
NEG = -1.0e30


def wait(eng, sem, value):
    if isinstance(value, int) and value <= 0:
        return
    eng.wait_ge(sem, value)


def build(nc, x, ctx, mask, Wq0, Wk0, Wv0, Wo0, gq, gk, w_fc, w_proj,
          Wq1, Wk1, Wv1, Wo1, gate_w, w_gate, w_up, w_down, sw_gate, sw_up, sw_down, out):
    with ExitStack() as st:
        def sb(name, shape, dt=F32):
            return st.enter_context(nc.sbuf_tensor(name, shape, dt))

        def ps(name, shape, dt=F32):
            return st.enter_context(nc.psum_tensor(name, shape, dt))

        def sem(name):
            return st.enter_context(nc.semaphore(name))

        ctx_flat = sb("ctx_sb", [128, B * KT * CW])[:, :]
        ctx_sb = ctx_flat.rearrange("p (b t c) -> p b t c", b=B, t=KT)
        ctxT_flat = sb("ctxT", [128, 2 * B * KT * KP], F16)[:, :]
        ctxT = ctxT_flat.rearrange("p (l b t n) -> p l b t n", l=2, b=B, t=KT)
        S_flat = sb("S", [128, 2 * SW])[:, :]
        S = S_flat.rearrange("p (r n) -> p r n", r=2)
        qk_flat = sb("qk", [128, B * 2 * 2 * QU], F16)[:, :]
        qk = qk_flat.rearrange("p (b g l n) -> p b g l n", b=B, g=2, l=2)
        acT = qk_flat.bitcast(F32).rearrange("p (b g n) -> p b g n", b=B, g=2)
        wbuf = sb("wbuf", [128, 6144])
        x_sb = sb("x_sb", [TP, NT, DM])
        xn = sb("xn", [TP, NT, DM])
        xnT = sb("xnT", [128, KK, TOK])
        ident = sb("ident", [128, 128])
        ident16 = sb("ident16", [128, 128], F16)
        ones = sb("ones", [128, 128])
        macc = sb("macc", [KP, QU])
        msp = sb("msp", [KP, QU])
        mcol = sb("mcol", [TP, QJ])
        acn = xn[:, 0:2, :].rearrange("p j d -> p (j d)").rearrange("p (j c) -> p j c", c=CD)
        rden = sb("rden", [TP, QJ])
        ssq = sb("ssq", [KP, KT, HU])
        krstd = sb("krstd", [KP, KT, HU])
        mask_u8 = sb("mask_u8", [KP, B, KT], U8)
        mask_f = sb("mask_f", [KP, B, KT])
        mbias = sb("mbias", [KP, B, KT])
        mhalf = sb("mhalf", [128, 1])
        stats = sb("stats", [TP, NT, 2, 6])
        mv = sb("mv", [TP, NT, 2])
        lnv = sb("lnv", [TP, NT])
        lnr = sb("lnr", [TP, NT])
        qss = sb("qss", [TP, HU])
        qvar = sb("qvar", [TP, HU])
        qrstd = sb("qrstd", [TP, HU])
        g2 = sb("g2", [128, 3])
        wsum = sb("wsum", [128, 2])
        gam = sb("gam", [128, 2])
        thr = sb("thr", [128, 2, 2])
        amx = sb("amx", [TP, NT])
        namx = sb("namx", [TP, NT])

        S0, S1 = S[:, 0, :], S[:, 1, :]
        wq_sb = S0[:, 0:KK * H * HD].rearrange("p (k n) -> p k n", k=KK)
        qn = S0[0:TP, 4096:5120]
        wk_sb = S1[:, 2048:4096]
        wk16 = S1[:, 0:2048].bitcast(F16).rearrange("p (l n) -> p l n", l=2)
        sq = S1[:, 2048:4096].rearrange("p (r n) -> p r n", r=2)
        qsq = S1[0:TP, 4096:5120]
        wk1_sb = S1[:, 0:KV1 * HD]
        wkT = wbuf[:, 0:2048].rearrange("p (h c) -> p h c", h=H)
        qT = wbuf[:, 2048:2048 + HU * TOK].rearrange("p (h t) -> p h t", h=HU)
        wv_sb = wbuf[:, 0:2048].rearrange("p (h c) -> p h c", h=H)
        wo_sb = wbuf[:, 2048:6144].rearrange("p (h n) -> p h n", h=H)
        oT = S0[:, 0:2 * TOK].rearrange("p (r t) -> p r t", r=2)
        wfc_sb = S0[:, 0:2048].rearrange("p (o d) -> p o d", o=FO)
        wpj_sb = S0[:, 2048:4096].rearrange("p (o d) -> p o d", o=KK)
        tneg = S1[:, 4096:5120].bitcast(F16)
        t_fc = S1[:, 0:1024].bitcast(F16).rearrange("p (o d) -> p o d", o=FO)
        t_pj = S1[:, 1024:2048].bitcast(F16).rearrange("p (o d) -> p o d", o=KK)
        fcT = S1[:, 2048:3072].bitcast(F16).rearrange("p (k n) -> p k n", k=KK)
        pjT = S1[:, 3072:4096].bitcast(F16).rearrange("p (o n) -> p o n", o=FO)
        zT = S1[:, 4096:4096 + 896].bitcast(F16).rearrange("p (l k t) -> p l k t", l=2, k=KK)
        wabs_out = qk_flat.bitcast(F32)[:, 0:2 * FF * DM // 128].rearrange("p (r n) -> p r n", r=2)
        hbuf = qk_flat.bitcast(F32)[0:TP, 0:NT * FF] \
            .rearrange("p (j n) -> p j n", j=NT)
        hT16 = wbuf[:, 0:3584].bitcast(F16).rearrange("p (l o t) -> p l o t", l=2, o=FO)
        moe = ctxT_flat.bitcast(F32)
        wg_sb = moe[:, 0:2816].rearrange("p (e k i) -> p e k i", e=E, k=KK)
        wu_sb = moe[:, 2816:5632].rearrange("p (e k i) -> p e k i", e=E, k=KK)
        sg_sb = moe[:, 5632:6336].rearrange("p (k i) -> p k i", k=KK)
        su_sb = moe[:, 6336:7040].rearrange("p (k i) -> p k i", k=KK)
        gw_sb = moe[0:E, 7040:7296]
        gwT = moe[:, 7296:7312].rearrange("p (k e) -> p k e", k=KK)
        sil = moe[0:IT, 7400:7400 + 2 * TOK].rearrange("p (r t) -> p r t", r=2)
        lg = moe[0:TP, 8400:8432].rearrange("p (j e) -> p j e", j=NT)
        ex = moe[0:TP, 8432:8464].rearrange("p (j e) -> p j e", j=NT)
        comb = moe[0:TP, 8464:8496].rearrange("p (j e) -> p j e", j=NT)
        rank = moe[0:TP, 8496:8528].rearrange("p (j e) -> p j e", j=NT)
        rmx = moe[0:TP, 8528:8532]
        rsm = moe[0:TP, 8532:8536]
        gt = moe[0:TP, 8600:8856].rearrange("p (j a b) -> p j a b", j=NT, a=E)
        eq = moe[0:TP, 8856:9112].rearrange("p (j a b) -> p j a b", j=NT, a=E)
        tri = moe[0:TP, 9112:9176].rearrange("p (a b) -> p a b", a=E)
        wd_sb = ctx_flat[0:IT, 0:(NHT + NST) * DM] \
            .rearrange("p (n d) -> p n d", d=DM)
        hT = S_flat[0:IT, 0:(NHT + NST) * TOK] \
            .rearrange("p (n t) -> p n t", t=TOK)

        pk = ps("pk", [128, 2, 1024])
        praw = ps("praw", [128, 2, 512])
        pA = ps("pA", [128, 512])
        pB = ps("pB", [128, 512])
        pA16 = pA[:, :].bitcast(F16)
        pB16 = pB[:, :].bitcast(F16)
        bank = [pk[:, 0, 0:512], pk[:, 0, 512:1024], pk[:, 1, 0:512], pk[:, 1, 512:1024]]

        ld_x, ld_g, ld_wk, ld_wq, ld_mask = sem("ld_x"), sem("ld_g"), sem("ld_wk"), sem("ld_wq"), sem("ld_mask")
        ld_ctx = [sem(f"ld_ctx{b}") for b in range(B)]
        ld_wvo = [sem(f"ld_wvo{l}") for l in range(2)]
        ld_ffn, ld_wq1, ld_wk1, ld_moe, ld_wd = sem("ld_ffn"), sem("ld_wq1"), sem("ld_wk1"), sem("ld_moe"), sem("ld_wd")
        idz, consts, chain, pchain = sem("idz"), sem("consts"), sem("chain"), sem("pchain")
        ln_var, ln_rstd, xn_ready, xnT_ps, xnT_ready = (sem("ln_var"), sem("ln_rstd"), sem("xn_ready"),
                                                        sem("xnT_ps"), sem("xnT_ready"))
        ctxT_ps, ctxT_hi, ctxT_lo = sem("ctxT_ps"), sem("ctxT_hi"), sem("ctxT_lo")
        wk_hi, wk_lo, wkT_ps, wkT_ready, g_ready = (sem("wk_hi"), sem("wk_lo"), sem("wkT_ps"),
                                                    sem("wkT_ready"), sem("g_ready"))
        q_ps, q_sq, q_var, q_rstd, qn_ready, qT_ps, qT_ready = (sem("q_ps"), sem("q_sq"), sem("q_var"), sem("q_rstd"),
                                                                sem("qn_ready"), sem("qT_ps"), sem("qT_ready"))
        qk_ps, qk_hi, qk_lo = sem("qk_ps"), sem("qk_hi"), sem("qk_lo")
        k_ps, k_sq, k_red, k_var, k_rstd = sem("k_ps"), sem("k_sq"), sem("k_red"), sem("k_var"), sem("k_rstd")
        mask_ready, ctx_masked = sem("mask_ready"), sem("ctx_masked")

        class Attn:
            def __init__(self, l):
                self.raw = sem(f"raw{l}")
                self.score = sem(f"score{l}")
                self.mstep = sem(f"mstep{l}")
                self.maccT = sem(f"maccT{l}")
                self.mcol = sem(f"mcol{l}")
                self.mbc = sem(f"mbc{l}")
                self.msp = sem(f"msp{l}")
                self.sub = sem(f"sub{l}")
                self.exp = sem(f"exp{l}")
                self.pv = sem(f"pv{l}")
                self.rden = sem(f"rden{l}")
                self.acn = sem(f"acn{l}")
                self.acTps = sem(f"acTps{l}")
                self.ac = sem(f"ac{l}")
                self.oT_ps = sem(f"oT_ps{l}")
                self.oT = sem(f"oT{l}")
                self.y = sem(f"y{l}")
                self.x = sem(f"x{l}")
        at = [Attn(0), Attn(1)]
        wabs, wsum_ps, gam_ready, tern, ternT_ps, ternT = (sem("wabs"), sem("wsum_ps"), sem("gam_ready"),
                                                          sem("tern"), sem("ternT_ps"), sem("ternT"))
        z_ready, zT_ps, zT_hi, zT_lo = sem("z_ready"), sem("zT_ps"), sem("zT_hi"), sem("zT_lo")
        h_ps, h_act, h_ready, hT_ps, hT_hi, hT_lo, f_ps, f_done = (sem("h_ps"), sem("h_act"), sem("h_ready"),
            sem("hT_ps"), sem("hT_hi"), sem("hT_lo"), sem("f_ps"), sem("f_done"))
        gwT_ps, gwT_ready, lg_ps, lg_sub, lg_exp, comb_ready = (sem("gwT_ps"), sem("gwT_ready"), sem("lg_ps"),
            sem("lg_sub"), sem("lg_exp"), sem("comb_ready"))
        gu_ps, silu, moeh, ye_ps, ye_used, tri_ready = (sem("gu_ps"), sem("silu"), sem("moeh"), sem("ye_ps"),
                                                       sem("ye_used"), sem("tri_ready"))
        stored = sem("stored")

        block = st.enter_context(nc.Block())

        @block.sync
        def _(sp):
            xv = x.rearrange("b s d -> (b s) d").rearrange("(j p) d -> p j d", p=TP)
            cv = ctx.rearrange("b (p t) c -> p b t c", t=KT)
            sp.dma_start(x_sb[:, :, :], xv).then_inc(ld_x, 16)
            sp.dma_start(wk_sb, Wk0).then_inc(ld_wk, 16)
            sp.dma_start(ctx_sb[0:KP, 0, :, 0:CD], cv[:, 0]).then_inc(ld_ctx[0], 16)
            sp.dma_start(wq_sb, Wq0.rearrange("(k p) n -> p k n", p=128)).then_inc(ld_wq, 16)
            sp.dma_start(g2[:, 0:1], gq.rearrange("(d a) -> d a", a=1)).then_inc(ld_g, 16)
            sp.dma_start(g2[:, 1:2], gk.rearrange("(d a) -> d a", a=1)).then_inc(ld_g, 16)
            for b in range(1, B):
                sp.dma_start(ctx_sb[0:KP, b, :, 0:CD], cv[:, b]).then_inc(ld_ctx[b], 16)
            sp.dma_start(mask_u8[:, :, :], mask.rearrange("b (p t) -> p b t", t=KT)).then_inc(ld_mask, 16)
            wait(sp, qk_ps, H)
            sp.dma_start(wv_sb, Wv0.rearrange("c (h d) -> c h d", h=H)).then_inc(ld_wvo[0], 16)
            sp.dma_start(wo_sb, Wo0.rearrange("(h d) n -> d h n", h=H)).then_inc(ld_wvo[0], 16)
            wait(sp, at[0].y, 1)
            sp.dma_start(wfc_sb, w_fc.rearrange("(o p) d -> p o d", p=128)).then_inc(ld_ffn, 16)
            sp.dma_start(wpj_sb, w_proj.rearrange("(o p) d -> p o d", p=128)).then_inc(ld_ffn, 16)
            wait(sp, tern, 2)
            sp.dma_start(wq_sb, Wq1.rearrange("(k p) n -> p k n", p=128)).then_inc(ld_wq1, 16)
            wait(sp, ternT_ps, 8)
            sp.dma_start(wk1_sb, Wk1).then_inc(ld_wk1, 16)
            wait(sp, qk_ps, 2 * H)
            sp.dma_start(wv_sb[:, 0:KV1, :], Wv1.rearrange("c (h d) -> c h d", h=KV1)).then_inc(ld_wvo[1], 16)
            sp.dma_start(wo_sb, Wo1.rearrange("(h d) n -> d h n", h=H)).then_inc(ld_wvo[1], 16)
            wait(sp, at[1].raw, NU * KT)
            for e in range(E):
                sp.dma_start(wg_sb[:, e], w_gate[e].rearrange("(k p) i -> p k i", p=128)).then_inc(ld_moe, 16)
                sp.dma_start(wu_sb[:, e], w_up[e].rearrange("(k p) i -> p k i", p=128)).then_inc(ld_moe, 16)
            sp.dma_start(sg_sb, sw_gate.rearrange("(k p) i -> p k i", p=128)).then_inc(ld_moe, 16)
            sp.dma_start(su_sb, sw_up.rearrange("(k p) i -> p k i", p=128)).then_inc(ld_moe, 16)
            sp.dma_start(gw_sb, gate_w).then_inc(ld_moe, 16)
            wait(sp, at[1].pv, 2 * NU)
            sp.dma_start(wd_sb[:, 0:NHT, :], w_down.rearrange("e (a p) d -> p (e a) d", p=IT)).then_inc(ld_wd, 16)
            sp.dma_start(wd_sb[:, NHT:NHT + NST, :], sw_down.rearrange("(a p) d -> p a d", p=IT)).then_inc(ld_wd, 16)
            ov = out.rearrange("b s d -> (b s) d").rearrange("(j p) d -> p j d", p=TP)
            wait(sp, ye_used, NT * (E + 1))
            sp.dma_start(ov, x_sb[:, :, :]).then_inc(stored, 16)
            sp.wait_ge(stored, 16)

        @block.gpsimd
        def _(pool):
            pool.memset(ident[:, :], 0.0).then_inc(idz, 1)
            pool.memset(ident16[:, :], 0.0).then_inc(idz, 1)
            pool.wait_ge(idz, 2)
            for m in (ident, ident16):
                pool.affine_select(out=m[:, :], in_=m[:, :], compare_op=ALU.not_equal, fill=1.0, base=0,
                                   pattern=[[-1, 128]], channel_multiplier=1).then_inc(consts, 1)
            pool.memset(ones[:, :], 1.0).then_inc(consts, 1)
            pool.memset(mhalf[:, :], -0.5).then_inc(consts, 1)
            pool.memset(ctx_sb[0:KP, :, :, CD:CW], 1.0).then_inc(consts, 1)
            pool.wait_ge(consts, 5)

            def ln_pow(n):
                pool.wait_ge(ln_var, n + 1)
                pool.tensor_tensor(lnr[:, :], lnv[:, :], mhalf[0:TP, :].broadcast_to([TP, NT]), ALU.pow).then_inc(ln_rstd, 1)

            ln_pow(0)
            for i in range(2 * NT):
                pool.wait_ge(q_var, i + 1)
                pool.tensor_tensor(qrstd[:, :], qvar[:, :], mhalf[0:TP, :].broadcast_to([TP, HU]), ALU.pow).then_inc(q_rstd, 1)

            def key_pow(u):
                pool.wait_ge(k_var, u + 1)
                pool.tensor_tensor(krstd[:, :, :], ssq[:, :, :], mhalf[0:KP, :].unsqueeze(2).broadcast_to([KP, KT, HU]),
                                   ALU.pow).then_inc(k_rstd, 1)

            def unit0(b, g, last):
                a, u = at[0], 2 * b + g
                pool.wait_ge(a.msp, u + 1)
                for c in range(KT // EXPG):
                    s = S[0:KP, 0, c * EXPG * QU:(c + 1) * EXPG * QU].rearrange("p (t n) -> p t n", t=EXPG)
                    pool.tensor_tensor(s, s, msp[:, :].unsqueeze(1).broadcast_to([KP, EXPG, QU]),
                                       ALU.subtract).then_inc(a.sub, 1)
                if not last:
                    key_pow(u + 1)

            def unit1(b, g):
                if g == 0:
                    pool.tensor_tensor(ctx_sb[0:KP, b, :, :], ctx_sb[0:KP, b, :, :],
                                       mask_f[:, b, :].unsqueeze(2).broadcast_to([KP, KT, CW]),
                                       ALU.mult).then_inc(ctx_masked, 1)

            key_pow(0)
            for g in range(2):
                unit0(0, g, False)
            with pool.Fori(1, B - 1) as b:
                for g in range(2):
                    unit0(b, g, False)
            for g in range(2):
                unit0(B - 1, g, g == 1)
            for n in range(1, 5):
                ln_pow(n)
            pool.wait_ge(mask_ready, 2)
            with pool.Fori(0, B) as b:
                unit1(b, 0)
            pool.wait_ge(at[1].raw, NU * KT)
            pool.memset(tri, 1.0).then_inc(pchain, 1)
            pool.wait_ge(pchain, 1)
            pool.affine_select(out=tri, in_=tri, compare_op=ALU.is_gt, fill=0.0, base=0,
                               pattern=[[1, E], [-1, E]], channel_multiplier=0).then_inc(tri_ready, 1)
            ln_pow(5)

        @block.tensor
        def _(pe):
            def transpose(out_, in_, idn):
                k = in_.shape[0]
                return pe.transpose(out_, in_, idn[0:k, 0:k])

            def stream_T(n, ready, count):
                wait(pe, ready, count)
                for k in range(KK):
                    for j in range(NT):
                        mm = transpose(bank[2 + k][:, j * TP:(j + 1) * TP], xn[:, j, k * 128:(k + 1) * 128], ident)
                    mm.then_inc(xnT_ps, 1)

            pe.wait_ge(consts, 5)
            pe.wait_ge(ld_wk, 16)
            for q in range(4):
                wait(pe, wkT_ready, q - 1)
                for i in range(4):
                    h = 4 * q + i
                    mm = transpose(bank[q % 2][:, i * 128:(i + 1) * 128], wk_sb[:, h * 128:(h + 1) * 128], ident)
                mm.then_inc(wkT_ps, 1)
            def context_T(b):
                pe.wait_ge(ld_ctx[b], 16)
                for q in range(3):
                    n = 3 * b + q
                    wait(pe, ctxT_lo, n - 1)
                    for i in range(4):
                        mm = transpose(praw[:, n % 2, i * KP:(i + 1) * KP], ctx_sb[0:KP, b, 4 * q + i, 0:CD], ident)
                    mm.then_inc(ctxT_ps, 1)
            for b in range(B):
                context_T(b)
            wait(pe, wkT_ready, 4)
            stream_T(0, xn_ready, NT)
            pe.wait_ge(ld_wq, 16)
            pe.wait_ge(xnT_ready, 2)
            pe.wait_ge(ctxT_lo, 3 * B)

            def fold(l, g):
                for i in range(HU):
                    n = l * H + g * HU + i
                    wait(pe, qk_lo, n - 1)
                    h = g * HU + i
                    w = wkT[:, h, :] if l == 0 else wkT[:, h // 2, :]
                    pe.matmul(praw[:, n % 2, 0:TOK], w, qT[:, i, :], start=True, stop=True).then_inc(qk_ps, 1)

            for g in range(2):
                for j in range(NT):
                    i = g * NT + j
                    wait(pe, qn_ready, i - 1)
                    for n in range(2):
                        for k in range(KK):
                            mm = pe.matmul(pk[0:TP, i % 2, n * 512:(n + 1) * 512], xnT[:, k, j * TP:(j + 1) * TP],
                                           wq_sb[:, k, g * 1024 + n * 512:g * 1024 + (n + 1) * 512],
                                           start=(k == 0), stop=(k == KK - 1))
                    mm.then_inc(q_ps, 1)
                    pe.wait_ge(qn_ready, i + 1)
                    for n in range(2):
                        m = 2 * i + n
                        wait(pe, qT_ready, m - 1)
                        pt = pA if n == 0 else pB
                        for r in range(4):
                            hh = 4 * n + r
                            mm = transpose(pt[:, r * TP:(r + 1) * TP], qn[:, hh * 128:(hh + 1) * 128], ident)
                        mm.then_inc(qT_ps, 1)
                pe.wait_ge(qT_ready, 2 * NT * (g + 1))
                fold(0, g)

            def keys(b, g, before=None):
                u = 2 * b + g
                for t in range(KT):
                    if before:
                        before(t)
                    wait(pe, k_sq, u * KT + t - 1)
                    for n in range(2):
                        o = pk[0:KP, t % 2, n * 512:(n + 1) * 512]
                        c0 = g * 1024 + n * 512
                        for i, (lc, lw) in enumerate(((0, 0), (0, 1), (1, 0))):
                            mm = pe.matmul(o, ctxT[:, lc, b, t, :], wk16[:, lw, c0:c0 + 512],
                                           start=(i == 0), stop=(i == 2))
                    mm.then_inc(k_ps, 1)

            def scores(l, b, g, before=None):
                a, u = at[l], 2 * b + g
                for t in range(KT):
                    if before:
                        before(t)
                    wait(pe, a.score, u * KT + t - 1)
                    for i, (lc, lq) in enumerate(((0, 0), (0, 1), (1, 0))):
                        mm = pe.matmul(praw[0:KP, t % 2, 0:QU], ctxT[:, lc, b, t, :], qk[:, b, g, lq, :],
                                       start=(i == 0), stop=(i == 2))
                    mm.then_inc(a.raw, 1)

            def max_T(l, u):
                a = at[l]
                pe.wait_ge(a.mstep, (KT - 1) * (u + 1))
                for j in range(QJ):
                    mm = transpose(pA[0:TP, j * KP:(j + 1) * KP], macc[:, j * TP:(j + 1) * TP], ident)
                mm.then_inc(a.maccT, 1)

            def max_spread(l, u):
                a = at[l]
                pe.wait_ge(a.mcol, u + 1)
                for j in range(QJ):
                    mm = pe.transpose(pA[0:KP, j * TP:(j + 1) * TP], mcol[:, j:j + 1].broadcast_to([TP, KP]),
                                      ident[0:TP, 0:TP])
                mm.then_inc(a.mbc, 1)

            def attend(l, b, g, slot, outs, between=None):
                a, u = at[l], 2 * b + g
                s = S[0:KP, slot, :].rearrange("p (t n) -> p t n", t=KT)
                for c in range(2):
                    for j in range(2):
                        for t in range(KT):
                            if c == 0 and j == 0 and t % EXPG == 0:
                                pe.wait_ge(a.exp, u * (KT // EXPG) + t // EXPG + 1)
                            q = 2 * c + j
                            mm = pe.matmul(outs[c][0:TP, j * CW:(j + 1) * CW], s[:, t, q * TP:(q + 1) * TP],
                                           ctx_sb[0:KP, b, t, :], start=(t == 0), stop=(t == KT - 1))
                    mm.then_inc(a.pv, 1)
                    if c == 0 and between:
                        between()

            def attended_T(l, u):
                a = at[l]
                pe.wait_ge(a.acn, 2 * u + 2)
                wait(pe, a.ac, u)
                for j in range(QJ):
                    mm = transpose(pB[:, j * TP:(j + 1) * TP], acn[:, j, :], ident)
                mm.then_inc(a.acTps, 1)

            pe.wait_ge(wk_lo, 1)
            keys(0, 0)
            pe.wait_ge(qk_lo, H)

            def unit0(b, g, first, last):
                u = 2 * b + g

                def in_scores(t):
                    if t == 6 and not first:
                        attended_T(0, u - 1)
                scores(0, b, g, in_scores)

                def in_keys(t):
                    if t == 7:
                        max_T(0, u)
                    if t == 8:
                        max_spread(0, u)
                if last:
                    max_T(0, u)
                    max_spread(0, u)
                else:
                    bn, gn = (b, 1) if g == 0 else (b + 1, 0)
                    keys(bn, gn, in_keys)
                wait(pe, at[0].ac, u)
                attend(0, b, g, 0, (pB, pA))

            for g in range(2):
                unit0(0, g, g == 0, False)
            with pe.Fori(1, B - 1) as b:
                for g in range(2):
                    unit0(b, g, False, False)
            for g in range(2):
                unit0(B - 1, g, False, g == 1)
            attended_T(0, NU - 1)

            def project(l):
                a = at[l]
                pe.wait_ge(a.ac, NU)
                pe.wait_ge(ld_wvo[l], 32)
                for h in range(H + 1):
                    if h < H:
                        wait(pe, a.oT, h - 1)
                        g, i = h // HU, h % HU
                        w = wv_sb[:, h, :] if l == 0 else wv_sb[:, h // 2, :]
                        pe.matmul(praw[:, h % 2, 0:TOK].rearrange("p (b q) -> p b q", b=B), w,
                                  acT[:, :, g, i * SQ:(i + 1) * SQ],
                                  start=True, stop=True).then_inc(a.oT_ps, 1)
                    if h > 0:
                        pe.wait_ge(a.oT, h)
                        for j in range(NT):
                            mm = pe.matmul(bank[j][0:TP, 0:DM], oT[:, (h - 1) % 2, j * TP:(j + 1) * TP],
                                           wo_sb[:, h - 1, :], start=(h == 1), stop=(h == H))
                mm.then_inc(a.y, 1)
            project(0)

            pe.wait_ge(wabs, 2)
            pe.matmul(pA[:, 0:2], ones[:, :], wsum[:, :], start=True, stop=True).then_inc(wsum_ps, 1)
            pe.wait_ge(tern, 2)
            for q in range(8):
                wait(pe, ternT, q - 1)
                pt = pA16 if q % 2 == 0 else pB16
                for i in range(4):
                    if q < 4:
                        src = t_fc[:, 4 * (q % 2) + i, (q // 2) * 128:(q // 2 + 1) * 128]
                    else:
                        o = 2 * (q - 4) + i // 2
                        src = t_pj[:, i % 2, o * 128:(o + 1) * 128]
                    mm = transpose(pt[:, i * 128:(i + 1) * 128], src, ident16)
                mm.then_inc(ternT_ps, 1)
            pe.wait_ge(at[0].x, NT)
            stream_T(1, z_ready, NT)
            pe.wait_ge(ternT, 8)
            pe.wait_ge(zT_lo, 2)
            for j in range(NT):
                wait(pe, h_act, j - 1)
                for n in range(2):
                    i = 0
                    for k in range(KK):
                        for l in range(2):
                            mm = pe.matmul(pk[0:TP, j % 2, n * 512:(n + 1) * 512], zT[:, l, k, j * TP:(j + 1) * TP],
                                           fcT[:, k, n * 512:(n + 1) * 512], start=(i == 0), stop=(i == 3))
                            i += 1
                mm.then_inc(h_ps, 1)
            for o in range(FO):
                wait(pe, hT_lo, o - 1)
                pe.wait_ge(h_ready, NT)
                for j in range(NT):
                    mm = transpose(praw[:, o % 2, j * TP:(j + 1) * TP], hbuf[:, j, o * 128:(o + 1) * 128], ident)
                mm.then_inc(hT_ps, 1)
            pe.wait_ge(hT_lo, FO)
            for j in range(NT):
                for o in range(FO):
                    for l in range(2):
                        mm = pe.matmul(bank[j][0:TP, 0:DM], hT16[:, l, o, j * TP:(j + 1) * TP], pjT[:, o, :],
                                       start=(o == 0 and l == 0), stop=(o == FO - 1 and l == 1))
                mm.then_inc(f_ps, 1)

            pe.wait_ge(ld_wk1, 16)
            for q in range(2):
                for i in range(4):
                    h = 4 * q + i
                    mm = transpose((pA if q == 0 else pB)[:, i * 128:(i + 1) * 128],
                                   wk1_sb[:, h * 128:(h + 1) * 128], ident)
                mm.then_inc(wkT_ps, 1)
            pe.wait_ge(f_done, NT)
            stream_T(2, xn_ready, 2 * NT)
            pe.wait_ge(xnT_ready, 4)
            pe.wait_ge(ld_wq1, 16)
            for g in range(2):
                if g == 1:
                    pe.wait_ge(qk_ps, H + HU)
                for i in range(HU):
                    m = g * HU + i
                    wait(pe, qT_ready, 16 + m - 1)
                    for k in range(KK):
                        h = g * HU + i
                        mm = pe.matmul(bank[m % 2][:, 0:TOK], wq_sb[:, k, h * 128:(h + 1) * 128], xnT[:, k, :],
                                       start=(k == 0), stop=(k == KK - 1))
                    mm.then_inc(qT_ps, 1)
                pe.wait_ge(qT_ready, 16 + HU * (g + 1))
                pe.wait_ge(wkT_ready, 6)
                fold(1, g)
            pe.wait_ge(qk_lo, 2 * H)
            pe.wait_ge(qT_ready, 16 + H)

            def unit1(b, g, first, last):
                u = 2 * b + g
                if not last:
                    bn, gn = (b, 1) if g == 0 else (b + 1, 0)

                    def in_scores(t):
                        if t == 8 and not first:
                            attended_T(1, u - 1)
                    scores(1, bn, gn, in_scores)
                elif not first:
                    attended_T(1, u - 1)

                def between():
                    if not last:
                        max_T(1, u + 1)
                if g == 0:
                    pe.wait_ge(ctx_masked, b + 1)
                attend(1, b, g, g, (bank[0], bank[1]), between)
                if not last:
                    max_spread(1, u + 1)
            scores(1, 0, 0)
            max_T(1, 0)
            max_spread(1, 0)
            for g in range(2):
                unit1(0, g, g == 0, False)
            with pe.Fori(1, B - 1) as b:
                for g in range(2):
                    unit1(b, g, False, False)
            for g in range(2):
                unit1(B - 1, g, False, g == 1)
            attended_T(1, NU - 1)
            project(1)

            pe.wait_ge(ld_moe, 16 * (2 * E + 3))
            for k in range(KK):
                mm = transpose(pA[:, k * E:(k + 1) * E], gw_sb[:, k * 128:(k + 1) * 128], ident)
            mm.then_inc(gwT_ps, 1)
            pe.wait_ge(at[1].x, NT)
            stream_T(3, xn_ready, 3 * NT)
            pe.wait_ge(xnT_ready, 6)
            pe.wait_ge(gwT_ready, 1)
            for j in range(NT):
                for k in range(KK):
                    mm = pe.matmul(pB[0:TP, j * E:(j + 1) * E], xnT[:, k, j * TP:(j + 1) * TP], gwT[:, k, :],
                                   start=(k == 0), stop=(k == KK - 1))
            mm.then_inc(lg_ps, 1)
            for n in range(NHT + NST):
                wait(pe, moeh, n - 1)
                for wi, (we, ws) in enumerate(((wg_sb, sg_sb), (wu_sb, su_sb))):
                    for k in range(KK):
                        if n < NHT:
                            w = we[:, n // 2, k, (n % 2) * IT:(n % 2 + 1) * IT]
                        else:
                            w = ws[:, k, (n - NHT) * IT:(n - NHT + 1) * IT]
                        mm = pe.matmul(bank[2 * (n % 2) + wi][0:IT, 0:TOK], w, xnT[:, k, :],
                                       start=(k == 0), stop=(k == KK - 1))
                mm.then_inc(gu_ps, 1)
            pe.wait_ge(ld_wd, 32)
            pe.wait_ge(moeh, NHT + NST)
            i = 0
            for j in range(NT):
                for e in range(E + 1):
                    wait(pe, ye_used, i - 1)
                    tiles = range(2 * e, 2 * e + 2) if e < E else range(NHT, NHT + NST)
                    for n in tiles:
                        mm = pe.matmul(praw[0:TP, i % 2, 0:DM], hT[:, n, j * TP:(j + 1) * TP], wd_sb[:, n, :],
                                       start=(n == tiles[0]), stop=(n == tiles[-1]))
                    mm.then_inc(ye_ps, 1)
                    i += 1

        @block.scalar
        def _(act):
            act.wait_ge(ld_wk, 16)
            act.activation(wk16[:, 0, :], wk_sb, ACT.Copy, scale=16.0).then_inc(wk_hi, 1)

            for n in range(3 * B):
                b, q = n // 3, n % 3
                act.wait_ge(ctxT_ps, n + 1)
                act.activation(ctxT[:, 0, b, 4 * q:4 * q + 4, :].rearrange("p t n -> p (t n)"),
                               praw[:, n % 2, 0:4 * KP], ACT.Copy).then_inc(ctxT_hi, 1)

            def stream_copy(n):
                for k in range(KK):
                    act.wait_ge(xnT_ps, KK * n + k + 1)
                    act.activation(xnT[:, k, :], bank[2 + k][:, 0:TOK], ACT.Copy).then_inc(xnT_ready, 1)
            stream_copy(0)

            def fold_hi(l, g):
                for i in range(HU):
                    n = l * H + g * HU + i
                    act.wait_ge(qk_ps, n + 1)
                    act.activation(qk[:, :, g, 0, i * SQ:(i + 1) * SQ],
                                   praw[:, n % 2, 0:TOK].rearrange("p (b q) -> p b q", b=B),
                                   ACT.Copy).then_inc(qk_hi, 1)

            for g in range(2):
                for j in range(NT):
                    i = g * NT + j
                    act.wait_ge(q_ps, i + 1)
                    wait(act, q_var, i)
                    act.activation(qsq, pk[0:TP, i % 2, :], ACT.Square).then_inc(q_sq, 1)
                    for n in range(2):
                        m = 2 * i + n
                        act.wait_ge(qT_ps, m + 1)
                        if g == 1 and j == 0 and n == 0:
                            act.wait_ge(qk_ps, HU)
                        pt = pA if n == 0 else pB
                        act.activation(qT[:, 4 * n:4 * n + 4, j * TP:(j + 1) * TP],
                                       pt[:, 0:4 * TP].rearrange("p (h t) -> p h t", h=4),
                                       ACT.Copy).then_inc(qT_ready, 1)
                fold_hi(0, g)

            def square(u, t):
                act.wait_ge(k_ps, u * KT + t + 1)
                wait(act, k_red, u * KT + t - 1)
                act.activation(sq[0:KP, t % 2, :], pk[0:KP, t % 2, :], ACT.Square).then_inc(k_sq, 1)

            def exps(l, u, slot, c):
                a = at[l]
                act.wait_ge(a.sub, u * (KT // EXPG) + c + 1)
                s = S[0:KP, slot, c * EXPG * QU:(c + 1) * EXPG * QU]
                act.activation(s, s, ACT.Exp).then_inc(a.exp, 1)

            def copy_max(u):
                act.wait_ge(at[0].mbc, u + 1)
                act.activation(msp[:, :], pA[0:KP, 0:QU], ACT.Copy).then_inc(at[0].msp, 1)

            def store_ac(l, b, g):
                a, u = at[l], 2 * b + g
                act.wait_ge(a.acTps, u + 1)
                act.activation(acT[:, b, g, :], pB[:, 0:QU], ACT.Copy).then_inc(a.ac, 1)

            act.wait_ge(wkT_ps, 4)
            act.wait_ge(wk_lo, 1)
            for t in range(KT):
                square(0, t)

            def unit0(b, g, first, last):
                u = 2 * b + g
                if not first:
                    bp, gp = (b, 0) if g == 1 else (b - 1, 1)
                    store_ac(0, bp, gp)
                if last:
                    copy_max(u)
                    for c in range(KT // EXPG):
                        exps(0, u, 0, c)
                else:
                    for t in range(KT):
                        square(u + 1, t)
                        if t == 7:
                            copy_max(u)
                    for c in range(KT // EXPG):
                        exps(0, u, 0, c)
            for g in range(2):
                unit0(0, g, g == 0, False)
            with act.Fori(1, B - 1) as b:
                for g in range(2):
                    unit0(b, g, False, False)
            for g in range(2):
                unit0(B - 1, g, False, g == 1)
            store_ac(0, B - 1, 1)

            def project(l):
                a = at[l]
                for h in range(H):
                    act.wait_ge(a.oT_ps, h + 1)
                    act.activation(oT[:, h % 2, :], praw[:, h % 2, 0:TOK], ACT.Copy).then_inc(a.oT, 1)
            project(0)

            act.wait_ge(ld_ffn, 32)
            for i, w in enumerate((wfc_sb, wpj_sb)):
                act.activation(wabs_out[:, i, :], w.rearrange("p o d -> p (o d)"), ACT.Abs,
                               accum_out=wsum[:, i:i + 1]).then_inc(wabs, 1)
            for k in range(KK):
                act.wait_ge(xnT_ps, KK + k + 1)
                act.activation(zT[:, 0, k, :], bank[2 + k][:, 0:TOK], ACT.Copy).then_inc(zT_hi, 1)
            act.wait_ge(gam_ready, 1)
            for j in range(NT):
                act.wait_ge(h_ps, j + 1)
                act.activation(hbuf[:, j, :], pk[0:TP, j % 2, :], ACT.Gelu, scale=gam[0:TP, 0:1]).then_inc(h_act, 1)
            for o in range(FO):
                act.wait_ge(hT_ps, o + 1)
                act.activation(hT16[:, 0, o, :], praw[:, o % 2, 0:TOK], ACT.Copy).then_inc(hT_hi, 1)

            for k in range(KK):
                act.wait_ge(xnT_ps, 2 * KK + k + 1)
                act.activation(xnT[:, k, :], bank[2 + k][:, 0:TOK], ACT.Copy).then_inc(xnT_ready, 1)
            for g in range(2):
                for i in range(HU):
                    m = g * HU + i
                    act.wait_ge(qT_ps, 16 + m + 1)
                    if g == 1 and i == 0:
                        act.wait_ge(qk_ps, H + HU)
                    act.activation(qT[:, i, :], bank[m % 2][:, 0:TOK], ACT.Copy).then_inc(qT_ready, 1)
                fold_hi(1, g)

            def scale_scores(b, g):
                a, u = at[1], 2 * b + g
                s = S[0:KP, g, :].rearrange("p (t n) -> p t n", t=KT)
                for t in range(KT):
                    act.wait_ge(a.raw, u * KT + t + 1)
                    act.activation(s[:, t, :], praw[0:KP, t % 2, 0:QU], ACT.Identity, bias=mbias[:, b, t:t + 1],
                                   scale=float(HD) ** -0.5).then_inc(a.score, 1)

            def unit1(b, g, first, last):
                u = 2 * b + g
                for c in range(KT // EXPG):
                    exps(1, u, g, c)
                if not last:
                    bn, gn = (b, 1) if g == 0 else (b + 1, 0)
                    wait(act, at[1].pv, 2 * u)
                    scale_scores(bn, gn)
                if not first:
                    bp, gp = (b, 0) if g == 1 else (b - 1, 1)
                    store_ac(1, bp, gp)
            act.wait_ge(mask_ready, 2)
            scale_scores(0, 0)
            for g in range(2):
                unit1(0, g, g == 0, False)
            with act.Fori(1, B - 1) as b:
                for g in range(2):
                    unit1(b, g, False, False)
            for g in range(2):
                unit1(B - 1, g, False, g == 1)
            store_ac(1, B - 1, 1)
            project(1)

            for k in range(KK):
                act.wait_ge(xnT_ps, 3 * KK + k + 1)
                act.activation(xnT[:, k, :], bank[2 + k][:, 0:TOK], ACT.Copy).then_inc(xnT_ready, 1)
            act.wait_ge(lg_sub, 1)
            act.activation(ex, lg, ACT.Exp).then_inc(lg_exp, 1)
            for n in range(NHT + NST):
                act.wait_ge(gu_ps, n + 1)
                wait(act, moeh, n - 1)
                act.activation(sil[:, n % 2, :], bank[2 * (n % 2)][0:IT, 0:TOK], ACT.Silu).then_inc(silu, 1)

        @block.vector
        def _(dve):
            links = [0]

            def link(ins):
                links[0] += 1
                ins.then_inc(chain, 1)
                dve.wait_ge(chain, links[0])

            def normalise(n, src, dst, eps, ready):
                for j in range(NT):
                    s = dve.bn_stats(stats[:, j, 0, :], src[:, j, :])
                link(s)
                for j in range(NT):
                    s = dve.bn_aggr(mv[:, j, :], stats[:, j, 0, :])
                link(s)
                dve.tensor_scalar(lnv[:, :], mv[:, :, 1], eps, None, ALU.add).then_inc(ln_var, 1)
                dve.wait_ge(ln_rstd, n + 1)
                for j in range(NT):
                    s = dve.tensor_scalar(dst[:, j, :], src[:, j, :], mv[:, j, 0:1], lnr[:, j:j + 1],
                                          ALU.subtract, ALU.mult)
                    if ready is not None:
                        s.then_inc(ready, 1)
                if ready is None:
                    link(s)

            dve.wait_ge(ld_x, 16)
            normalise(0, x_sb, xn, 1e-5, xn_ready)
            dve.wait_ge(ld_g, 32)
            dve.tensor_tensor(g2[:, 2:3], g2[:, 0:1], g2[:, 1:2], ALU.mult).then_inc(g_ready, 1)
            dve.wait_ge(g_ready, 1)
            for q in range(4):
                dve.wait_ge(wkT_ps, q + 1)
                dve.tensor_scalar(wkT[:, 4 * q:4 * q + 4, :], bank[q % 2].rearrange("p (h c) -> p h c", h=4),
                                  g2[:, 2:3], None, ALU.mult).then_inc(wkT_ready, 1)
            dve.wait_ge(wk_hi, 1)
            dve.scalar_tensor_tensor(out=wk16[:, 1, :], in0=wk_sb, scalar=16.0, in1=wk16[:, 0, :],
                                     op0=ALU.mult, op1=ALU.subtract).then_inc(wk_lo, 1)
            for n in range(3 * B):
                b, q = n // 3, n % 3
                dve.wait_ge(ctxT_hi, n + 1)
                dve.tensor_tensor(ctxT[:, 1, b, 4 * q:4 * q + 4, :].rearrange("p t n -> p (t n)"),
                                  praw[:, n % 2, 0:4 * KP],
                                  ctxT[:, 0, b, 4 * q:4 * q + 4, :].rearrange("p t n -> p (t n)"),
                                  ALU.subtract).then_inc(ctxT_lo, 1)
            dve.wait_ge(ld_mask, 16)
            dve.tensor_copy(mask_f[:, :, :], mask_u8[:, :, :]).then_inc(mask_ready, 1)
            dve.wait_ge(mask_ready, 1)
            dve.tensor_scalar(mbias[:, :, :], mask_f[:, :, :], -NEG, NEG, ALU.mult, ALU.add).then_inc(mask_ready, 1)

            def fold_lo(l, g):
                for i in range(HU):
                    n = l * H + g * HU + i
                    dve.wait_ge(qk_hi, n + 1)
                    dve.tensor_tensor(qk[:, :, g, 1, i * SQ:(i + 1) * SQ],
                                      praw[:, n % 2, 0:TOK].rearrange("p (b q) -> p b q", b=B),
                                      qk[:, :, g, 0, i * SQ:(i + 1) * SQ], ALU.subtract).then_inc(qk_lo, 1)

            for g in range(2):
                for j in range(NT):
                    i = g * NT + j
                    dve.wait_ge(q_sq, i + 1)
                    link(dve.tensor_reduce(qss[:, :], qsq.rearrange("p (h d) -> p h d", h=HU), AX.X, ALU.add))
                    dve.tensor_scalar(qvar[:, :], qss[:, :], 1.0 / HD, 1e-5, ALU.mult, ALU.add).then_inc(q_var, 1)
                    dve.wait_ge(q_rstd, i + 1)
                    wait(dve, qT_ps, 2 * i)
                    dve.tensor_tensor(qn.rearrange("p (h d) -> p h d", h=HU),
                                      pk[0:TP, i % 2, :].rearrange("p (h d) -> p h d", h=HU),
                                      qrstd[:, :].unsqueeze(2).broadcast_to([TP, HU, HD]),
                                      ALU.mult).then_inc(qn_ready, 1)
                fold_lo(0, g)

            def key_sum(u, t):
                dve.wait_ge(k_sq, u * KT + t + 1)
                dve.tensor_reduce(ssq[:, t, :], sq[0:KP, t % 2, :].rearrange("p (h d) -> p h d", h=HU),
                                  AX.X, ALU.add).then_inc(k_red, 1)

            def key_var(u):
                dve.wait_ge(k_red, KT * (u + 1))
                dve.tensor_scalar(ssq[:, :, :], ssq[:, :, :], 1.0 / 256.0, HD * 1e-5, ALU.mult,
                                  ALU.add).then_inc(k_var, 1)

            def max_step(l, u, slot, t):
                a = at[l]
                s = S[0:KP, slot, :].rearrange("p (t n) -> p t n", t=KT)
                dve.wait_ge(a.score, u * KT + t + 1)
                if t > 1:
                    dve.wait_ge(a.mstep, u * (KT - 1) + t - 1)
                else:
                    wait(dve, a.maccT, u)
                dve.tensor_tensor(macc[:, :], s[:, 0, :] if t == 1 else macc[:, :], s[:, t, :],
                                  ALU.max).then_inc(a.mstep, 1)

            def max_col(l, u):
                a = at[l]
                dve.wait_ge(a.maccT, u + 1)
                dve.tensor_reduce(mcol[:, :], pA[0:TP, 0:QJ * KP].rearrange("p (j s) -> p j s", j=QJ), AX.X,
                                  ALU.max).then_inc(a.mcol, 1)

            def subtract(l, u, slot, c):
                a = at[l]
                if c == 0:
                    dve.wait_ge(a.mbc, u + 1)
                s = S[0:KP, slot, c * EXPG * QU:(c + 1) * EXPG * QU].rearrange("p (t n) -> p t n", t=EXPG)
                dve.tensor_tensor(s, s, pA[0:KP, 0:QU].unsqueeze(1).broadcast_to([KP, EXPG, QU]),
                                  ALU.subtract).then_inc(a.sub, 1)

            def finish(l, u, outs):
                a = at[l]
                for c in range(2):
                    dve.wait_ge(a.pv, 2 * u + c + 1)
                    v = outs[c][0:TP, 0:2 * CW].rearrange("p (j c) -> p j c", j=2)
                    if c == 0:
                        wait(dve, a.acTps, u)
                    r = rden[:, 2 * c:2 * c + 2]
                    dve.tensor_scalar(r, v[:, :, CD], 1e-30, None, ALU.max).then_inc(a.rden, 1)
                    dve.wait_ge(a.rden, 4 * u + 2 * c + 1)
                    dve.reciprocal(r, r).then_inc(a.rden, 1)
                    dve.wait_ge(a.rden, 4 * u + 2 * c + 2)
                    dve.tensor_tensor(acn[:, 2 * c:2 * c + 2, :], v[:, :, 0:CD],
                                      r.unsqueeze(2).broadcast_to([TP, 2, CD]), ALU.mult).then_inc(a.acn, 1)

            for t in range(KT):
                key_sum(0, t)
            key_var(0)

            def unit0(b, g, first, last):
                a, u = at[0], 2 * b + g
                s = S[0:KP, 0, :].rearrange("p (t h q) -> p t h q", t=KT, h=HU)
                dve.wait_ge(k_rstd, u + 1)
                if first:
                    dve.wait_ge(qT_ps, 4 * NT)
                for t in range(KT):
                    dve.wait_ge(a.raw, u * KT + t + 1)
                    dve.tensor_tensor(s[:, t, :, :], praw[0:KP, t % 2, 0:QU].rearrange("p (h q) -> p h q", h=HU),
                                      krstd[:, t, :].unsqueeze(2).broadcast_to([KP, HU, SQ]),
                                      ALU.mult).then_inc(a.score, 1)
                if last:
                    for t in range(1, KT):
                        max_step(0, u, 0, t)
                    max_col(0, u)
                else:
                    for t in range(KT):
                        for m in (2 * t + 1, 2 * t + 2):
                            if m < KT:
                                max_step(0, u, 0, m)
                        key_sum(u + 1, t)
                        if t == 6:
                            max_col(0, u)
                    key_var(u + 1)
                finish(0, u, (pB, pA))
            for g in range(2):
                unit0(0, g, g == 0, False)
            with dve.Fori(1, B - 1) as b:
                for g in range(2):
                    unit0(b, g, False, False)
            for g in range(2):
                unit0(B - 1, g, False, g == 1)

            def residual(l):
                dve.wait_ge(at[l].y, 1)
                for j in range(NT):
                    dve.tensor_tensor(x_sb[:, j, :], bank[j][0:TP, 0:DM], x_sb[:, j, :],
                                      ALU.add).then_inc(at[l].x, 1)
                dve.wait_ge(at[l].x, NT)
            residual(0)

            dve.wait_ge(wsum_ps, 1)
            inv = 1.0 / float(FF * DM)
            dve.tensor_scalar(gam[:, :], pA[:, 0:2], inv, None, ALU.mult).then_inc(gam_ready, 1)
            dve.wait_ge(gam_ready, 1)
            dve.tensor_scalar(thr[:, 0, :], gam[:, :], 1e-6, 0.5, ALU.add, ALU.mult)
            link(dve.tensor_scalar(thr[:, 1, :], gam[:, :], 1e-6, -0.5, ALU.add, ALU.mult))
            for i, (w, tt) in enumerate(((wfc_sb, t_fc), (wpj_sb, t_pj))):
                w2, t2 = w.rearrange("p o d -> p (o d)"), tt.rearrange("p o d -> p (o d)")
                wait(dve, tern, i)
                link(dve.tensor_scalar(tneg, w2, thr[:, 1, i:i + 1], None, ALU.is_lt))
                dve.scalar_tensor_tensor(out=t2, in0=w2, scalar=thr[:, 0, i:i + 1], in1=tneg,
                                         op0=ALU.is_gt, op1=ALU.subtract).then_inc(tern, 1)
            for q in range(8):
                dve.wait_ge(ternT_ps, q + 1)
                pt = (pA16 if q % 2 == 0 else pB16)[:, 0:512]
                if q < 4:
                    dve.tensor_copy(fcT[:, q // 2, 512 * (q % 2):512 * (q % 2) + 512], pt).then_inc(ternT, 1)
                else:
                    dve.tensor_copy(pjT[:, 2 * (q - 4):2 * (q - 4) + 2, :],
                                    pt.rearrange("p (o n) -> p o n", o=2)).then_inc(ternT, 1)

            def clip_absmax(src, j, ready):
                dve.tensor_scalar(src[:, j, :], src[:, j, :], amx[:, j:j + 1], namx[:, j:j + 1],
                                  ALU.min, ALU.max).then_inc(ready, 1)

            def absmax(src):
                for j in range(NT):
                    dve.tensor_reduce(amx[:, j:j + 1], src[:, j, :], AX.X, ALU.max)
                    s = dve.tensor_reduce(namx[:, j:j + 1], src[:, j, :], AX.X, ALU.min)
                link(s)
                link(dve.scalar_tensor_tensor(out=namx[:, :], in0=amx[:, :], scalar=-1.0, in1=namx[:, :],
                                              op0=ALU.mult, op1=ALU.min))
                link(dve.tensor_scalar(amx[:, :], namx[:, :], -1.0, None, ALU.mult))

            normalise(1, x_sb, xn, 1e-5, None)
            normalise(2, xn, xn, 1e-6, None)
            absmax(xn)
            for j in range(NT):
                clip_absmax(xn, j, z_ready)
            for k in range(KK):
                dve.wait_ge(zT_hi, k + 1)
                dve.tensor_tensor(zT[:, 1, k, :], bank[2 + k][:, 0:TOK], zT[:, 0, k, :],
                                  ALU.subtract).then_inc(zT_lo, 1)
            for j in range(NT):
                dve.wait_ge(h_act, j + 1)
                for n in range(2):
                    s = dve.bn_stats(stats[:, j, n, :], hbuf[:, j, n * 512:(n + 1) * 512])
            link(s)
            for j in range(NT):
                s = dve.bn_aggr(mv[:, j, :], stats[:, j, :, :])
            link(s)
            dve.tensor_scalar(lnv[:, :], mv[:, :, 1], 1e-6, None, ALU.add).then_inc(ln_var, 1)
            dve.wait_ge(ln_rstd, 4)
            for j in range(NT):
                s = dve.tensor_scalar(hbuf[:, j, :], hbuf[:, j, :], mv[:, j, 0:1], lnr[:, j:j + 1],
                                      ALU.subtract, ALU.mult)
            link(s)
            absmax(hbuf)
            for j in range(NT):
                clip_absmax(hbuf, j, h_ready)
            for o in range(FO):
                dve.wait_ge(hT_hi, o + 1)
                dve.tensor_tensor(hT16[:, 1, o, :], praw[:, o % 2, 0:TOK], hT16[:, 0, o, :],
                                  ALU.subtract).then_inc(hT_lo, 1)
            for j in range(NT):
                dve.wait_ge(f_ps, j + 1)
                dve.scalar_tensor_tensor(out=x_sb[:, j, :], in0=bank[j][0:TP, 0:DM], scalar=gam[0:TP, 1:2],
                                         in1=x_sb[:, j, :], op0=ALU.mult, op1=ALU.add).then_inc(f_done, 1)
            dve.wait_ge(f_done, NT)

            for q in range(2):
                dve.wait_ge(wkT_ps, 5 + q)
                dve.tensor_copy(wkT[:, 4 * q:4 * q + 4, :],
                                (pA if q == 0 else pB)[:, :].rearrange("p (h c) -> p h c", h=4)).then_inc(wkT_ready, 1)
            normalise(4, x_sb, xn, 1e-5, xn_ready)
            for g in range(2):
                fold_lo(1, g)

            def unit1(b, g, first, last):
                u = 2 * b + g
                if first:
                    for t in range(1, KT):
                        max_step(1, 0, 0, t)
                    max_col(1, 0)
                for c in range(KT // EXPG):
                    subtract(1, u, g, c)
                if not last:
                    for t in range(1, KT):
                        max_step(1, u + 1, 1 - g, t)
                    max_col(1, u + 1)
                finish(1, u, (bank[0], bank[1]))
            for g in range(2):
                unit1(0, g, g == 0, False)
            with dve.Fori(1, B - 1) as b:
                for g in range(2):
                    unit1(b, g, False, False)
            for g in range(2):
                unit1(B - 1, g, False, g == 1)
            residual(1)

            normalise(5, x_sb, xn, 1e-5, xn_ready)
            dve.wait_ge(gwT_ps, 1)
            dve.tensor_copy(gwT, pA[:, 0:KK * E].rearrange("p (k e) -> p k e", k=KK)).then_inc(gwT_ready, 1)
            dve.wait_ge(lg_ps, 1)
            pl = pB[0:TP, 0:NT * E].rearrange("p (j e) -> p j e", j=NT)
            link(dve.tensor_reduce(rmx, pl, AX.X, ALU.max))
            dve.tensor_tensor(lg, pl, rmx.unsqueeze(2).broadcast_to([TP, NT, E]), ALU.subtract).then_inc(lg_sub, 1)
            dve.wait_ge(lg_exp, 1)
            link(dve.tensor_reduce(rsm, ex, AX.X, ALU.add))
            link(dve.reciprocal(rsm, rsm))
            link(dve.tensor_tensor(lg, ex, rsm.unsqueeze(2).broadcast_to([TP, NT, E]), ALU.mult))
            other = lg.unsqueeze(2).broadcast_to([TP, NT, E, E])
            own = lg.unsqueeze(3).broadcast_to([TP, NT, E, E])
            dve.tensor_tensor(gt, other, own, ALU.is_gt)
            link(dve.tensor_tensor(eq, other, own, ALU.is_equal))
            dve.wait_ge(tri_ready, 1)
            link(dve.tensor_tensor(eq, eq, tri.unsqueeze(1).broadcast_to([TP, NT, E, E]), ALU.mult))
            link(dve.tensor_tensor(gt, gt, eq, ALU.add))
            link(dve.tensor_reduce(rank, gt, AX.X, ALU.add))
            dve.scalar_tensor_tensor(out=comb, in0=rank, scalar=1.5, in1=lg, op0=ALU.is_lt,
                                     op1=ALU.mult).then_inc(comb_ready, 1)
            for n in range(NHT + NST):
                dve.wait_ge(silu, n + 1)
                dve.tensor_tensor(hT[:, n, :], sil[:, n % 2, :], bank[2 * (n % 2) + 1][0:IT, 0:TOK],
                                  ALU.mult).then_inc(moeh, 1)
            dve.wait_ge(comb_ready, 1)
            i = 0
            for j in range(NT):
                for e in range(E + 1):
                    dve.wait_ge(ye_ps, i + 1)
                    wait(dve, ye_used, i)
                    y = praw[0:TP, i % 2, 0:DM]
                    if e < E:
                        dve.scalar_tensor_tensor(out=x_sb[:, j, :], in0=y, scalar=comb[:, j, e:e + 1],
                                                 in1=x_sb[:, j, :], op0=ALU.mult, op1=ALU.add).then_inc(ye_used, 1)
                    else:
                        dve.tensor_tensor(x_sb[:, j, :], y, x_sb[:, j, :], ALU.add).then_inc(ye_used, 1)
                    i += 1


_INS = ['x', 'ctx_1024', 'mask_BxS2_bf1', 'L0_xattn_Wq', 'L0_xattn_Wk', 'L0_xattn_Wv', 'L0_xattn_Wo',
        'L0_xattn_gq', 'L0_xattn_gk', 'L0_ffn_w_fc', 'L0_ffn_w_proj', 'L1_xattn_Wq', 'L1_xattn_Wk',
        'L1_xattn_Wv', 'L1_xattn_Wo', 'L1_ffn_gate_w', 'L1_ffn_w_gate', 'L1_ffn_w_up', 'L1_ffn_w_down',
        'L1_ffn_sw_gate', 'L1_ffn_sw_up', 'L1_ffn_sw_down']


def kernel(**inputs):
    import numpy as _np
    import concourse.bacc as _bacc
    from concourse import mybir as _mybir
    from concourse.bass_utils import run_bass_kernel_spmd as _run

    nc = _bacc.Bacc("TRN2", target_bir_lowering=False, num_devices=1)
    arrays, args = {}, []
    for name in _INS:
        a = _np.ascontiguousarray(inputs[name])
        if a.dtype == _np.bool_:
            a = a.view(_np.uint8)
        arrays[f"in_{name}_dram"] = a
        args.append(nc.dram_tensor(f"in_{name}_dram", a.shape, _mybir.dt.from_np(a.dtype), kind="ExternalInput").ap())
    out = nc.dram_tensor("out_dram", (B, SQ, DM), F32, kind="ExternalOutput").ap()
    build(nc, *args, out)
    r = _run(nc, [arrays], core_ids=[0])
    return r.results[0]["out_dram"]
```

```python
from contextlib import ExitStack

import concourse.bass as bass
from concourse import mybir

ALU = mybir.AluOpType
ACT = mybir.ActivationFunctionType
AX = mybir.AxisListType
F32 = mybir.dt.float32
F16 = mybir.dt.float16
U8 = mybir.dt.uint8

B, SQ, DM = 8, 56, 256
SK, CD = 1500, 128
H, HD = 16, 128
KV1 = 8
KP, KT = 125, 12
CW = CD + 1
NT, TP = 4, 112
TOK = NT * TP
KK = DM // 128
HU = 8
QU = HU * SQ
QJ = QU // TP
NU = B * H // HU
SW = KT * QU
FF = 4 * DM
FO = FF // 128
E, EI = 8, 176
IT = 88
NHT = E * EI // IT
NST = 2 * EI // IT
EXPG = 3
NEG = -1.0e30


def wait(eng, sem, value):
    if isinstance(value, int) and value <= 0:
        return
    eng.wait_ge(sem, value)


def build(nc, x, ctx, mask, Wq0, Wk0, Wv0, Wo0, gq, gk, w_fc, w_proj,
          Wq1, Wk1, Wv1, Wo1, gate_w, w_gate, w_up, w_down, sw_gate, sw_up, sw_down, out):
    with ExitStack() as st:
        def sb(name, shape, dt=F32):
            return st.enter_context(nc.sbuf_tensor(name, shape, dt))

        def ps(name, shape, dt=F32):
            return st.enter_context(nc.psum_tensor(name, shape, dt))

        def sem(name):
            return st.enter_context(nc.semaphore(name))

        ctx_flat = sb("ctx_sb", [128, B * KT * CW])[:, :]
        ctx_sb = ctx_flat.rearrange("p (b t c) -> p b t c", b=B, t=KT)
        ctxT_flat = sb("ctxT", [128, 2 * B * KT * KP], F16)[:, :]
        ctxT = ctxT_flat.rearrange("p (l b t n) -> p l b t n", l=2, b=B, t=KT)
        S_flat = sb("S", [128, 2 * SW])[:, :]
        S = S_flat.rearrange("p (r n) -> p r n", r=2)
        qk_flat = sb("qk", [128, B * 2 * 2 * QU], F16)[:, :]
        qk = qk_flat.rearrange("p (b g l n) -> p b g l n", b=B, g=2, l=2)
        acT = qk_flat.bitcast(F32).rearrange("p (b g n) -> p b g n", b=B, g=2)
        wbuf = sb("wbuf", [128, 6144])
        x_sb = sb("x_sb", [TP, NT, DM])
        xn = sb("xn", [TP, NT, DM])
        xnT = sb("xnT", [128, KK, TOK])
        ident = sb("ident", [128, 128])
        ident16 = sb("ident16", [128, 128], F16)
        macc = sb("macc", [KP, QU])
        msp = sb("msp", [KP, QU])
        mcol = sb("mcol", [TP, QJ])
        acn = xn[:, 0:2, :].rearrange("p j d -> p (j d)").rearrange("p (j c) -> p j c", c=CD)
        rden = sb("rden", [TP, QJ])
        ssq = sb("ssq", [KP, KT, HU])
        krstd = sb("krstd", [KP, KT, HU])
        ktmp = sb("ktmp", [KP, KT, HU])
        mask_u8 = sb("mask_u8", [KP, B, KT], U8)
        mask_f = sb("mask_f", [KP, B, KT])
        half_bias = sb("half_bias", [KP, B, KT])
        mbias = sb("mbias", [KP, 3, KT])
        mhalf = sb("mhalf", [128, 1])
        stats = sb("stats", [TP, NT, 2, 6])
        mv = sb("mv", [TP, NT, 2])
        lnv = sb("lnv", [TP, NT])
        lnr = sb("lnr", [TP, NT])
        qss = sb("qss", [TP, HU])
        qvar = sb("qvar", [TP, HU])
        qrstd = sb("qrstd", [TP, HU])
        g2 = sb("g2", [128, 3])
        wsum = sb("wsum", [128, 2])
        gam = sb("gam", [128, 2])
        thr = sb("thr", [128, 2, 2])
        amx = sb("amx", [TP, NT])
        namx = sb("namx", [TP, NT])

        S0, S1 = S[:, 0, :], S[:, 1, :]
        slots = [S0, S1, wbuf[:, 0:SW]]

        def tiles(slot):
            return slots[slot][0:KP].rearrange("p (t n) -> p t n", t=KT)

        def slot_of(l, u):
            return (0, 2)[u % 2] if l == 0 else u % 3

        wq_sb = S0[:, 0:KK * H * HD].rearrange("p (k n) -> p k n", k=KK)
        qn = S0[0:TP, 4096:5120]
        wk1_sb = S0[:, 4096:4096 + KV1 * HD]
        wkT = [wbuf[:, 0:2048].rearrange("p (h c) -> p h c", h=H),
               wbuf[:, 4096:5120].rearrange("p (h c) -> p h c", h=KV1)]
        qT = [wbuf[:, 2048:2048 + HU * TOK].rearrange("p (h t) -> p h t", h=HU),
              S1[:, 0:HU * TOK].rearrange("p (h t) -> p h t", h=HU)]
        wk_sb = S1[:, 2048:4096]
        wk16 = S1[:, 0:2048].bitcast(F16).rearrange("p (l n) -> p l n", l=2)
        sq = S1[:, 2048:4096].rearrange("p (r n) -> p r n", r=2)
        qsq = S1[0:TP, 4096:5120]
        wv_sb = S1[:, 0:2048].rearrange("p (h c) -> p h c", h=H)
        wo_lo = S1[:, 2048:4096].rearrange("p (h n) -> p h n", h=HU)
        wo_hi = [S0[:, 0:2048].rearrange("p (h n) -> p h n", h=HU),
                 wbuf[:, 0:2048].rearrange("p (h n) -> p h n", h=HU)]
        oT = [S0[:, 2048:2048 + 2 * TOK].rearrange("p (r t) -> p r t", r=2),
              wbuf[:, 2048:2048 + 2 * TOK].rearrange("p (r t) -> p r t", r=2)]
        wfc_sb = wbuf[:, 0:2048].rearrange("p (o d) -> p o d", o=FO)
        wpj_sb = wbuf[:, 2048:4096].rearrange("p (o d) -> p o d", o=KK)
        t_fc = wbuf[:, 4096:5120].bitcast(F16).rearrange("p (o d) -> p o d", o=FO)
        t_pj = wbuf[:, 5120:6144].bitcast(F16).rearrange("p (o d) -> p o d", o=KK)
        tneg = S0[:, 2944:3968].bitcast(F16)
        wabs_out = S0[:, 3968:4992].bitcast(F16)
        ones = S0[:, 4992:5120]
        fcT = wbuf[:, 0:1024].bitcast(F16).rearrange("p (k n) -> p k n", k=KK)
        pjT = wbuf[:, 1024:2048].bitcast(F16).rearrange("p (o n) -> p o n", o=FO)
        hT16 = S1[:, 0:3584].bitcast(F16).rearrange("p (l o t) -> p l o t", l=2, o=FO)
        zT = S1[:, 3584:3584 + 896].bitcast(F16).rearrange("p (l k t) -> p l k t", l=2, k=KK)
        hbuf = qk_flat.bitcast(F32)[0:TP, 0:NT * FF] \
            .rearrange("p (j n) -> p j n", j=NT)
        moe = ctxT_flat.bitcast(F32)
        wg_sb = moe[:, 0:2816].rearrange("p (e k i) -> p e k i", e=E, k=KK)
        wu_sb = moe[:, 2816:5632].rearrange("p (e k i) -> p e k i", e=E, k=KK)
        sg_sb = moe[:, 5632:6336].rearrange("p (k i) -> p k i", k=KK)
        su_sb = moe[:, 6336:7040].rearrange("p (k i) -> p k i", k=KK)
        gw_sb = moe[0:E, 7040:7296]
        gwT = moe[:, 7296:7312].rearrange("p (k e) -> p k e", k=KK)
        sil = moe[0:IT, 7400:7400 + 2 * TOK].rearrange("p (r t) -> p r t", r=2)
        lg = moe[0:TP, 8400:8432].rearrange("p (j e) -> p j e", j=NT)
        ex = moe[0:TP, 8432:8464].rearrange("p (j e) -> p j e", j=NT)
        comb = moe[0:TP, 8464:8496].rearrange("p (j e) -> p j e", j=NT)
        rank = moe[0:TP, 8496:8528].rearrange("p (j e) -> p j e", j=NT)
        rmx = moe[0:TP, 8528:8532]
        rsm = moe[0:TP, 8532:8536]
        gt = moe[0:TP, 8600:8856].rearrange("p (j a b) -> p j a b", j=NT, a=E)
        eq = moe[0:TP, 8856:9112].rearrange("p (j a b) -> p j a b", j=NT, a=E)
        tri = moe[0:TP, 9112:9176].rearrange("p (a b) -> p a b", a=E)
        wd_sb = ctx_flat[0:IT, 0:(NHT + NST) * DM] \
            .rearrange("p (n d) -> p n d", d=DM)
        hT = S_flat[0:IT, 0:(NHT + NST) * TOK] \
            .rearrange("p (n t) -> p n t", t=TOK)

        pk = ps("pk", [128, 2, 1024])
        praw = ps("praw", [128, 2, 512])
        pA = ps("pA", [128, 512])
        pB = ps("pB", [128, 512])
        pA16 = pA[:, :].bitcast(F16)
        pB16 = pB[:, :].bitcast(F16)
        bank = [pk[:, 0, 0:512], pk[:, 0, 512:1024], pk[:, 1, 0:512], pk[:, 1, 512:1024]]

        def fold_bank(l, n):
            return (praw[:, n % 2, :] if l == 0 or n % 4 < 2 else (pA, pB)[n % 2][:, :])[:, 0:TOK]

        ld_x, ld_g, ld_wk, ld_wq, ld_mask = sem("ld_x"), sem("ld_g"), sem("ld_wk"), sem("ld_wq"), sem("ld_mask")
        ld_ctx = [sem(f"ld_ctx{b}") for b in range(B)]
        ld_wvo = [sem(f"ld_wvo{l}") for l in range(2)]
        ld_wo_hi = [sem(f"ld_wo_hi{l}") for l in range(2)]
        ld_ffn, ld_wq1, ld_wk1, ld_moe, ld_wd = sem("ld_ffn"), sem("ld_wq1"), sem("ld_wk1"), sem("ld_moe"), sem("ld_wd")
        idz, consts, chain, pchain = sem("idz"), sem("consts"), sem("chain"), sem("pchain")
        ln_var, ln_rstd, xn_ready, xnT_ps, xnT_ready = (sem("ln_var"), sem("ln_rstd"), sem("xn_ready"),
                                                        sem("xnT_ps"), sem("xnT_ready"))
        ctxT_ps, ctxT_hi, ctxT_lo = sem("ctxT_ps"), sem("ctxT_hi"), sem("ctxT_lo")
        wk_hi, wk_lo, wkT_ps, wkT_ready, g_ready = (sem("wk_hi"), sem("wk_lo"), sem("wkT_ps"),
                                                    sem("wkT_ready"), sem("g_ready"))
        q_ps, q_sq, q_var, q_rstd, qn_ready, qT_ps, qT_ready = (sem("q_ps"), sem("q_sq"), sem("q_var"), sem("q_rstd"),
                                                                sem("qn_ready"), sem("qT_ps"), sem("qT_ready"))
        qk_ps, qk_hi, qk_lo = sem("qk_ps"), sem("qk_hi"), sem("qk_lo")
        k_ps, k_sq, k_red, k_var, k_rstd = sem("k_ps"), sem("k_sq"), sem("k_red"), sem("k_var"), sem("k_rstd")
        k_ln, k_r0, k_newton = sem("k_ln"), sem("k_r0"), sem("k_newton")
        mask_ready, mbias_ready, ctx_masked = sem("mask_ready"), sem("mbias_ready"), sem("ctx_masked")

        class Attn:
            def __init__(self, l):
                self.raw = sem(f"raw{l}")
                self.score = sem(f"score{l}")
                self.mstep = sem(f"mstep{l}")
                self.maccT = sem(f"maccT{l}")
                self.mcol = sem(f"mcol{l}")
                self.mbc = sem(f"mbc{l}")
                self.msp = sem(f"msp{l}")
                self.sub = sem(f"sub{l}")
                self.exp = sem(f"exp{l}")
                self.pv = sem(f"pv{l}")
                self.rden = sem(f"rden{l}")
                self.acn = sem(f"acn{l}")
                self.acTps = sem(f"acTps{l}")
                self.ac = sem(f"ac{l}")
                self.oT_ps = sem(f"oT_ps{l}")
                self.oT = sem(f"oT{l}")
                self.y = sem(f"y{l}")
                self.x = sem(f"x{l}")
        at = [Attn(0), Attn(1)]
        wabs, wsum_ps, gam_ready, tern, ternT_ps, ternT = (sem("wabs"), sem("wsum_ps"), sem("gam_ready"),
                                                          sem("tern"), sem("ternT_ps"), sem("ternT"))
        z_ready, zT_ps, zT_hi, zT_lo = sem("z_ready"), sem("zT_ps"), sem("zT_hi"), sem("zT_lo")
        h_ps, h_act, h_ready, hT_ps, hT_hi, hT_lo, f_ps, f_done = (sem("h_ps"), sem("h_act"), sem("h_ready"),
            sem("hT_ps"), sem("hT_hi"), sem("hT_lo"), sem("f_ps"), sem("f_done"))
        gwT_ps, gwT_ready, lg_ps, lg_sub, lg_exp, comb_ready = (sem("gwT_ps"), sem("gwT_ready"), sem("lg_ps"),
            sem("lg_sub"), sem("lg_exp"), sem("comb_ready"))
        gu_ps, silu, moeh, ye_ps, ye_used, tri_ready = (sem("gu_ps"), sem("silu"), sem("moeh"), sem("ye_ps"),
                                                       sem("ye_used"), sem("tri_ready"))
        ones_ready, stored = sem("ones_ready"), sem("stored")

        block = st.enter_context(nc.Block())

        @block.sync
        def _(sp):
            xv = x.rearrange("b s d -> (b s) d").rearrange("(j p) d -> p j d", p=TP)
            cv = ctx.rearrange("b (p t) c -> p b t c", t=KT)
            sp.dma_start(x_sb[:, :, :], xv).then_inc(ld_x, 16)
            sp.dma_start(wk_sb, Wk0).then_inc(ld_wk, 16)
            sp.dma_start(ctx_sb[0:KP, 0, :, 0:CD], cv[:, 0]).then_inc(ld_ctx[0], 16)
            sp.dma_start(wq_sb, Wq0.rearrange("(k p) n -> p k n", p=128)).then_inc(ld_wq, 16)
            sp.dma_start(g2[:, 0:1], gq.rearrange("(d a) -> d a", a=1)).then_inc(ld_g, 16)
            sp.dma_start(g2[:, 1:2], gk.rearrange("(d a) -> d a", a=1)).then_inc(ld_g, 16)
            for b in range(1, B):
                sp.dma_start(ctx_sb[0:KP, b, :, 0:CD], cv[:, b]).then_inc(ld_ctx[b], 16)
            sp.dma_start(mask_u8[:, :, :], mask.rearrange("b (p t) -> p b t", t=KT)).then_inc(ld_mask, 16)
            wait(sp, k_ps, NU * KT)
            wait(sp, k_red, NU * KT)
            sp.dma_start(wv_sb, Wv0.rearrange("c (h d) -> c h d", h=H)).then_inc(ld_wvo[0], 16)
            wo0_v = Wo0.rearrange("(h d) n -> d h n", h=H)
            sp.dma_start(wo_lo, wo0_v[:, 0:HU, :]).then_inc(ld_wvo[0], 16)
            wait(sp, at[0].pv, 2 * (NU - 1))
            sp.dma_start(wo_hi[0], wo0_v[:, HU:H, :]).then_inc(ld_wo_hi[0], 16)
            wait(sp, at[0].pv, 2 * NU)
            sp.dma_start(wfc_sb, w_fc.rearrange("(o p) d -> p o d", p=128)).then_inc(ld_ffn, 16)
            sp.dma_start(wpj_sb, w_proj.rearrange("(o p) d -> p o d", p=128)).then_inc(ld_ffn, 16)
            wait(sp, at[0].y, 1)
            wait(sp, tern, 2)
            sp.dma_start(wk1_sb, Wk1).then_inc(ld_wk1, 16)
            sp.dma_start(wq_sb, Wq1.rearrange("(k p) n -> p k n", p=128)).then_inc(ld_wq1, 16)
            wait(sp, at[1].pv, 2 * (NU - 2))
            sp.dma_start(wv_sb[:, 0:KV1, :], Wv1.rearrange("c (h d) -> c h d", h=KV1)).then_inc(ld_wvo[1], 16)
            wo1_v = Wo1.rearrange("(h d) n -> d h n", h=H)
            sp.dma_start(wo_lo, wo1_v[:, 0:HU, :]).then_inc(ld_wvo[1], 16)
            wait(sp, at[1].pv, 2 * (NU - 1))
            sp.dma_start(wo_hi[1], wo1_v[:, HU:H, :]).then_inc(ld_wo_hi[1], 16)
            wait(sp, at[1].raw, NU * KT)
            for e in range(E):
                sp.dma_start(wg_sb[:, e], w_gate[e].rearrange("(k p) i -> p k i", p=128)).then_inc(ld_moe, 16)
                sp.dma_start(wu_sb[:, e], w_up[e].rearrange("(k p) i -> p k i", p=128)).then_inc(ld_moe, 16)
            sp.dma_start(sg_sb, sw_gate.rearrange("(k p) i -> p k i", p=128)).then_inc(ld_moe, 16)
            sp.dma_start(su_sb, sw_up.rearrange("(k p) i -> p k i", p=128)).then_inc(ld_moe, 16)
            sp.dma_start(gw_sb, gate_w).then_inc(ld_moe, 16)
            wait(sp, at[1].pv, 2 * NU)
            sp.dma_start(wd_sb[:, 0:NHT, :], w_down.rearrange("e (a p) d -> p (e a) d", p=IT)).then_inc(ld_wd, 16)
            sp.dma_start(wd_sb[:, NHT:NHT + NST, :], sw_down.rearrange("(a p) d -> p a d", p=IT)).then_inc(ld_wd, 16)
            ov = out.rearrange("b s d -> (b s) d").rearrange("(j p) d -> p j d", p=TP)
            wait(sp, ye_used, NT * (E + 1))
            sp.dma_start(ov, x_sb[:, :, :]).then_inc(stored, 16)
            sp.wait_ge(stored, 16)

        @block.gpsimd
        def _(pool):
            pool.memset(ident[:, :], 0.0).then_inc(idz, 1)
            pool.memset(ident16[:, :], 0.0).then_inc(idz, 1)
            pool.wait_ge(idz, 2)
            for m in (ident, ident16):
                pool.affine_select(out=m[:, :], in_=m[:, :], compare_op=ALU.not_equal, fill=1.0, base=0,
                                   pattern=[[-1, 128]], channel_multiplier=1).then_inc(consts, 1)
            pool.memset(mhalf[:, :], -0.5).then_inc(consts, 1)
            pool.memset(ctx_sb[0:KP, :, :, CD:CW], 1.0).then_inc(consts, 1)
            pool.wait_ge(consts, 4)

            def ln_pow(n):
                pool.wait_ge(ln_var, n + 1)
                pool.tensor_tensor(lnr[:, :], lnv[:, :], mhalf[0:TP, :].broadcast_to([TP, NT]), ALU.pow).then_inc(ln_rstd, 1)

            ln_pow(0)
            for i in range(2 * NT):
                pool.wait_ge(q_var, i + 1)
                pool.tensor_tensor(qrstd[:, :], qvar[:, :], mhalf[0:TP, :].broadcast_to([TP, HU]), ALU.pow).then_inc(q_rstd, 1)

            def subtract0(u, slot):
                a = at[0]
                pool.wait_ge(a.msp, u + 1)
                for c in range(KT // EXPG):
                    s = tiles(slot)[:, c * EXPG:(c + 1) * EXPG, :]
                    pool.tensor_tensor(s, s, msp[:, :].unsqueeze(1).broadcast_to([KP, EXPG, QU]),
                                       ALU.subtract).then_inc(a.sub, 1)

            def batch1(b, mb, first):
                if not first:
                    pool.wait_ge(at[1].score, 2 * KT * (b - 2) + 1)
                pool.tensor_tensor(mbias[:, mb, :], half_bias[:, b, :], half_bias[:, b, :],
                                   ALU.add).then_inc(mbias_ready, 1)
                pool.tensor_tensor(ctx_sb[0:KP, b, :, :], ctx_sb[0:KP, b, :, :],
                                   mask_f[:, b, :].unsqueeze(2).broadcast_to([KP, KT, CW]),
                                   ALU.mult).then_inc(ctx_masked, 1)

            for g in range(2):
                subtract0(g, slot_of(0, g))
            with pool.Fori(1, B) as b:
                for g in range(2):
                    subtract0(2 * b + g, slot_of(0, g))
            wait(pool, at[0].pv, 2 * (NU - 1))
            pool.memset(ones, 1.0).then_inc(ones_ready, 1)
            for n in range(1, 5):
                ln_pow(n)
            pool.wait_ge(mask_ready, 2)
            for b in range(2):
                batch1(b, b, True)
            with pool.Fori(0, 2) as i:
                for k in range(3):
                    batch1(3 * i + 2 + k, (2 + k) % 3, False)
            pool.wait_ge(at[1].raw, NU * KT)
            pool.memset(tri, 1.0).then_inc(pchain, 1)
            pool.wait_ge(pchain, 1)
            pool.affine_select(out=tri, in_=tri, compare_op=ALU.is_gt, fill=0.0, base=0,
                               pattern=[[1, E], [-1, E]], channel_multiplier=0).then_inc(tri_ready, 1)
            ln_pow(5)

        @block.tensor
        def _(pe):
            def transpose(out_, in_, idn):
                k = in_.shape[0]
                return pe.transpose(out_, in_, idn[0:k, 0:k])

            def stream_T(n, ready, count):
                wait(pe, ready, count)
                for k in range(KK):
                    for j in range(NT):
                        mm = transpose(bank[2 + k][:, j * TP:(j + 1) * TP], xn[:, j, k * 128:(k + 1) * 128], ident)
                    mm.then_inc(xnT_ps, 1)

            pe.wait_ge(consts, 4)
            pe.wait_ge(ld_wk, 16)
            for q in range(4):
                wait(pe, wkT_ready, q - 1)
                for i in range(4):
                    h = 4 * q + i
                    mm = transpose(bank[q % 2][:, i * 128:(i + 1) * 128], wk_sb[:, h * 128:(h + 1) * 128], ident)
                mm.then_inc(wkT_ps, 1)
            def context_T(b):
                pe.wait_ge(ld_ctx[b], 16)
                for q in range(3):
                    n = 3 * b + q
                    wait(pe, ctxT_lo, n - 1)
                    for i in range(4):
                        mm = transpose(praw[:, n % 2, i * KP:(i + 1) * KP], ctx_sb[0:KP, b, 4 * q + i, 0:CD], ident)
                    mm.then_inc(ctxT_ps, 1)
            stream_T(0, xn_ready, NT)

            def fold(l, g):
                for i in range(HU):
                    n = l * H + g * HU + i
                    wait(pe, qk_lo, n - (1 if l == 0 else 3))
                    h = g * HU + i
                    w = wkT[0][:, h, :] if l == 0 else wkT[1][:, h // 2, :]
                    if l == 0 and i == 0:
                        pe.wait_ge(ctxT_lo, 12 + 12 * g)
                    pe.matmul(fold_bank(l, n), w, qT[l][:, i, :], start=True, stop=True).then_inc(qk_ps, 1)

            def queries(i):
                g, j = i // NT, i % NT
                wait(pe, qn_ready, i - 1)
                for n in range(2):
                    for k in range(KK):
                        mm = pe.matmul(pk[0:TP, i % 2, n * 512:(n + 1) * 512], xnT[:, k, j * TP:(j + 1) * TP],
                                       wq_sb[:, k, g * 1024 + n * 512:g * 1024 + (n + 1) * 512],
                                       start=(k == 0), stop=(k == KK - 1))
                mm.then_inc(q_ps, 1)

            pe.wait_ge(ld_wq, 16)
            pe.wait_ge(xnT_ready, 2)
            pe.wait_ge(wkT_ready, 4)
            queries(0)
            for i in range(2 * NT):
                if i == NT:
                    pe.wait_ge(qk_lo, HU)
                context_T(i)
                if i + 1 < 2 * NT:
                    queries(i + 1)
                pe.wait_ge(qn_ready, i + 1)
                for n in range(2):
                    m = 2 * i + n
                    wait(pe, qT_ready, m - 1)
                    pt = pA if n == 0 else pB
                    for r in range(4):
                        hh = 4 * n + r
                        mm = transpose(pt[:, r * TP:(r + 1) * TP], qn[:, hh * 128:(hh + 1) * 128], ident)
                    mm.then_inc(qT_ps, 1)
                if i == NT - 1:
                    pe.wait_ge(qT_ready, 2 * NT)
                    fold(0, 0)

            def keys(b, g, before=None):
                u = 2 * b + g
                for t in range(KT):
                    if before:
                        before(t)
                    wait(pe, k_sq, u * KT + t - 1)
                    for n in range(2):
                        o = pk[0:KP, t % 2, n * 512:(n + 1) * 512]
                        c0 = g * 1024 + n * 512
                        for i, (lc, lw) in enumerate(((0, 0), (0, 1), (1, 0))):
                            mm = pe.matmul(o, ctxT[:, lc, b, t, :], wk16[:, lw, c0:c0 + 512],
                                           start=(i == 0), stop=(i == 2))
                    mm.then_inc(k_ps, 1)

            def scores(l, b, g, before=None):
                a, u = at[l], 2 * b + g
                for t in range(KT):
                    if before:
                        before(t)
                    wait(pe, a.score, u * KT + t - 1)
                    for i, (lc, lq) in enumerate(((0, 0), (0, 1), (1, 0))):
                        mm = pe.matmul(praw[0:KP, t % 2, 0:QU], ctxT[:, lc, b, t, :], qk[:, b, g, lq, :],
                                       start=(i == 0), stop=(i == 2))
                    mm.then_inc(a.raw, 1)

            def max_T(l, u):
                a = at[l]
                pe.wait_ge(a.mstep, (KT - 1) * (u + 1))
                for j in range(QJ):
                    mm = transpose(pA[0:TP, j * KP:(j + 1) * KP], macc[:, j * TP:(j + 1) * TP], ident)
                mm.then_inc(a.maccT, 1)

            def max_spread(l, u):
                a = at[l]
                pe.wait_ge(a.mcol, u + 1)
                for j in range(QJ):
                    mm = pe.transpose(pA[0:KP, j * TP:(j + 1) * TP], mcol[:, j:j + 1].broadcast_to([TP, KP]),
                                      ident[0:TP, 0:TP])
                mm.then_inc(a.mbc, 1)

            def attend(l, b, g, slot, outs, between=None):
                a, u = at[l], 2 * b + g
                s = tiles(slot)
                for c in range(2):
                    if l == 0 and c == 0:
                        wait(pe, a.msp, u + 1)
                    if l == 0 and c == 1:
                        wait(pe, a.ac, u)
                    if l == 1:
                        wait(pe, a.acn, 2 * u + c - 1)
                    for j in range(2):
                        for t in range(KT):
                            if c == 0 and j == 0 and t % EXPG == 0:
                                pe.wait_ge(a.exp, u * (KT // EXPG) + t // EXPG + 1)
                            q = 2 * c + j
                            mm = pe.matmul(outs[c][0:TP, j * CW:(j + 1) * CW], s[:, t, q * TP:(q + 1) * TP],
                                           ctx_sb[0:KP, b, t, :], start=(t == 0), stop=(t == KT - 1))
                    mm.then_inc(a.pv, 1)
                    if c == 0 and between:
                        between()

            def attended_T(l, u):
                a = at[l]
                pe.wait_ge(a.acn, 2 * u + 2)
                if l == 1:
                    wait(pe, a.ac, u)
                for j in range(QJ):
                    mm = transpose(pB[:, j * TP:(j + 1) * TP], acn[:, j, :], ident)
                mm.then_inc(a.acTps, 1)

            pe.wait_ge(wk_lo, 1)
            pe.wait_ge(qn_ready, 2 * NT)
            keys(0, 0)
            pe.wait_ge(qT_ready, 4 * NT)
            fold(0, 1)
            pe.wait_ge(qk_lo, H)

            def step0(b, g, n):
                u = 2 * b + g

                def in_scores(t):
                    if t == 3 and n != 0:
                        max_spread(0, u - 1)
                    if t == 8 and n not in (0, 1):
                        attended_T(0, u - 2)
                scores(0, b, g, in_scores)
                if n != -1:
                    bn, gn = (b, 1) if g == 0 else (b + 1, 0)
                    keys(bn, gn)
                if n != 0:
                    bp, gp = (b, 0) if g == 1 else (b - 1, 1)
                    attend(0, bp, gp, slot_of(0, gp), (pA, pB))
                    pe.wait_ge(at[0].acn, 2 * u - 1)
                max_T(0, u)

            for g in range(2):
                step0(0, g, g)
            with pe.Fori(1, B - 1) as b:
                for g in range(2):
                    step0(b, g, None)
            step0(B - 1, 0, None)
            step0(B - 1, 1, -1)
            max_spread(0, NU - 1)
            attended_T(0, NU - 2)
            attend(0, B - 1, 1, slot_of(0, 1), (pA, pB))
            attended_T(0, NU - 1)

            def project(l):
                a = at[l]
                pe.wait_ge(a.ac, NU)
                pe.wait_ge(ld_wvo[l], 32)
                for h in range(H + 1):
                    if h < H:
                        wait(pe, a.oT, h - 1)
                        g, i = h // HU, h % HU
                        w = wv_sb[:, h, :] if l == 0 else wv_sb[:, h // 2, :]
                        pe.matmul(praw[:, h % 2, 0:TOK].rearrange("p (b q) -> p b q", b=B), w,
                                  acT[:, :, g, i * SQ:(i + 1) * SQ],
                                  start=True, stop=True).then_inc(a.oT_ps, 1)
                    if h > 0:
                        pe.wait_ge(a.oT, h)
                        if h == HU + 1:
                            pe.wait_ge(ld_wo_hi[l], 16)
                        w = wo_lo[:, h - 1, :] if h <= HU else wo_hi[l][:, h - 1 - HU, :]
                        for j in range(NT):
                            mm = pe.matmul(bank[j][0:TP, 0:DM], oT[l][:, (h - 1) % 2, j * TP:(j + 1) * TP],
                                           w, start=(h == 1), stop=(h == H))
                        if h == H:
                            mm.then_inc(a.y, 1)
                    if l == 0 and h == HU:
                        pe.wait_ge(wabs, 2)
                        pe.wait_ge(ones_ready, 1)
                        pe.matmul(pA[:, 0:2], ones, wsum[:, :], start=True, stop=True).then_inc(wsum_ps, 1)
            project(0)

            pe.wait_ge(gam_ready, 1)
            pe.wait_ge(tern, 2)
            for q in range(8):
                wait(pe, ternT, q - 1)
                pt = pA16 if q % 2 == 0 else pB16
                for i in range(4):
                    if q < 4:
                        src = t_fc[:, 4 * (q % 2) + i, (q // 2) * 128:(q // 2 + 1) * 128]
                    else:
                        o = 2 * (q - 4) + i // 2
                        src = t_pj[:, i % 2, o * 128:(o + 1) * 128]
                    mm = transpose(pt[:, i * 128:(i + 1) * 128], src, ident16)
                mm.then_inc(ternT_ps, 1)
            pe.wait_ge(at[0].x, NT)
            stream_T(1, z_ready, NT)
            pe.wait_ge(ternT, 8)
            pe.wait_ge(zT_lo, 2)
            for j in range(NT):
                wait(pe, h_act, j - 1)
                for n in range(2):
                    i = 0
                    for k in range(KK):
                        for l in range(2):
                            mm = pe.matmul(pk[0:TP, j % 2, n * 512:(n + 1) * 512], zT[:, l, k, j * TP:(j + 1) * TP],
                                           fcT[:, k, n * 512:(n + 1) * 512], start=(i == 0), stop=(i == 3))
                            i += 1
                mm.then_inc(h_ps, 1)
            for o in range(FO):
                wait(pe, hT_lo, o - 1)
                pe.wait_ge(h_ready, NT)
                for j in range(NT):
                    mm = transpose(praw[:, o % 2, j * TP:(j + 1) * TP], hbuf[:, j, o * 128:(o + 1) * 128], ident)
                mm.then_inc(hT_ps, 1)
            pe.wait_ge(hT_lo, FO)
            for j in range(NT):
                for o in range(FO):
                    for l in range(2):
                        mm = pe.matmul(bank[j][0:TP, 0:DM], hT16[:, l, o, j * TP:(j + 1) * TP], pjT[:, o, :],
                                       start=(o == 0 and l == 0), stop=(o == FO - 1 and l == 1))
                mm.then_inc(f_ps, 1)

            pe.wait_ge(ld_wk1, 16)
            for q in range(2):
                for i in range(4):
                    h = 4 * q + i
                    mm = transpose((pA if q == 0 else pB)[:, i * 128:(i + 1) * 128],
                                   wk1_sb[:, h * 128:(h + 1) * 128], ident)
                mm.then_inc(wkT_ps, 1)
            pe.wait_ge(f_done, NT)
            stream_T(2, xn_ready, 2 * NT)
            pe.wait_ge(xnT_ready, 4)
            pe.wait_ge(ld_wq1, 16)
            pe.wait_ge(wkT_ready, 6)
            for g in range(2):
                for i in range(HU):
                    m = g * HU + i
                    wait(pe, qT_ready, 16 + m - 1)
                    for k in range(KK):
                        mm = pe.matmul(bank[m % 2][:, 0:TOK], wq_sb[:, k, m * 128:(m + 1) * 128], xnT[:, k, :],
                                       start=(k == 0), stop=(k == KK - 1))
                    mm.then_inc(qT_ps, 1)
                pe.wait_ge(qT_ready, 16 + HU * (g + 1))
                fold(1, g)
            pe.wait_ge(qk_lo, 2 * H)

            def step1(b, g, slot, n):
                u = 2 * b + g

                def in_scores(t):
                    if t == 3 and n >= 1:
                        max_spread(1, u - 1)
                    if t == 8 and n >= 3:
                        attended_T(1, u - 3)
                scores(1, b, g, in_scores)

                def between():
                    if n >= 1:
                        pe.wait_ge(at[1].sub, 4 * u)
                    max_T(1, u)
                if n >= 2:
                    pe.wait_ge(ctx_masked, b)
                    attend(1, b - 1, g, (slot + 1) % 3, (bank[0], bank[1]), between)
                else:
                    between()
            for u in range(4):
                step1(u // 2, u % 2, slot_of(1, u), u)
            with pe.Fori(0, 2) as i:
                for k in range(6):
                    step1(3 * i + 2 + k // 2, k % 2, slot_of(1, 4 + k), 9)
            max_spread(1, NU - 1)
            attended_T(1, NU - 3)
            pe.wait_ge(ctx_masked, B)
            attend(1, B - 1, 0, slot_of(1, NU - 2), (bank[0], bank[1]))
            attended_T(1, NU - 2)
            attend(1, B - 1, 1, slot_of(1, NU - 1), (bank[0], bank[1]))
            attended_T(1, NU - 1)
            project(1)

            pe.wait_ge(ld_moe, 16 * (2 * E + 3))
            for k in range(KK):
                mm = transpose(pA[:, k * E:(k + 1) * E], gw_sb[:, k * 128:(k + 1) * 128], ident)
            mm.then_inc(gwT_ps, 1)
            pe.wait_ge(at[1].x, NT)
            stream_T(3, xn_ready, 3 * NT)
            pe.wait_ge(xnT_ready, 6)
            pe.wait_ge(gwT_ready, 1)
            for j in range(NT):
                for k in range(KK):
                    mm = pe.matmul(pB[0:TP, j * E:(j + 1) * E], xnT[:, k, j * TP:(j + 1) * TP], gwT[:, k, :],
                                   start=(k == 0), stop=(k == KK - 1))
            mm.then_inc(lg_ps, 1)
            for n in range(NHT + NST):
                wait(pe, moeh, n - 1)
                for wi, (we, ws) in enumerate(((wg_sb, sg_sb), (wu_sb, su_sb))):
                    for k in range(KK):
                        if n < NHT:
                            w = we[:, n // 2, k, (n % 2) * IT:(n % 2 + 1) * IT]
                        else:
                            w = ws[:, k, (n - NHT) * IT:(n - NHT + 1) * IT]
                        mm = pe.matmul(bank[2 * (n % 2) + wi][0:IT, 0:TOK], w, xnT[:, k, :],
                                       start=(k == 0), stop=(k == KK - 1))
                mm.then_inc(gu_ps, 1)
            pe.wait_ge(ld_wd, 32)
            pe.wait_ge(moeh, NHT + NST)
            i = 0
            for j in range(NT):
                for e in range(E + 1):
                    wait(pe, ye_used, i - 1)
                    parts = range(2 * e, 2 * e + 2) if e < E else range(NHT, NHT + NST)
                    for n in parts:
                        mm = pe.matmul(praw[0:TP, i % 2, 0:DM], hT[:, n, j * TP:(j + 1) * TP], wd_sb[:, n, :],
                                       start=(n == parts[0]), stop=(n == parts[-1]))
                    mm.then_inc(ye_ps, 1)
                    i += 1

        @block.scalar
        def _(act):
            act.wait_ge(ld_wk, 16)
            act.activation(wk16[:, 0, :], wk_sb, ACT.Copy, scale=16.0).then_inc(wk_hi, 1)

            def context_hi(b):
                for q in range(3):
                    n = 3 * b + q
                    act.wait_ge(ctxT_ps, n + 1)
                    act.activation(ctxT[:, 0, b, 4 * q:4 * q + 4, :].rearrange("p t n -> p (t n)"),
                                   praw[:, n % 2, 0:4 * KP], ACT.Copy).then_inc(ctxT_hi, 1)

            def stream_copy(n):
                for k in range(KK):
                    act.wait_ge(xnT_ps, KK * n + k + 1)
                    act.activation(xnT[:, k, :], bank[2 + k][:, 0:TOK], ACT.Copy).then_inc(xnT_ready, 1)
            stream_copy(0)

            def fold_hi(l, g):
                for i in range(HU):
                    n = l * H + g * HU + i
                    act.wait_ge(qk_ps, n + 1)
                    act.activation(qk[:, :, g, 0, i * SQ:(i + 1) * SQ],
                                   fold_bank(l, n).rearrange("p (b q) -> p b q", b=B),
                                   ACT.Copy).then_inc(qk_hi, 1)

            for g in range(2):
                for j in range(NT):
                    i = g * NT + j
                    act.wait_ge(q_ps, i + 1)
                    wait(act, q_var, i)
                    act.activation(qsq, pk[0:TP, i % 2, :], ACT.Square).then_inc(q_sq, 1)
                    context_hi(i)
                    for n in range(2):
                        m = 2 * i + n
                        act.wait_ge(qT_ps, m + 1)
                        if g == 1 and j == 0 and n == 0:
                            act.wait_ge(qk_ps, HU)
                        pt = pA if n == 0 else pB
                        act.activation(qT[0][:, 4 * n:4 * n + 4, j * TP:(j + 1) * TP],
                                       pt[:, 0:4 * TP].rearrange("p (h t) -> p h t", h=4),
                                       ACT.Copy).then_inc(qT_ready, 1)
                if g == 0:
                    fold_hi(0, 0)

            def square(u, t):
                act.wait_ge(k_ps, u * KT + t + 1)
                wait(act, k_red, u * KT + t - 1)
                act.activation(sq[0:KP, t % 2, :], pk[0:KP, t % 2, :], ACT.Square).then_inc(k_sq, 1)

            def exps(l, u, slot, c):
                a = at[l]
                act.wait_ge(a.sub, u * (KT // EXPG) + c + 1)
                s = slots[slot][0:KP, c * EXPG * QU:(c + 1) * EXPG * QU]
                act.activation(s, s, ACT.Exp).then_inc(a.exp, 1)

            def copy_max(u):
                act.wait_ge(at[0].mbc, u + 1)
                act.activation(msp[:, :], pA[0:KP, 0:QU], ACT.Copy).then_inc(at[0].msp, 1)

            def store_ac(l, b, g):
                a, u = at[l], 2 * b + g
                act.wait_ge(a.acTps, u + 1)
                act.activation(acT[:, b, g, :], pB[:, 0:QU], ACT.Copy).then_inc(a.ac, 1)

            def key_r0(u):
                act.wait_ge(k_var, u + 1)
                act.activation(ktmp[:, :, :], ssq[:, :, :], ACT.Ln).then_inc(k_ln, 1)
                act.wait_ge(k_ln, u + 1)
                act.activation(krstd[:, :, :], ktmp[:, :, :], ACT.Exp, scale=-0.5).then_inc(k_r0, 1)

            act.wait_ge(wkT_ps, 4)
            act.wait_ge(wk_lo, 1)
            for t in range(KT):
                square(0, t)
            key_r0(0)
            fold_hi(0, 1)

            def step0(b, g, n):
                u = 2 * b + g
                if n != 0:
                    copy_max(u - 1)
                if n not in (0, 1):
                    store_ac(0, b - 1, g)
                for t in range(KT):
                    if n != -1:
                        square(u + 1, t)
                    if n != 0 and t % 3 == 2:
                        exps(0, u - 1, slot_of(0, 1 - g), t // 3)
                if n != -1:
                    key_r0(u + 1)
            for g in range(2):
                step0(0, g, g)
            with act.Fori(1, B - 1) as b:
                for g in range(2):
                    step0(b, g, None)
            step0(B - 1, 0, None)
            step0(B - 1, 1, -1)
            copy_max(NU - 1)
            store_ac(0, B - 1, 0)
            for c in range(KT // EXPG):
                exps(0, NU - 1, slot_of(0, 1), c)
            store_ac(0, B - 1, 1)

            def project(l):
                a = at[l]
                for h in range(H):
                    act.wait_ge(a.oT_ps, h + 1)
                    act.activation(oT[l][:, h % 2, :], praw[:, h % 2, 0:TOK], ACT.Copy).then_inc(a.oT, 1)
                    if l == 0 and h in (3, 5):
                        i = (h - 3) // 2
                        act.wait_ge(ld_ffn, 32)
                        wait(act, wabs, i)
                        act.activation(wabs_out, (wfc_sb, wpj_sb)[i].rearrange("p o d -> p (o d)"), ACT.Abs,
                                       accum_out=wsum[:, i:i + 1]).then_inc(wabs, 1)
            project(0)

            for k in range(KK):
                act.wait_ge(xnT_ps, KK + k + 1)
                act.activation(zT[:, 0, k, :], bank[2 + k][:, 0:TOK], ACT.Copy).then_inc(zT_hi, 1)
            act.wait_ge(gam_ready, 1)
            for j in range(NT):
                act.wait_ge(h_ps, j + 1)
                act.activation(hbuf[:, j, :], pk[0:TP, j % 2, :], ACT.Gelu, scale=gam[0:TP, 0:1]).then_inc(h_act, 1)
            for o in range(FO):
                act.wait_ge(hT_ps, o + 1)
                act.activation(hT16[:, 0, o, :], praw[:, o % 2, 0:TOK], ACT.Copy).then_inc(hT_hi, 1)

            for k in range(KK):
                act.wait_ge(xnT_ps, 2 * KK + k + 1)
                act.activation(xnT[:, k, :], bank[2 + k][:, 0:TOK], ACT.Copy).then_inc(xnT_ready, 1)
            for g in range(2):
                for i in range(HU):
                    m = g * HU + i
                    act.wait_ge(qT_ps, 16 + m + 1)
                    if g == 1 and i == 0:
                        act.wait_ge(qk_ps, H + HU)
                    act.activation(qT[1][:, i, :], bank[m % 2][:, 0:TOK], ACT.Copy).then_inc(qT_ready, 1)
                fold_hi(1, g)

            def step1(b, g, mb, slot, n):
                a, u = at[1], 2 * b + g
                if g == 0:
                    act.wait_ge(mbias_ready, b + 1)
                if n >= 3:
                    act.wait_ge(a.pv, 2 * (u - 2))
                for t in range(KT):
                    act.wait_ge(a.raw, u * KT + t + 1)
                    act.activation(tiles(slot)[:, t, :], praw[0:KP, t % 2, 0:QU], ACT.Identity,
                                   bias=mbias[:, mb, t:t + 1], scale=float(HD) ** -0.5).then_inc(a.score, 1)
                if n >= 3:
                    bp, gp = (b - 1, 0) if g == 1 else (b - 2, 1)
                    store_ac(1, bp, gp)
                if n >= 1:
                    for c in range(KT // EXPG):
                        exps(1, u - 1, (slot + 2) % 3, c)
            for u in range(4):
                step1(u // 2, u % 2, u // 2, slot_of(1, u), u)
            with act.Fori(0, 2) as i:
                for k in range(6):
                    step1(3 * i + 2 + k // 2, k % 2, (2 + k // 2) % 3, slot_of(1, 4 + k), 9)
            store_ac(1, B - 2, 1)
            for c in range(KT // EXPG):
                exps(1, NU - 1, slot_of(1, NU - 1), c)
            store_ac(1, B - 1, 0)
            store_ac(1, B - 1, 1)
            project(1)

            for k in range(KK):
                act.wait_ge(xnT_ps, 3 * KK + k + 1)
                act.activation(xnT[:, k, :], bank[2 + k][:, 0:TOK], ACT.Copy).then_inc(xnT_ready, 1)
            act.wait_ge(lg_sub, 1)
            act.activation(ex, lg, ACT.Exp).then_inc(lg_exp, 1)
            for n in range(NHT + NST):
                act.wait_ge(gu_ps, n + 1)
                wait(act, moeh, n - 1)
                act.activation(sil[:, n % 2, :], bank[2 * (n % 2)][0:IT, 0:TOK], ACT.Silu).then_inc(silu, 1)

        @block.vector
        def _(dve):
            links = [0]

            def link(ins):
                links[0] += 1
                ins.then_inc(chain, 1)
                dve.wait_ge(chain, links[0])

            def normalise(n, src, dst, eps, ready):
                for j in range(NT):
                    s = dve.bn_stats(stats[:, j, 0, :], src[:, j, :])
                link(s)
                for j in range(NT):
                    s = dve.bn_aggr(mv[:, j, :], stats[:, j, 0, :])
                link(s)
                dve.tensor_scalar(lnv[:, :], mv[:, :, 1], eps, None, ALU.add).then_inc(ln_var, 1)
                dve.wait_ge(ln_rstd, n + 1)
                for j in range(NT):
                    s = dve.tensor_scalar(dst[:, j, :], src[:, j, :], mv[:, j, 0:1], lnr[:, j:j + 1],
                                          ALU.subtract, ALU.mult)
                    if ready is not None:
                        s.then_inc(ready, 1)
                if ready is None:
                    link(s)

            dve.wait_ge(ld_x, 16)
            normalise(0, x_sb, xn, 1e-5, xn_ready)
            dve.wait_ge(ld_g, 32)
            dve.tensor_tensor(g2[:, 2:3], g2[:, 0:1], g2[:, 1:2], ALU.mult).then_inc(g_ready, 1)
            dve.wait_ge(g_ready, 1)
            for q in range(4):
                dve.wait_ge(wkT_ps, q + 1)
                dve.tensor_scalar(wkT[0][:, 4 * q:4 * q + 4, :], bank[q % 2].rearrange("p (h c) -> p h c", h=4),
                                  g2[:, 2:3], None, ALU.mult).then_inc(wkT_ready, 1)
            dve.wait_ge(wk_hi, 1)
            dve.scalar_tensor_tensor(out=wk16[:, 1, :], in0=wk_sb, scalar=16.0, in1=wk16[:, 0, :],
                                     op0=ALU.mult, op1=ALU.subtract).then_inc(wk_lo, 1)
            def context_lo(b):
                for q in range(3):
                    n = 3 * b + q
                    dve.wait_ge(ctxT_hi, n + 1)
                    dve.tensor_tensor(ctxT[:, 1, b, 4 * q:4 * q + 4, :].rearrange("p t n -> p (t n)"),
                                      praw[:, n % 2, 0:4 * KP],
                                      ctxT[:, 0, b, 4 * q:4 * q + 4, :].rearrange("p t n -> p (t n)"),
                                      ALU.subtract).then_inc(ctxT_lo, 1)

            def fold_lo(l, g):
                for i in range(HU):
                    n = l * H + g * HU + i
                    dve.wait_ge(qk_hi, n + 1)
                    dve.tensor_tensor(qk[:, :, g, 1, i * SQ:(i + 1) * SQ],
                                      fold_bank(l, n).rearrange("p (b q) -> p b q", b=B),
                                      qk[:, :, g, 0, i * SQ:(i + 1) * SQ], ALU.subtract).then_inc(qk_lo, 1)

            for g in range(2):
                for j in range(NT):
                    i = g * NT + j
                    dve.wait_ge(q_sq, i + 1)
                    link(dve.tensor_reduce(qss[:, :], qsq.rearrange("p (h d) -> p h d", h=HU), AX.X, ALU.add))
                    dve.tensor_scalar(qvar[:, :], qss[:, :], 1.0 / HD, 1e-5, ALU.mult, ALU.add).then_inc(q_var, 1)
                    context_lo(i)
                    dve.wait_ge(q_rstd, i + 1)
                    wait(dve, qT_ps, 2 * i)
                    dve.tensor_tensor(qn.rearrange("p (h d) -> p h d", h=HU),
                                      pk[0:TP, i % 2, :].rearrange("p (h d) -> p h d", h=HU),
                                      qrstd[:, :].unsqueeze(2).broadcast_to([TP, HU, HD]),
                                      ALU.mult).then_inc(qn_ready, 1)
                if g == 0:
                    fold_lo(0, 0)
            dve.wait_ge(ld_mask, 16)
            dve.tensor_copy(mask_f[:, :, :], mask_u8[:, :, :]).then_inc(mask_ready, 1)
            dve.wait_ge(mask_ready, 1)
            dve.tensor_scalar(half_bias[:, :, :], mask_f[:, :, :], -NEG / 2, NEG / 2, ALU.mult,
                              ALU.add).then_inc(mask_ready, 1)

            def key_sum(u, t):
                dve.wait_ge(k_sq, u * KT + t + 1)
                dve.tensor_reduce(ssq[:, t, :], sq[0:KP, t % 2, :].rearrange("p (h d) -> p h d", h=HU),
                                  AX.X, ALU.add).then_inc(k_red, 1)

            def key_var(u):
                dve.wait_ge(k_red, KT * (u + 1))
                dve.tensor_scalar(ssq[:, :, :], ssq[:, :, :], 1.0 / 256.0, HD * 1e-5, ALU.mult,
                                  ALU.add).then_inc(k_var, 1)

            def max_step(l, u, slot, t):
                a = at[l]
                s = tiles(slot)
                dve.wait_ge(a.score, u * KT + t + 1)
                if t > 1:
                    dve.wait_ge(a.mstep, u * (KT - 1) + t - 1)
                else:
                    wait(dve, a.maccT, u)
                dve.tensor_tensor(macc[:, :], s[:, 0, :] if t == 1 else macc[:, :], s[:, t, :],
                                  ALU.max).then_inc(a.mstep, 1)

            def max_col(l, u):
                a = at[l]
                dve.wait_ge(a.maccT, u + 1)
                dve.tensor_reduce(mcol[:, :], pA[0:TP, 0:QJ * KP].rearrange("p (j s) -> p j s", j=QJ), AX.X,
                                  ALU.max).then_inc(a.mcol, 1)

            def subtract(l, u, slot, c):
                a = at[l]
                if c == 0:
                    dve.wait_ge(a.mbc, u + 1)
                s = tiles(slot)[:, c * EXPG:(c + 1) * EXPG, :]
                dve.tensor_tensor(s, s, pA[0:KP, 0:QU].unsqueeze(1).broadcast_to([KP, EXPG, QU]),
                                  ALU.subtract).then_inc(a.sub, 1)

            def finish(l, u, outs, c):
                a = at[l]
                dve.wait_ge(a.pv, 2 * u + c + 1)
                v = outs[c][0:TP, 0:2 * CW].rearrange("p (j c) -> p j c", j=2)
                if c == 0:
                    wait(dve, a.acTps, u)
                r = rden[:, 2 * c:2 * c + 2]
                dve.tensor_scalar(r, v[:, :, CD], 1e-30, None, ALU.max).then_inc(a.rden, 1)
                dve.wait_ge(a.rden, 4 * u + 2 * c + 1)
                dve.reciprocal(r, r).then_inc(a.rden, 1)
                dve.wait_ge(a.rden, 4 * u + 2 * c + 2)
                dve.tensor_tensor(acn[:, 2 * c:2 * c + 2, :], v[:, :, 0:CD],
                                  r.unsqueeze(2).broadcast_to([TP, 2, CD]), ALU.mult).then_inc(a.acn, 1)

            def key_newton(u):
                r0, t, v = krstd[:, :, :], ktmp[:, :, :], ssq[:, :, :]
                dve.wait_ge(k_r0, u + 1)
                dve.scalar_tensor_tensor(out=t, in0=r0, scalar=-0.5, in1=r0, op0=ALU.mult,
                                         op1=ALU.mult).then_inc(k_newton, 1)
                dve.wait_ge(k_newton, 2 * u + 1)
                dve.tensor_tensor(t, t, v, ALU.mult).then_inc(k_newton, 1)
                dve.wait_ge(k_newton, 2 * u + 2)
                dve.scalar_tensor_tensor(out=r0, in0=t, scalar=1.5, in1=r0, op0=ALU.add,
                                         op1=ALU.mult).then_inc(k_rstd, 1)

            for t in range(KT):
                key_sum(0, t)
            key_var(0)
            fold_lo(0, 1)
            key_newton(0)

            def step0(b, g, n):
                a, u = at[0], 2 * b + g
                s = tiles(slot_of(0, g)).rearrange("p t (h q) -> p t h q", h=HU)
                dve.wait_ge(k_rstd, u + 1)
                if n == 0:
                    dve.wait_ge(qT_ps, 4 * NT)
                    dve.wait_ge(qk_ps, H)
                if n not in (0, 1):
                    dve.wait_ge(a.pv, 2 * (u - 1))
                for t in range(KT):
                    dve.wait_ge(a.raw, u * KT + t + 1)
                    dve.tensor_tensor(s[:, t, :, :], praw[0:KP, t % 2, 0:QU].rearrange("p (h q) -> p h q", h=HU),
                                      krstd[:, t, :].unsqueeze(2).broadcast_to([KP, HU, SQ]),
                                      ALU.mult).then_inc(a.score, 1)
                m = 1
                if n != -1:
                    for t in range(KT):
                        key_sum(u + 1, t)
                        if t in (3, 6, 9):
                            max_step(0, u, slot_of(0, g), m)
                            m += 1
                    key_var(u + 1)
                for t in range(m, KT):
                    max_step(0, u, slot_of(0, g), t)
                if n != -1:
                    key_newton(u + 1)
                if n != 0:
                    finish(0, u - 1, (pA, pB), 0)
                    finish(0, u - 1, (pA, pB), 1)
                max_col(0, u)
            for g in range(2):
                step0(0, g, g)
            with dve.Fori(1, B - 1) as b:
                for g in range(2):
                    step0(b, g, None)
            step0(B - 1, 0, None)
            step0(B - 1, 1, -1)
            for c in range(2):
                finish(0, NU - 1, (pA, pB), c)

            def residual(l):
                dve.wait_ge(at[l].y, 1)
                for j in range(NT):
                    dve.tensor_tensor(x_sb[:, j, :], bank[j][0:TP, 0:DM], x_sb[:, j, :],
                                      ALU.add).then_inc(at[l].x, 1)
                dve.wait_ge(at[l].x, NT)
            dve.wait_ge(wsum_ps, 1)
            inv = 1.0 / float(FF * DM)
            dve.tensor_scalar(gam[:, :], pA[:, 0:2], inv, None, ALU.mult).then_inc(gam_ready, 1)
            dve.wait_ge(gam_ready, 1)
            dve.tensor_scalar(thr[:, 0, :], gam[:, :], 1e-6, 0.5, ALU.add, ALU.mult)
            link(dve.tensor_scalar(thr[:, 1, :], gam[:, :], 1e-6, -0.5, ALU.add, ALU.mult))
            for i, (w, tt) in enumerate(((wfc_sb, t_fc), (wpj_sb, t_pj))):
                w2, t2 = w.rearrange("p o d -> p (o d)"), tt.rearrange("p o d -> p (o d)")
                wait(dve, tern, i)
                link(dve.tensor_scalar(tneg, w2, thr[:, 1, i:i + 1], None, ALU.is_lt))
                dve.scalar_tensor_tensor(out=t2, in0=w2, scalar=thr[:, 0, i:i + 1], in1=tneg,
                                         op0=ALU.is_gt, op1=ALU.subtract).then_inc(tern, 1)
            residual(0)

            for q in range(8):
                dve.wait_ge(ternT_ps, q + 1)
                pt = (pA16 if q % 2 == 0 else pB16)[:, 0:512]
                if q < 4:
                    dve.tensor_copy(fcT[:, q // 2, 512 * (q % 2):512 * (q % 2) + 512], pt).then_inc(ternT, 1)
                else:
                    dve.tensor_copy(pjT[:, 2 * (q - 4):2 * (q - 4) + 2, :],
                                    pt.rearrange("p (o n) -> p o n", o=2)).then_inc(ternT, 1)

            def clip_absmax(src, j, ready):
                dve.tensor_scalar(src[:, j, :], src[:, j, :], amx[:, j:j + 1], namx[:, j:j + 1],
                                  ALU.min, ALU.max).then_inc(ready, 1)

            def absmax(src):
                for j in range(NT):
                    dve.tensor_reduce(amx[:, j:j + 1], src[:, j, :], AX.X, ALU.max)
                    s = dve.tensor_reduce(namx[:, j:j + 1], src[:, j, :], AX.X, ALU.min)
                link(s)
                link(dve.scalar_tensor_tensor(out=namx[:, :], in0=amx[:, :], scalar=-1.0, in1=namx[:, :],
                                              op0=ALU.mult, op1=ALU.min))
                link(dve.tensor_scalar(amx[:, :], namx[:, :], -1.0, None, ALU.mult))

            normalise(1, x_sb, xn, 1e-5, None)
            normalise(2, xn, xn, 1e-6, None)
            absmax(xn)
            for j in range(NT):
                clip_absmax(xn, j, z_ready)
            for k in range(KK):
                dve.wait_ge(zT_hi, k + 1)
                dve.tensor_tensor(zT[:, 1, k, :], bank[2 + k][:, 0:TOK], zT[:, 0, k, :],
                                  ALU.subtract).then_inc(zT_lo, 1)
            for j in range(NT):
                dve.wait_ge(h_act, j + 1)
                for n in range(2):
                    s = dve.bn_stats(stats[:, j, n, :], hbuf[:, j, n * 512:(n + 1) * 512])
            link(s)
            for j in range(NT):
                s = dve.bn_aggr(mv[:, j, :], stats[:, j, :, :])
            link(s)
            dve.tensor_scalar(lnv[:, :], mv[:, :, 1], 1e-6, None, ALU.add).then_inc(ln_var, 1)
            dve.wait_ge(ln_rstd, 4)
            for j in range(NT):
                s = dve.tensor_scalar(hbuf[:, j, :], hbuf[:, j, :], mv[:, j, 0:1], lnr[:, j:j + 1],
                                      ALU.subtract, ALU.mult)
            link(s)
            absmax(hbuf)
            for j in range(NT):
                clip_absmax(hbuf, j, h_ready)
            for o in range(FO):
                dve.wait_ge(hT_hi, o + 1)
                dve.tensor_tensor(hT16[:, 1, o, :], praw[:, o % 2, 0:TOK], hT16[:, 0, o, :],
                                  ALU.subtract).then_inc(hT_lo, 1)
            for j in range(NT):
                dve.wait_ge(f_ps, j + 1)
                dve.scalar_tensor_tensor(out=x_sb[:, j, :], in0=bank[j][0:TP, 0:DM], scalar=gam[0:TP, 1:2],
                                         in1=x_sb[:, j, :], op0=ALU.mult, op1=ALU.add).then_inc(f_done, 1)
            dve.wait_ge(f_done, NT)

            for q in range(2):
                dve.wait_ge(wkT_ps, 5 + q)
                dve.tensor_copy(wkT[1][:, 4 * q:4 * q + 4, :],
                                (pA if q == 0 else pB)[:, :].rearrange("p (h c) -> p h c", h=4)).then_inc(wkT_ready, 1)
            normalise(4, x_sb, xn, 1e-5, xn_ready)
            for g in range(2):
                fold_lo(1, g)

            def step1(b, g, slot, n):
                u = 2 * b + g
                subs = list(range(KT // EXPG)) if n >= 1 else []
                for t in range(1, KT):
                    max_step(1, u, slot, t)
                    if t >= 4 and t % 2 == 0 and subs:
                        subtract(1, u - 1, (slot + 2) % 3, subs.pop(0))
                if n >= 2:
                    finish(1, u - 2, (bank[0], bank[1]), 0)
                max_col(1, u)
                if n >= 2:
                    finish(1, u - 2, (bank[0], bank[1]), 1)
            for u in range(4):
                step1(u // 2, u % 2, slot_of(1, u), u)
            with dve.Fori(0, 2) as i:
                for k in range(6):
                    step1(3 * i + 2 + k // 2, k % 2, slot_of(1, 4 + k), 9)
            for c in range(KT // EXPG):
                subtract(1, NU - 1, slot_of(1, NU - 1), c)
            for u in (NU - 2, NU - 1):
                for c in range(2):
                    finish(1, u, (bank[0], bank[1]), c)
            residual(1)

            normalise(5, x_sb, xn, 1e-5, xn_ready)
            dve.wait_ge(gwT_ps, 1)
            dve.tensor_copy(gwT, pA[:, 0:KK * E].rearrange("p (k e) -> p k e", k=KK)).then_inc(gwT_ready, 1)
            dve.wait_ge(lg_ps, 1)
            pl = pB[0:TP, 0:NT * E].rearrange("p (j e) -> p j e", j=NT)
            link(dve.tensor_reduce(rmx, pl, AX.X, ALU.max))
            dve.tensor_tensor(lg, pl, rmx.unsqueeze(2).broadcast_to([TP, NT, E]), ALU.subtract).then_inc(lg_sub, 1)
            dve.wait_ge(lg_exp, 1)
            link(dve.tensor_reduce(rsm, ex, AX.X, ALU.add))
            link(dve.reciprocal(rsm, rsm))
            link(dve.tensor_tensor(lg, ex, rsm.unsqueeze(2).broadcast_to([TP, NT, E]), ALU.mult))
            other = lg.unsqueeze(2).broadcast_to([TP, NT, E, E])
            own = lg.unsqueeze(3).broadcast_to([TP, NT, E, E])
            dve.tensor_tensor(gt, other, own, ALU.is_gt)
            link(dve.tensor_tensor(eq, other, own, ALU.is_equal))
            dve.wait_ge(tri_ready, 1)
            link(dve.tensor_tensor(eq, eq, tri.unsqueeze(1).broadcast_to([TP, NT, E, E]), ALU.mult))
            link(dve.tensor_tensor(gt, gt, eq, ALU.add))
            link(dve.tensor_reduce(rank, gt, AX.X, ALU.add))
            dve.scalar_tensor_tensor(out=comb, in0=rank, scalar=1.5, in1=lg, op0=ALU.is_lt,
                                     op1=ALU.mult).then_inc(comb_ready, 1)
            for n in range(NHT + NST):
                dve.wait_ge(silu, n + 1)
                dve.tensor_tensor(hT[:, n, :], sil[:, n % 2, :], bank[2 * (n % 2) + 1][0:IT, 0:TOK],
                                  ALU.mult).then_inc(moeh, 1)
            dve.wait_ge(comb_ready, 1)
            i = 0
            for j in range(NT):
                for e in range(E + 1):
                    dve.wait_ge(ye_ps, i + 1)
                    wait(dve, ye_used, i)
                    y = praw[0:TP, i % 2, 0:DM]
                    if e < E:
                        dve.scalar_tensor_tensor(out=x_sb[:, j, :], in0=y, scalar=comb[:, j, e:e + 1],
                                                 in1=x_sb[:, j, :], op0=ALU.mult, op1=ALU.add).then_inc(ye_used, 1)
                    else:
                        dve.tensor_tensor(x_sb[:, j, :], y, x_sb[:, j, :], ALU.add).then_inc(ye_used, 1)
                    i += 1


_INS = ['x', 'ctx_1024', 'mask_BxS2_bf1', 'L0_xattn_Wq', 'L0_xattn_Wk', 'L0_xattn_Wv', 'L0_xattn_Wo',
        'L0_xattn_gq', 'L0_xattn_gk', 'L0_ffn_w_fc', 'L0_ffn_w_proj', 'L1_xattn_Wq', 'L1_xattn_Wk',
        'L1_xattn_Wv', 'L1_xattn_Wo', 'L1_ffn_gate_w', 'L1_ffn_w_gate', 'L1_ffn_w_up', 'L1_ffn_w_down',
        'L1_ffn_sw_gate', 'L1_ffn_sw_up', 'L1_ffn_sw_down']


def kernel(**inputs):
    import numpy as _np
    import concourse.bacc as _bacc
    from concourse import mybir as _mybir
    from concourse.bass_utils import run_bass_kernel_spmd as _run

    nc = _bacc.Bacc("TRN2", target_bir_lowering=False, num_devices=1)
    arrays, args = {}, []
    for name in _INS:
        a = _np.ascontiguousarray(inputs[name])
        if a.dtype == _np.bool_:
            a = a.view(_np.uint8)
        arrays[f"in_{name}_dram"] = a
        args.append(nc.dram_tensor(f"in_{name}_dram", a.shape, _mybir.dt.from_np(a.dtype), kind="ExternalInput").ap())
    out = nc.dram_tensor("out_dram", (B, SQ, DM), F32, kind="ExternalOutput").ap()
    build(nc, *args, out)
    r = _run(nc, [arrays], core_ids=[0])
    return r.results[0]["out_dram"]
```

```python
import math
from contextlib import ExitStack

import concourse.bass as bass
from concourse import mybir

ALU = mybir.AluOpType
ACT = mybir.ActivationFunctionType
AX = mybir.AxisListType
F32 = mybir.dt.float32
F16 = mybir.dt.float16
U8 = mybir.dt.uint8

B, SQ, DM = 8, 56, 256
SK, CD = 1500, 128
H, HD = 16, 128
KV1 = 8
KP, KT = 125, 12
NT, TP = 4, 112
TOK = NT * TP
KK = DM // 128
HU = 8
QU = HU * SQ
QJ = QU // TP
NU = B * H // HU
SW = KT * QU
FF = 4 * DM
FO = FF // 128
E, EI = 8, 176
EH, HID = E * EI, (E + 2) * EI
NHC = -(-HID // 128)
NEC = EH // 128
LR = HID - 128 * (NHC - 1)
WOS = 64.0
HSCALE = 2.0 ** 11
KR = KT // 2
LATE = 3
EXPG = 3
NC = KT // EXPG
CH = EXPG * QU
NSC = 2
SHIFT = 11 * math.log(2.0)
NEG = -1.0e30


def wait(eng, sem, value):
    if isinstance(value, int) and value <= 0:
        return
    eng.wait_ge(sem, value)


def build(nc, x, ctx, mask, Wq0, Wk0, Wv0, Wo0, gq, gk, w_fc, w_proj,
          Wq1, Wk1, Wv1, Wo1, gate_w, w_gate, w_up, w_down, sw_gate, sw_up, sw_down, out):
    with ExitStack() as st:
        def sb(name, shape, dt=F32):
            return st.enter_context(nc.sbuf_tensor(name, shape, dt))

        def ps(name, shape, dt=F32):
            return st.enter_context(nc.psum_tensor(name, shape, dt))

        def sem(name):
            return st.enter_context(nc.semaphore(name))

        ctx_flat = sb("ctx16", [128, B * 2 * KT * CD], F16)[:, :]
        ctx16 = ctx_flat.rearrange("p (b l t c) -> p b l t c", b=B, l=2, t=KT)
        ctxT_flat = sb("ctxT", [128, 2 * B * KT * KP], F16)[:, :]
        ctxT = ctxT_flat.rearrange("p (l b t n) -> p l b t n", l=2, b=B, t=KT)
        S_flat = sb("S", [128, 2 * SW])[:, :]
        S = S_flat.rearrange("p (r n) -> p r n", r=2)
        qk_flat = sb("qk", [128, B * 2 * 2 * QU], F16)[:, :]
        qk = qk_flat.rearrange("p (g b l n) -> p b g l n", b=B, g=2, l=2)
        acT = qk_flat.bitcast(F32).rearrange("p (g b n) -> p b g n", b=B, g=2)
        CB = KT * CD
        stages = [t[0:KP].rearrange("p (t c) -> p t c", t=KT) for t in (
            qk_flat.bitcast(F32)[:, B * QU:B * QU + CB], qk_flat.bitcast(F32)[:, B * QU + CB:B * QU + 2 * CB],
            ctx_flat.bitcast(F32)[:, (B - 1) * CB:B * CB])]

        def stage(b):
            return stages[b % 3]

        wbuf = sb("wbuf", [128, 6144])
        x_sb = sb("x_sb", [TP, NT, DM])
        xn_flat = sb("xn", [128, NT * DM])[:, :]
        xn = xn_flat[0:TP].rearrange("p (j d) -> p j d", j=NT)
        xnT = sb("xnT", [128, KK, TOK])
        ident = sb("ident", [128, 128])
        ident16 = sb("ident16", [128, 128], F16)
        ones = sb("ones", [128, 128])
        ones16 = sb("ones16", [128, 128], F16)
        macc_flat = sb("macc", [128, QU])[:, :]
        macc = macc_flat[0:KP]
        rden = macc_flat
        msp = sb("msp", [KP, QU])
        mcol = sb("mcol", [TP, QJ])
        ssq, krstd, ktmp = [t.rearrange("p (t h) -> p t h", t=KT) for t in (
            xnT[0:KP, :, :].rearrange("p k n -> p (k n)")[:, CH // 2:CH // 2 + KT * HU],
            xnT[0:KP, :, :].rearrange("p k n -> p (k n)")[:, CH // 2 + KT * HU:CH // 2 + 2 * KT * HU],
            wbuf[0:KP, SW + CH // 2:SW + CH // 2 + KT * HU])]
        mask_u8 = sb("mask_u8", [KP, B, KT], U8)
        mask_f = sb("mask_f", [KP, B, KT])
        half_bias = sb("half_bias", [KP, B + 3, KT])
        shift = sb("shift", [128, 1])
        mbias = sb("mbias", [KP, 3, KT])
        mhalf = sb("mhalf", [128, 1])
        stats = sb("stats", [TP, NT, 2, 6])
        mv = sb("mv", [TP, NT, 2])
        lnv = sb("lnv", [TP, NT])
        lnr = sb("lnr", [TP, NT])
        qss = sb("qss", [TP, HU])
        qvar = sb("qvar", [TP, HU])
        qrstd = sb("qrstd", [TP, HU])
        g2 = sb("g2", [128, 3])
        wsum = sb("wsum", [128, 2])
        gam = sb("gam", [128, 2])
        thr = sb("thr", [128, 2, 2])
        ext = sb("ext", [TP, NT, 2])
        amx = sb("amx", [TP, NT])
        namx = sb("namx", [TP, NT])

        S0, S1 = S[:, 0, :], S[:, 1, :]
        slots = [S0, S1, wbuf[:, 0:SW]]

        xnT_flat = xnT[:, :, :].rearrange("p k n -> p (k n)")
        hi_place = [t[0:KP].bitcast(F16).rearrange("p (t n) -> p t n", t=EXPG) for t in (
            wbuf[:, SW:SW + CH // 2], xnT_flat[:, 0:CH // 2], xn_flat[:, 0:CH // 2], S1[:, 4608:4608 + CH // 2])]
        dacc = [S1[0:KP, 4096:4096 + QU], msp[:, :]]

        def p_hi(l, slot, c):
            return hi_place[c if l == 0 else (slot + c) % 3]

        def chunk(slot, c):
            return slots[slot][0:KP, c * CH:(c + 1) * CH].rearrange("p (t n) -> p t n", t=EXPG)

        def p_lo(slot, c):
            return slots[slot][0:KP, c * CH:c * CH + CH // 2].bitcast(F16).rearrange("p (t n) -> p t n", t=EXPG)

        def tiles(slot):
            return slots[slot][0:KP].rearrange("p (t n) -> p t n", t=KT)

        def slot_of(l, u):
            return (0, 2)[u % 2] if l == 0 else u % 3

        wq_sb = S0[:, 0:KK * H * HD].rearrange("p (k n) -> p k n", k=KK)
        qn = S0[0:TP, 4096:5120]
        wk1_sb = S0[:, 4096:4096 + KV1 * HD]
        wkT = [wbuf[:, 0:2048].rearrange("p (h c) -> p h c", h=H),
               wbuf[:, 4096:5120].rearrange("p (h c) -> p h c", h=KV1)]
        qT = [wbuf[:, 2048:2048 + HU * TOK].rearrange("p (h t) -> p h t", h=HU),
              S1[:, 0:HU * TOK].rearrange("p (h t) -> p h t", h=HU)]
        NWQ, QW = 4, KK * H * HD // 4
        wq_quarter = [S0[:, QW * q:QW * (q + 1)] for q in range(NWQ)]
        wq_h16 = wbuf[:, 2048:4096].bitcast(F16)
        wq_l16 = [w.bitcast(F16)[:, 0:QW] for w in wq_quarter]
        xq16 = xnT_flat.bitcast(F16).rearrange("p (l k t) -> p l k t", l=2, k=KK)
        wk_sb = S1[:, 2048:4096]
        wk16 = S1[:, 0:2048].bitcast(F16).rearrange("p (l n) -> p l n", l=2)
        sq = S1[:, 2048:4096].rearrange("p (r n) -> p r n", r=2)
        qsq = S1[0:TP, 4096:5120]
        wv_sb = S1[:, 0:2048].rearrange("p (h c) -> p h c", h=H)
        wo_lo = S1[:, 2048:4096].rearrange("p (h n) -> p h n", h=HU)
        wo_hi = [S0[:, 0:2048].rearrange("p (h n) -> p h n", h=HU),
                 wbuf[:, 0:2048].rearrange("p (h n) -> p h n", h=HU)]
        oT = [t.bitcast(F16).rearrange("p (l r t) -> p l r t", l=2, r=2)
              for t in (S0[:, 2048:2048 + 2 * TOK], wbuf[:, 2048:2048 + 2 * TOK])]
        wo_h16 = [t.bitcast(F16).rearrange("p (h n) -> p h n", h=H)
                  for t in (S0[:, 2944:4992], wbuf[:, 2944:4992])]

        WQ = 4

        def wo_part(l, q):
            t, h = (wo_lo, WQ * q) if WQ * q < HU else (wo_hi[l], WQ * q - HU)
            return t[:, h:h + WQ, :]

        def wo_l16(l, q):
            return wo_part(l, q).rearrange("p h n -> p (h n)").bitcast(F16)[:, 0:WQ * DM] \
                .rearrange("p (h n) -> p h n", h=WQ)

        wfc_sb = wbuf[:, 0:2048].rearrange("p (o d) -> p o d", o=FO)
        wpj_sb = wbuf[:, 2048:4096].rearrange("p (o d) -> p o d", o=KK)
        t_fc = wbuf[:, 4096:5120].bitcast(F16).rearrange("p (o d) -> p o d", o=FO)
        t_pj = wbuf[:, 5120:6144].bitcast(F16).rearrange("p (o d) -> p o d", o=KK)
        tneg = S0[:, 2944:3968].bitcast(F16)
        wabs_out = S1[:, 4096:5120].bitcast(F16)
        fcT = wbuf[:, 0:1024].bitcast(F16).rearrange("p (k n) -> p k n", k=KK)
        pjT = wbuf[:, 1024:2048].bitcast(F16).rearrange("p (o n) -> p o n", o=FO)
        hT16 = S1[:, 0:3584].bitcast(F16).rearrange("p (l o t) -> p l o t", l=2, o=FO)
        zT = S1[:, 3584:3584 + 896].bitcast(F16).rearrange("p (l k t) -> p l k t", l=2, k=KK)
        hbuf = qk_flat.bitcast(F32)[0:TP, 0:NT * FF] \
            .rearrange("p (j n) -> p j n", j=NT)
        moe = ctxT_flat.bitcast(F32)
        GU = 2 * KK * HID
        gu16 = ctx_flat[:, 0:2 * GU].rearrange("p (l n) -> p l n", l=2)
        gu16c = gu16.rearrange("p l (w k c) -> p l w k c", w=2, k=KK)
        WDW = NHC * DM
        wd16_flat = ctxT_flat[:, 0:2 * WDW].rearrange("p (l n) -> p l n", l=2)
        wd16 = wd16_flat.rearrange("p l (n d) -> p l n d", d=DM)
        gu_sb = moe[:, 0:GU].rearrange("p (w k c) -> p w k c", w=2, k=KK)
        gw_sb = moe[0:E, 7040:7296]
        gwT = moe[:, 7296:7312].rearrange("p (k e) -> p k e", k=KK)
        sil = moe[:, 7400:7400 + 2 * TOK].rearrange("p (r t) -> p r t", r=2)
        lg = moe[0:TP, 8400:8432].rearrange("p (j e) -> p j e", j=NT)
        ex = moe[0:TP, 8432:8464].rearrange("p (j e) -> p j e", j=NT)
        comb = moe[0:TP, 8464:8496].rearrange("p (j e) -> p j e", j=NT)
        rank = moe[0:TP, 8496:8528].rearrange("p (j e) -> p j e", j=NT)
        rmx = moe[0:TP, 8528:8532]
        rsm = moe[0:TP, 8532:8536]
        gt = moe[0:TP, 8600:8856].rearrange("p (j a b) -> p j a b", j=NT, a=E)
        eq = moe[0:TP, 8856:9112].rearrange("p (j a b) -> p j a b", j=NT, a=E)
        tri = moe[0:TP, 9112:9176].rearrange("p (a b) -> p a b", a=E)
        sel = moe[0:E, 9200:9200 + EH // 2].bitcast(F16)
        combT16 = moe[0:E, 9904:9904 + TOK].bitcast(F16).rearrange("p (l t) -> p l t", l=2)
        wd_flat = ctx_flat.bitcast(F32)[:, GU:GU + WDW]
        wd_sb = wd_flat.rearrange("p (n d) -> p n d", d=DM)
        h16 = S_flat[:, :].bitcast(F16)[:, 0:2 * NHC * TOK].rearrange("p (l n t) -> p l n t", l=2, t=TOK)
        xnT16 = wbuf[:, 3072:3072 + KK * TOK].bitcast(F16).rearrange("p (l k t) -> p l k t", l=2, k=KK)
        hprod = wbuf[:, 4096:4096 + 2 * TOK].rearrange("p (r t) -> p r t", r=2)
        CHUNKS = (*range(NEC, NHC), *range(NEC))
        NSH = NHC - NEC

        def chunk_rows(n):
            return LR if n == NHC - 1 else 128

        pk = ps("pk", [128, 2, 1024])
        praw = ps("praw", [128, 2, 512])
        pA = ps("pA", [128, 512])
        pB = ps("pB", [128, 512])
        ye = (pA[0:TP, 0:DM], pA[0:TP, DM:2 * DM], pB[0:TP, 0:DM], pB[0:TP, DM:2 * DM])
        pA16 = pA[:, :].bitcast(F16)
        pB16 = pB[:, :].bitcast(F16)
        bank = [pk[:, 0, 0:512], pk[:, 0, 512:1024], pk[:, 1, 0:512], pk[:, 1, 512:1024]]

        PV0, DEN0 = pB[:, 0:QU], pA[:, 0:QU]

        PV_LAST, DEN_LAST = bank[0][:, 0:QU], bank[1][:, 0:QU]
        DEN1 = bank[2][:, 0:QU]

        RAW = ((*bank, praw[:, 0, :], praw[:, 1, :]), (praw[:, 0, :], praw[:, 1, :], bank[3]))

        def raw_bank(l, t):
            return RAW[l][t % len(RAW[l])][0:KP, 0:QU]

        def fold_bank(n):
            return (praw[:, n % 2, :] if n % 4 < 2 else (pA, pB)[n % 2][:, :])[:, 0:TOK]

        ld_x, ld_g, ld_wk, ld_wq, ld_mask = sem("ld_x"), sem("ld_g"), sem("ld_wk"), sem("ld_wq"), sem("ld_mask")
        ld_ctx = [sem(f"ld_ctx{b}") for b in range(B)]
        ld_wvo = [sem(f"ld_wvo{l}") for l in range(2)]
        ld_wo_hi = [sem(f"ld_wo_hi{l}") for l in range(2)]
        ld_ffn, ld_wq1, ld_wk1, ld_moe, ld_wd = sem("ld_ffn"), sem("ld_wq1"), sem("ld_wk1"), sem("ld_moe"), sem("ld_wd")
        idz, consts, chain, pchain = sem("idz"), sem("consts"), sem("chain"), sem("pchain")
        ln_var, ln_rstd, xn_ready, xnT_ps, xnT_ready = (sem("ln_var"), sem("ln_rstd"), sem("xn_ready"),
                                                        sem("xnT_ps"), sem("xnT_ready"))
        ctxT_ps, ctxT_hi, ctxT_lo = sem("ctxT_ps"), sem("ctxT_hi"), sem("ctxT_lo")
        ctx_hi, ctx_lo = sem("ctx_hi"), sem("ctx_lo")
        wk_hi, wk_lo, wkT_ps, wkT_ready, g_ready = (sem("wk_hi"), sem("wk_lo"), sem("wkT_ps"),
                                                    sem("wkT_ready"), sem("g_ready"))
        q_ps, q_sq, q_var, q_rstd, qn_ready, qT_ps, qT_ready = (sem("q_ps"), sem("q_sq"), sem("q_var"), sem("q_rstd"),
                                                                sem("qn_ready"), sem("qT_ps"), sem("qT_ready"))
        qk_ps, qk_hi, qk_lo = sem("qk_ps"), sem("qk_hi"), sem("qk_lo")
        k_ps, k_sq, k_red, k_var, k_rstd = sem("k_ps"), sem("k_sq"), sem("k_red"), sem("k_var"), sem("k_rstd")
        k_ln, k_r0, k_newton = sem("k_ln"), sem("k_r0"), sem("k_newton")
        mask_ready, mbias_ready, ctx_masked = sem("mask_ready"), sem("mbias_ready"), sem("ctx_masked")

        class Attn:
            def __init__(self, l):
                self.raw = sem(f"raw{l}")
                self.score = sem(f"score{l}")
                self.mstep = sem(f"mstep{l}")
                self.maccT = sem(f"maccT{l}")
                self.mcol = sem(f"mcol{l}")
                self.mbc = sem(f"mbc{l}")
                self.msp = sem(f"msp{l}")
                self.sub = sem(f"sub{l}")
                self.exp = sem(f"exp{l}")
                self.hi = sem(f"hi{l}")
                self.dsum = sem(f"dsum{l}")
                self.lo = sem(f"lo{l}")
                self.pv = sem(f"pv{l}")
                self.den = sem(f"den{l}")
                self.rden = sem(f"rden{l}")
                self.ac = sem(f"ac{l}")
                self.oT_ps = sem(f"oT_ps{l}")
                self.oT = sem(f"oT{l}")
                self.oT_lo = sem(f"oT_lo{l}")
                self.wo = sem(f"wo{l}")
                self.wo_l = sem(f"wo_l{l}")
                self.y = sem(f"y{l}")
                self.x = sem(f"x{l}")
        at = [Attn(0), Attn(1)]
        last_sub, last_lo = sem("last_sub"), sem("last_lo")

        def wait_used(eng, l, v, c):
            if c < NSC:
                wait(eng, at[l].pv, NC * v + c + 1)
            else:
                wait(eng, at[l].den, (NC - NSC) * v + c - NSC + 1)

        wabs, wsum_ps, gam_ready, tern, ternT_ps, ternT = (sem("wabs"), sem("wsum_ps"), sem("gam_ready"),
                                                          sem("tern"), sem("ternT_ps"), sem("ternT"))
        h_var, h_rstd = sem("h_var"), sem("h_rstd")
        z_ready, zT_ps, zT_hi, zT_lo = sem("z_ready"), sem("zT_ps"), sem("zT_hi"), sem("zT_lo")
        h_ps, h_act, h_ready, hT_ps, hT_hi, hT_lo, f_ps, f_done = (sem("h_ps"), sem("h_act"), sem("h_ready"),
            sem("hT_ps"), sem("hT_hi"), sem("hT_lo"), sem("f_ps"), sem("f_done"))
        w_hi, w_lo, xn_hi, xn_lo, moeh_hi, moeh_lo = (sem("w_hi"), sem("w_lo"), sem("xn_hi"), sem("xn_lo"),
                                                      sem("moeh_hi"), sem("moeh_lo"))
        gwT_ps, gwT_ready, lg_ps, lg_sub, lg_exp, comb_ready = (sem("gwT_ps"), sem("gwT_ready"), sem("lg_ps"),
            sem("lg_sub"), sem("lg_exp"), sem("comb_ready"))
        gu_ps, silu, moeh, ye_ps, ye_used, tri_ready = (sem("gu_ps"), sem("silu"), sem("moeh"), sem("ye_ps"),
                                                       sem("ye_used"), sem("tri_ready"))
        sel_ready, combT_ps, combT_hi, combT_lo, wt_ps, glu = (sem("sel_ready"), sem("combT_ps"), sem("combT_hi"),
                                                              sem("combT_lo"), sem("wt_ps"), sem("glu"))
        stored = sem("stored")

        GUP, WDH, WDF = 4, NHC // 2 * DM, (NHC - 1) * DM
        pieces = [(moe[:, n0:n1], gu16[:, 0, n0:n1], gu16[:, 1, n0:n1])
                  for n0, n1 in ((q * GU // GUP, (q + 1) * GU // GUP) for q in range(GUP))] \
            + [(wd_flat[0:rows, n0:n1], wd16_flat[0:rows, 0, n0:n1], wd16_flat[0:rows, 1, n0:n1])
               for rows, n0, n1 in ((128, 0, WDH), (128, WDH, WDF), (LR, WDF, WDW))]
        NPC = len(pieces)
        WSTEPS = (5, 6, 8, 9, 11, 12, 14)
        LD_MOE = 16 * (2 * KK + 3)

        block = st.enter_context(nc.Block())

        @block.sync
        def _(sp):
            xv = x.rearrange("b s d -> (b s) d").rearrange("(j p) d -> p j d", p=TP)
            cv = ctx.rearrange("b (p t) c -> p b t c", t=KT)
            sp.dma_start(x_sb[:, :, :], xv).then_inc(ld_x, 16)
            sp.dma_start(wk_sb, Wk0).then_inc(ld_wk, 16)
            sp.dma_start(g2[:, 0:1], gq.rearrange("(d a) -> d a", a=1)).then_inc(ld_g, 16)
            sp.dma_start(g2[:, 1:2], gk.rearrange("(d a) -> d a", a=1)).then_inc(ld_g, 16)
            sp.dma_start(stage(0), cv[:, 0]).then_inc(ld_ctx[0], 16)
            sp.dma_start(wq_sb, Wq0.rearrange("(k p) n -> p k n", p=128)).then_inc(ld_wq, 16)
            sp.dma_start(stage(1), cv[:, 1]).then_inc(ld_ctx[1], 16)
            sp.dma_start(mask_u8[:, :, :], mask.rearrange("b (p t) -> p b t", t=KT)).then_inc(ld_mask, 16)
            for b in range(2, B):
                wait(sp, ctxT_ps, 3 * (b - 2))
                wait(sp, ctx_lo, b - 2)
                sp.dma_start(stage(b), cv[:, b]).then_inc(ld_ctx[b], 16)
            wait(sp, k_ps, NU * KT)
            wait(sp, k_red, NU * KT)
            sp.dma_start(wv_sb, Wv0.rearrange("c (h d) -> c h d", h=H)).then_inc(ld_wvo[0], 16)
            wo0_v = Wo0.rearrange("(h d) n -> d h n", h=H)
            sp.dma_start(wo_lo, wo0_v[:, 0:HU, :]).then_inc(ld_wvo[0], 16)
            wait_used(sp, 0, NU - 2, NC - 1)
            sp.dma_start(wo_hi[0], wo0_v[:, HU:H, :]).then_inc(ld_wo_hi[0], 16)
            wait_used(sp, 0, NU - 1, NC - 1)
            sp.dma_start(wfc_sb, w_fc.rearrange("(o p) d -> p o d", p=128)).then_inc(ld_ffn, 16)
            sp.dma_start(wpj_sb, w_proj.rearrange("(o p) d -> p o d", p=128)).then_inc(ld_ffn, 16)
            wait(sp, at[0].y, 1)
            wait(sp, tern, 2)
            sp.dma_start(wk1_sb, Wk1).then_inc(ld_wk1, 16)
            sp.dma_start(wq_sb, Wq1.rearrange("(k p) n -> p k n", p=128)).then_inc(ld_wq1, 16)
            wait_used(sp, 1, NU - 3, NC - 1)
            sp.dma_start(wv_sb[:, 0:KV1, :], Wv1.rearrange("c (h d) -> c h d", h=KV1)).then_inc(ld_wvo[1], 16)
            wo1_v = Wo1.rearrange("(h d) n -> d h n", h=H)
            sp.dma_start(wo_lo, wo1_v[:, 0:HU, :]).then_inc(ld_wvo[1], 16)
            wait_used(sp, 1, NU - 2, NC - 1)
            sp.dma_start(wo_hi[1], wo1_v[:, HU:H, :]).then_inc(ld_wo_hi[1], 16)
            wait(sp, at[1].raw, NU * KT)
            for w, (experts, shared) in enumerate(((w_gate, sw_gate), (w_up, sw_up))):
                for k in range(KK):
                    sp.dma_start(gu_sb[:, w, k, 0:EH].rearrange("p (e i) -> p e i", e=E),
                                 experts[:, k * 128:(k + 1) * 128, :].rearrange("e p i -> p e i")).then_inc(ld_moe, 16)
                sp.dma_start(gu_sb[:, w, :, EH:HID], shared.rearrange("(k p) i -> p k i", p=128)).then_inc(ld_moe, 16)
            sp.dma_start(gw_sb, gate_w).then_inc(ld_moe, 16)
            wait_used(sp, 1, NU - 1, NC - 1)
            sp.dma_start(wd_sb[:, 0:NEC, :], w_down.rearrange("e i d -> (e i) d")
                         .rearrange("(n p) d -> p n d", p=128)).then_inc(ld_wd, 16)
            sp.dma_start(wd_sb[:, NEC:NHC - 1, :], sw_down[0:2 * EI - LR, :]
                         .rearrange("(n p) d -> p n d", p=128)).then_inc(ld_wd, 16)
            sp.dma_start(wd_sb[0:LR, NHC - 1, :], sw_down[2 * EI - LR:2 * EI, :]).then_inc(ld_wd, 16)
            ov = out.rearrange("b s d -> (b s) d").rearrange("(j p) d -> p j d", p=TP)
            for i in range(2):
                sp.wait_ge(ye_used, 2 * i + 2)
                sp.dma_start(ov[:, 2 * i:2 * i + 2, :], x_sb[:, 2 * i:2 * i + 2, :]).then_inc(stored, 16)
            sp.wait_ge(stored, 32)

        @block.gpsimd
        def _(pool):
            pool.memset(ident[:, :], 0.0).then_inc(idz, 1)
            pool.memset(ident16[:, :], 0.0).then_inc(idz, 1)
            pool.wait_ge(idz, 2)
            for m in (ident, ident16):
                pool.affine_select(out=m[:, :], in_=m[:, :], compare_op=ALU.not_equal, fill=1.0, base=0,
                                   pattern=[[-1, 128]], channel_multiplier=1).then_inc(consts, 1)
            pool.memset(mhalf[:, :], -0.5).then_inc(consts, 1)
            pool.memset(ones[:, :], 1.0).then_inc(consts, 1)
            pool.memset(ones16[:, :], 1.0).then_inc(consts, 1)
            pool.memset(shift[:, :], SHIFT).then_inc(consts, 1)
            pool.memset(half_bias[:, B:B + 3, :], 0.0).then_inc(consts, 1)
            pool.wait_ge(consts, 7)

            def ln_pow(n):
                pool.wait_ge(ln_var, n + 1)
                pool.tensor_tensor(lnr[:, :], lnv[:, :], mhalf[0:TP, :].broadcast_to([TP, NT]), ALU.pow).then_inc(ln_rstd, 1)

            ln_pow(0)
            def q_pow(i):
                pool.wait_ge(q_var, i + 1)
                pool.tensor_tensor(qrstd[:, :], qvar[:, :], mhalf[0:TP, :].broadcast_to([TP, HU]), ALU.pow).then_inc(q_rstd, 1)
            q_pow(0)
            for i in range(2 * NT):
                if i + 1 < 2 * NT:
                    q_pow(i + 1)
                pool.wait_ge(ctx_hi, i + 1)
                pool.tensor_tensor(ctx16[0:KP, i, 1], stage(i), ctx16[0:KP, i, 0],
                                   ALU.subtract).then_inc(ctx_lo, 1)

            def subtract0(u, slot, c):
                pool.tensor_tensor(chunk(slot, c), chunk(slot, c),
                                   msp[:, :].unsqueeze(1).broadcast_to([KP, EXPG, QU]),
                                   ALU.subtract).then_inc(at[0].sub, 1)

            def sum_weights(l, u, slot, c, first):
                a, s = at[l], chunk(slot, c)
                pool.wait_ge(a.exp, NC * u + c + 1)
                steps = (NSC * EXPG - 1) * u
                for t in range(EXPG):
                    i = c * EXPG + t
                    if i == 0:
                        continue
                    if i == 1:
                        if not first:
                            wait_used(pool, l, u - 1, NSC)
                    else:
                        pool.wait_ge(a.dsum, steps + i - 1)
                    pool.tensor_tensor(dacc[l], s[:, 0, :] if i == 1 else dacc[l], s[:, t, :], ALU.add).then_inc(a.dsum, 1)

            def low_halves(l, u, slot, c):
                a = at[l]
                pool.wait_ge(a.hi, NC * u + c + 1)
                if c < NSC:
                    pool.wait_ge(a.dsum, (NSC * EXPG - 1) * u + c * EXPG + EXPG - 1)
                pool.tensor_tensor(p_lo(slot, c), chunk(slot, c), p_hi(l, slot, c), ALU.subtract).then_inc(a.lo, 1)

            def unit0(u, slot, first):
                pool.wait_ge(at[0].msp, u + 1)
                subtract0(u, slot, 0)
                for c in range(NC):
                    if c + 1 < NC:
                        subtract0(u, slot, c + 1)
                    if c < NSC:
                        sum_weights(0, u, slot, c, first)
                    low_halves(0, u, slot, c)

            for g in range(2):
                unit0(g, slot_of(0, g), g == 0)
            with pool.Fori(1, B - 1) as b:
                for g in range(2):
                    unit0(2 * b + g, slot_of(0, g), False)
            unit0(NU - 2, slot_of(0, 0), False)
            for c in range(NSC):
                sum_weights(0, NU - 1, slot_of(0, 1), c, False)

            pool.wait_ge(at[0].pv, NC * NU)
            pool.wait_ge(mask_ready, 2)
            def mask_context(b):
                for l in range(2):
                    pool.tensor_tensor(ctx16[0:KP, b, l], ctx16[0:KP, b, l],
                                       mask_f[:, b, :].unsqueeze(2).broadcast_to([KP, KT, CD]),
                                       ALU.mult).then_inc(ctx_masked, 1)
            with pool.Fori(0, 5) as b:
                mask_context(b)
            for n in (1, 2):
                ln_pow(n)
            for j in range(NT):
                pool.wait_ge(h_var, j + 1)
                pool.tensor_tensor(lnr[:, j:j + 1], lnv[:, j:j + 1], mhalf[0:TP, :], ALU.pow).then_inc(h_rstd, 1)
                for q in ((), (0,), (1, 2), (3,))[j]:
                    pool.wait_ge(w_hi, q + 1)
                    pool.tensor_tensor(wq_l16[q], wq_quarter[q], wq_h16[:, QW * q:QW * (q + 1)],
                                       ALU.subtract).then_inc(w_lo, 1)
            ln_pow(3)
            with pool.Fori(5, B) as b:
                mask_context(b)

            def mask_bias(b, mb):
                pool.tensor_tensor(mbias[:, mb, :], half_bias[:, b, :], half_bias[:, b, :],
                                   ALU.add).then_inc(mbias_ready, 1)

            def unit1(b, g, mb, slot, first=False):
                u = 2 * b + g
                for c in range(NC):
                    if c < NSC:
                        sum_weights(1, u, slot, c, first)
                    low_halves(1, u, slot, c)
                if g == 1:
                    pool.wait_ge(at[1].score, KT * (u + 1))
                    mask_bias(b + 3, mb)
            for b in range(3):
                mask_bias(b, b)
            for u in range(4):
                unit1(u // 2, u % 2, u // 2, slot_of(1, u), u == 0)
            with pool.Fori(0, 2) as i:
                for k in range(6):
                    unit1(3 * i + 2 + k // 2, k % 2, (2 + k // 2) % 3, slot_of(1, 4 + k))
            pool.wait_ge(at[1].raw, NU * KT)
            pool.memset(tri, 1.0).then_inc(pchain, 1)
            pool.wait_ge(pchain, 1)
            pool.affine_select(out=tri, in_=tri, compare_op=ALU.is_gt, fill=0.0, base=0,
                               pattern=[[1, E], [-1, E]], channel_multiplier=0).then_inc(tri_ready, 1)
            pool.memset(sel, 1.0 / HSCALE).then_inc(pchain, 1)
            for i in range(2):
                pool.wait_ge(pchain, 2 + i)
                pool.affine_select(out=sel, in_=sel, compare_op=ALU.is_gt, fill=0.0, base=(1, EI)[i],
                                   pattern=[[(1, -1)[i], EH]],
                                   channel_multiplier=(-EI, EI)[i]).then_inc((pchain, sel_ready)[i], 1)
            ln_pow(4)
            for s, n in enumerate(CHUNKS):
                rows = chunk_rows(n)
                pool.wait_ge(moeh_hi, s + 1)
                pool.tensor_tensor(h16[0:rows, 1, n, :], hprod[0:rows, s % 2, :], h16[0:rows, 0, n, :],
                                   ALU.subtract).then_inc(moeh_lo, 1)

        @block.tensor
        def _(pe):
            def transpose(out_, in_, idn):
                k = in_.shape[0]
                return pe.transpose(out_, in_, idn[0:k, 0:k])

            def stream_T(n, ready, count):
                wait(pe, ready, count)
                for k in range(KK):
                    for j in range(NT):
                        mm = transpose(bank[2 + k][:, j * TP:(j + 1) * TP], xn[:, j, k * 128:(k + 1) * 128], ident)
                    mm.then_inc(xnT_ps, 1)

            pe.wait_ge(consts, 7)
            pe.wait_ge(ld_wk, 16)
            for q in range(4):
                wait(pe, wkT_ready, q - 1)
                for i in range(4):
                    h = 4 * q + i
                    mm = transpose(bank[q % 2][:, i * 128:(i + 1) * 128], wk_sb[:, h * 128:(h + 1) * 128], ident)
                mm.then_inc(wkT_ps, 1)
            def context_T(b, quads):
                pe.wait_ge(ld_ctx[b], 16)
                for q in quads:
                    n = 3 * b + q
                    wait(pe, ctxT_lo, n - 1)
                    for i in range(4):
                        mm = transpose(praw[:, n % 2, i * KP:(i + 1) * KP], stage(b)[:, 4 * q + i, :], ident)
                    mm.then_inc(ctxT_ps, 1)
            stream_T(0, xn_ready, NT)

            def fold_head(l, g, i):
                n, h = l * H + g * HU + i, g * HU + i
                wait(pe, qk_lo, n - 3)
                w = wkT[0][:, h, :] if l == 0 else wkT[1][:, h // 2, :]
                pe.matmul(fold_bank(n), w, qT[l][:, i, :], start=True, stop=True).then_inc(qk_ps, 1)

            def fold(l, g):
                for i in range(HU):
                    fold_head(l, g, i)

            def queries(i):
                g, j = i // NT, i % NT
                wait(pe, qn_ready, i - 1)
                for n in range(2):
                    for k in range(KK):
                        mm = pe.matmul(pk[0:TP, i % 2, n * 512:(n + 1) * 512], xnT[:, k, j * TP:(j + 1) * TP],
                                       wq_sb[:, k, g * 1024 + n * 512:g * 1024 + (n + 1) * 512],
                                       start=(k == 0), stop=(k == KK - 1))
                mm.then_inc(q_ps, 1)

            pe.wait_ge(ld_wq, 16)
            pe.wait_ge(xnT_ready, 2)
            pe.wait_ge(wkT_ready, 4)
            queries(0)
            for i in range(2 * NT):
                if i == NT:
                    pe.wait_ge(qk_lo, HU)
                context_T(i, (0, 1))
                if i + 1 < 2 * NT:
                    queries(i + 1)
                context_T(i, (2,))
                pe.wait_ge(qn_ready, i + 1)
                for n in range(2):
                    m = 2 * i + n
                    wait(pe, qT_ready, m - 1)
                    pt = pA if n == 0 else pB
                    for r in range(4):
                        hh = 4 * n + r
                        mm = transpose(pt[:, r * TP:(r + 1) * TP], qn[:, hh * 128:(hh + 1) * 128], ident)
                    mm.then_inc(qT_ps, 1)
                if i == NT - 1:
                    pe.wait_ge(qT_ready, 2 * NT)
                    pe.wait_ge(ctxT_lo, 3 * NT)
                    fold(0, 0)

            def keys(b, g, before=None):
                u = 2 * b + g
                for t in range(KT):
                    if before:
                        before(t)
                    nc.disable_value_cache = True
                    if t >= 2:
                        pe.wait_ge(k_sq, u * KT + t - 1)
                    else:
                        wait(pe, at[0].score, (u - 1) * KT + 8 + 2 * t)
                    for n in range(2):
                        o = pk[0:KP, t % 2, n * 512:(n + 1) * 512]
                        c0 = g * 1024 + n * 512
                        for i, (lc, lw) in enumerate(((0, 0), (0, 1), (1, 0))):
                            mm = pe.matmul(o, ctxT[:, lc, b, t, :], wk16[:, lw, c0:c0 + 512],
                                           start=(i == 0), stop=(i == 2))
                    mm.then_inc(k_ps, 1)
                    nc.disable_value_cache = False

            def scores(l, b, g, before=None):
                a, u = at[l], 2 * b + g
                for t in range(KT):
                    if before:
                        before(t)
                    if l == 1:
                        wait(pe, a.score, u * KT + t - len(RAW[1]) + 1)
                    elif t >= len(RAW[0]):
                        pe.wait_ge(a.score, u * KT + t - len(RAW[0]) + 1)
                    elif t in (0, 2):
                        pe.wait_ge(k_sq, u * KT + KT - 1 + t // 2)
                    elif t == 4:
                        wait(pe, a.score, u * KT)
                    for i, (lc, lq) in enumerate(((0, 0), (0, 1), (1, 0))):
                        mm = pe.matmul(raw_bank(l, t), ctxT[:, lc, b, t, :], qk[:, b, g, lq, :],
                                       start=(i == 0), stop=(i == 2))
                    mm.then_inc(a.raw, 1)

            def max_T(l, u):
                a = at[l]
                pe.wait_ge(a.mstep, (KT - 1) * (u + 1))
                for j in range(QJ):
                    mm = transpose(pA[0:TP, j * KP:(j + 1) * KP], macc[:, j * TP:(j + 1) * TP], ident)
                mm.then_inc(a.maccT, 1)

            def max_spread(l, u):
                a = at[l]
                pe.wait_ge(a.mcol, u + 1)
                for j in range(QJ):
                    mm = pe.transpose((pA, pB)[l][0:KP, j * TP:(j + 1) * TP], mcol[:, j:j + 1].broadcast_to([TP, KP]),
                                      ident[0:TP, 0:TP])
                mm.then_inc(a.mbc, 1)

            def attend(l, b, g, slot, c, pv):
                a, u = at[l], 2 * b + g
                nc.disable_value_cache = True
                if c == 0 and pv is not PV_LAST:
                    wait(pe, a.ac, u - l)
                pe.wait_ge(a.hi, NC * u + c + 1)
                for t in range(EXPG):
                    for lc in range(2):
                        pe.matmul(pv, ctx16[0:KP, b, lc, EXPG * c + t, :], p_hi(l, slot, c)[:, t, :],
                                  start=(c == 0 and t == 0 and lc == 0), stop=False)
                if l == 0 and isinstance(u, int) and u == NU - 1:
                    pe.wait_ge(last_lo, c + 1)
                else:
                    pe.wait_ge(a.lo, NC * u + c + 1)
                for t in range(EXPG):
                    mm = pe.matmul(pv, ctx16[0:KP, b, 0, EXPG * c + t, :], p_lo(slot, c)[:, t, :],
                                   start=False, stop=(c == NC - 1 and t == EXPG - 1))
                mm.then_inc(a.pv, 1)
                nc.disable_value_cache = False

            def total(l, u, slot, c, den):
                a = at[l]
                if c == NSC:
                    pe.wait_ge(a.dsum, (NSC * EXPG - 1) * (u + 1))
                    pe.matmul(den, ones[0:KP, :], dacc[l], start=True, stop=False)
                for t in range(EXPG):
                    pe.matmul(den, ones16[0:KP, :], p_hi(l, slot, c)[:, t, :], start=False, stop=False)
                    mm = pe.matmul(den, ones16[0:KP, :], p_lo(slot, c)[:, t, :], start=False,
                                   stop=(c == NC - 1 and t == EXPG - 1))
                mm.then_inc(a.den, 1)

            pe.wait_ge(wk_lo, 1)
            pe.wait_ge(qn_ready, 2 * NT)
            def fold_in_keys(t):
                if t == 2:
                    pe.wait_ge(qT_ready, 4 * NT)
                    pe.wait_ge(ctxT_lo, 6 * NT)
                if 2 <= t < 2 + HU:
                    fold_head(0, 1, t - 2)
            keys(0, 0, fold_in_keys)
            pe.wait_ge(qk_lo, H)
            pe.wait_ge(ctx_lo, B)

            def step0(b, g, n):
                u = 2 * b + g
                bp, gp = (b, 0) if g == 1 else (b - 1, 1)

                def in_scores(t):
                    if t == 5 and n != 0:
                        max_T(0, u - 1)
                    if t == 7 and n != 0:
                        max_spread(0, u - 1)
                    if t == 9 and n not in (0, 1):
                        pe.wait_ge(at[0].msp, u)
                        total(0, u - 2, slot_of(0, g), NSC, DEN0)
                        attend(0, b - 1, g, slot_of(0, g), NC - 1, PV0)
                        total(0, u - 2, slot_of(0, g), NC - 1, DEN0)

                def in_keys(t):
                    if t in (4, 9) and n != 0:
                        attend(0, bp, gp, slot_of(0, gp), t // 5, PV0)
                scores(0, b, g, in_scores)
                if n != -1:
                    bn, gn = (b, 1) if g == 0 else (b + 1, 0)
                    keys(bn, gn, in_keys)
                if n not in (0, -1):
                    attend(0, bp, gp, slot_of(0, gp), 2, PV0)

            for g in range(2):
                step0(0, g, g)
            with pe.Fori(1, B - 1) as b:
                for g in range(2):
                    step0(b, g, None)
            step0(B - 1, 0, None)
            step0(B - 1, 1, -1)
            attend(0, B - 1, 0, slot_of(0, 0), 0, PV0)
            max_T(0, NU - 1)
            max_spread(0, NU - 1)
            for c in range(1, NC):
                attend(0, B - 1, 0, slot_of(0, 0), c, PV0)
                if c == NSC:
                    pe.wait_ge(last_sub, NC)
                if c >= NSC:
                    total(0, NU - 2, slot_of(0, 0), c, DEN0)
            for c in range(NC):
                attend(0, B - 1, 1, slot_of(0, 1), c, PV_LAST)
                if c >= NSC:
                    total(0, NU - 1, slot_of(0, 1), c, DEN_LAST)

            def project(l):
                a = at[l]
                pe.wait_ge(a.ac, NU)
                pe.wait_ge(ld_wvo[l], 32)
                for h in range(H + 1):
                    if h < H:
                        wait(pe, a.oT_lo, h - 1)
                        g, i = h // HU, h % HU
                        w = wv_sb[:, h, :] if l == 0 else wv_sb[:, h // 2, :]
                        pe.matmul(praw[:, h % 2, 0:TOK].rearrange("p (b q) -> p b q", b=B), w,
                                  acT[:, :, g, i * SQ:(i + 1) * SQ],
                                  start=True, stop=True).then_inc(a.oT_ps, 1)
                    if h > 0:
                        pe.wait_ge(a.oT_lo, h)
                        q, r = (h - 1) // WQ, (h - 1) % WQ
                        if r == 0:
                            pe.wait_ge(a.wo_l, q + 1)
                        w = (wo_h16[l][:, h - 1, :], wo_l16(l, q)[:, r, :])
                        for j in range(NT):
                            for lo_, lw in ((0, 0), (0, 1), (1, 0)):
                                mm = pe.matmul(bank[j][0:TP, 0:DM], oT[l][:, lo_, (h - 1) % 2, j * TP:(j + 1) * TP],
                                               w[lw], start=(h == 1 and lo_ + lw == 0), stop=(h == H and lo_ == 1))
                        if h == H:
                            mm.then_inc(a.y, 1)
                    if l == 0 and h == HU:
                        pe.wait_ge(wabs, 2)
                        pe.matmul(pA[:, 0:2], ones[:, :], wsum[:, :], start=True, stop=True).then_inc(wsum_ps, 1)
            project(0)

            pe.wait_ge(gam_ready, 1)
            pe.wait_ge(tern, 2)
            for q in range(8):
                wait(pe, ternT, q - 1)
                pt = pA16 if q % 2 == 0 else pB16
                for i in range(4):
                    if q < 4:
                        src = t_fc[:, 4 * (q % 2) + i, (q // 2) * 128:(q // 2 + 1) * 128]
                    else:
                        o = 2 * (q - 4) + i // 2
                        src = t_pj[:, i % 2, o * 128:(o + 1) * 128]
                    mm = transpose(pt[:, i * 128:(i + 1) * 128], src, ident16)
                mm.then_inc(ternT_ps, 1)
            pe.wait_ge(at[0].x, NT)
            stream_T(1, z_ready, NT)
            pe.wait_ge(ternT, 8)
            pe.wait_ge(zT_lo, 2)
            for j in range(NT):
                wait(pe, h_act, j - 1)
                for n in range(2):
                    i = 0
                    for k in range(KK):
                        for l in range(2):
                            mm = pe.matmul(pk[0:TP, j % 2, n * 512:(n + 1) * 512], zT[:, l, k, j * TP:(j + 1) * TP],
                                           fcT[:, k, n * 512:(n + 1) * 512], start=(i == 0), stop=(i == 3))
                            i += 1
                mm.then_inc(h_ps, 1)
            for j in range(NT + 1):
                if j < NT:
                    pe.wait_ge(h_ready, j + 1)
                    wait(pe, hT_lo, 2 * j)
                    for r in range(2):
                        for o in range(4):
                            mm = transpose(praw[:, r, o * TP:(o + 1) * TP],
                                           hbuf[:, j, (4 * r + o) * 128:(4 * r + o + 1) * 128], ident)
                        mm.then_inc(hT_ps, 1)
                if j > 0:
                    pe.wait_ge(hT_lo, 2 * j)
                    if j == 1:
                        pe.wait_ge(h_act, NT)
                    for o in range(FO):
                        for l in range(2):
                            mm = pe.matmul(bank[j - 1][0:TP, 0:DM], hT16[:, l, o, (j - 1) * TP:j * TP], pjT[:, o, :],
                                           start=(o == 0 and l == 0), stop=(o == FO - 1 and l == 1))
                    mm.then_inc(f_ps, 1)

            pe.wait_ge(ld_wk1, 16)
            for q in range(2):
                for i in range(4):
                    h = 4 * q + i
                    mm = transpose((pA if q == 0 else pB)[:, i * 128:(i + 1) * 128],
                                   wk1_sb[:, h * 128:(h + 1) * 128], ident)
                mm.then_inc(wkT_ps, 1)
            pe.wait_ge(f_done, NT)
            stream_T(2, xn_ready, 2 * NT)
            pe.wait_ge(xnT_ready, 4)
            pe.wait_ge(w_lo, NWQ)
            pe.wait_ge(xn_lo, KK)
            pe.wait_ge(wkT_ready, 6)
            for m in range(H + 2):
                if m < H:
                    wait(pe, qT_ready, 16 + m - 1)
                    nc.disable_value_cache = True
                    for k in range(KK):
                        q, c = divmod((k * H + m) * HD, QW)
                        w = (wq_h16[:, q * QW + c:q * QW + c + HD], wq_l16[q][:, c:c + HD])
                        for lw, lx in ((0, 0), (0, 1), (1, 0)):
                            mm = pe.matmul(bank[m % 2][:, 0:TOK], w[lw], xq16[:, lx, k, :],
                                           start=(k == 0 and lw + lx == 0), stop=(k == KK - 1 and lw == 1))
                    nc.disable_value_cache = False
                    mm.then_inc(qT_ps, 1)
                if m >= 2:
                    pe.wait_ge(qT_ready, 16 + m - 1)
                    fold_head(1, (m - 2) // HU, (m - 2) % HU)
            pe.wait_ge(qk_lo, 2 * H)

            def attend1(b, g, slot, c):
                attend(1, b, g, slot, c, bank[g][:, 0:QU])
                if c == NSC:
                    wait(pe, at[1].rden, 2 * b + g)
                if c >= NSC:
                    total(1, 2 * b + g, slot, c, DEN1)

            def step1(b, g, slot, n):
                u = 2 * b + g

                def in_scores(t):
                    if t == 2 and n >= 1:
                        max_T(1, u - 1)
                    if t == 4 and n >= 1:
                        if n >= 2:
                            pe.wait_ge(at[1].sub, NC * (u - 1))
                        max_spread(1, u - 1)
                    if t > 0 and t % EXPG == 0 and n >= 2:
                        attend1(b - 1, g, (slot + 1) % 3, t // EXPG - 1)
                scores(1, b, g, in_scores)
                if n >= 2:
                    attend1(b - 1, g, (slot + 1) % 3, NC - 1)
            for u in range(4):
                step1(u // 2, u % 2, slot_of(1, u), u)
            with pe.Fori(0, 2) as i:
                for k in range(6):
                    step1(3 * i + 2 + k // 2, k % 2, slot_of(1, 4 + k), 9)
            max_T(1, NU - 1)
            for c in range(NC):
                attend1(B - 1, 0, slot_of(1, NU - 2), c)
                if c == 0:
                    pe.wait_ge(at[1].sub, NC * (NU - 1))
                    max_spread(1, NU - 1)
            for c in range(NC):
                attend1(B - 1, 1, slot_of(1, NU - 1), c)
            project(1)

            pe.wait_ge(ld_moe, LD_MOE)
            for k in range(KK):
                mm = transpose(pA[:, k * E:(k + 1) * E], gw_sb[:, k * 128:(k + 1) * 128], ident)
            mm.then_inc(gwT_ps, 1)
            pe.wait_ge(at[1].x, NT)
            stream_T(3, xn_ready, 3 * NT)
            pe.wait_ge(xnT_ready, 6)
            pe.wait_ge(gwT_ready, 1)
            for j in range(NT):
                for k in range(KK):
                    mm = pe.matmul(pB[0:TP, j * E:(j + 1) * E], xnT[:, k, j * TP:(j + 1) * TP], gwT[:, k, :],
                                   start=(k == 0), stop=(k == KK - 1))
            mm.then_inc(lg_ps, 1)
            pe.wait_ge(w_lo, NWQ + GUP)
            pe.wait_ge(xn_lo, 2 * KK)

            def gate_up(s):
                n, rows = CHUNKS[s], chunk_rows(CHUNKS[s])
                wait(pe, moeh, s - 1)
                for w in range(2):
                    for i, (k, lw, lx) in enumerate((k, lw, lx) for k in range(KK) for lw, lx in ((0, 0), (0, 1), (1, 0))):
                        mm = pe.matmul(bank[2 * (s % 2) + w][0:rows, 0:TOK],
                                       gu16c[:, lw, w, k, n * 128:n * 128 + rows],
                                       xnT16[:, lx, k, :], start=(i == 0), stop=(i == 3 * KK - 1))
                mm.then_inc(gu_ps, 1)

            def spread_combine(s):
                n = CHUNKS[s]
                for lc in range(2):
                    mm = pe.matmul(praw[:, s % 2, 0:TOK], sel[:, n * 128:(n + 1) * 128], combT16[:, lc, :],
                                   start=(lc == 0), stop=(lc == 1))
                mm.then_inc(wt_ps, 1)

            def down(s):
                n, rows = CHUNKS[s], chunk_rows(CHUNKS[s])
                pe.wait_ge(moeh_lo, s + 1)
                for j in range(NT):
                    for lh, lw in ((0, 0), (0, 1), (1, 0)):
                        mm = pe.matmul(ye[j], h16[0:rows, lh, n, j * TP:(j + 1) * TP], wd16[0:rows, lw, n, :],
                                       start=(s == 0 and lh + lw == 0 and j % 2 == 0),
                                       stop=(s == NHC - 1 and lh == 1 and j % 2 == 1))
                    if s == NHC - 1 and j % 2 == 1:
                        mm.then_inc(ye_ps, 1)

            for s in range(NHC):
                gate_up(s)
                if s == 1:
                    pe.wait_ge(comb_ready, 1)
                    for j in range(NT):
                        mm = transpose(praw[0:E, 0, j * TP:(j + 1) * TP], comb[:, j, :], ident)
                    mm.then_inc(combT_ps, 1)
                if s == NSH:
                    pe.wait_ge(sel_ready, 1)
                    pe.wait_ge(combT_lo, 1)
                if s >= NSH:
                    spread_combine(s)
                if s == 2:
                    pe.wait_ge(w_lo, NWQ + NPC)
                    pe.wait_ge(lg_sub, 1)
                if s >= 2:
                    down(s - 2)
            down(NHC - 2)
            down(NHC - 1)

        @block.scalar
        def _(act):
            act.wait_ge(ld_wk, 16)
            act.activation(wk16[:, 0, :], wk_sb, ACT.Copy, scale=16.0).then_inc(wk_hi, 1)

            def context_hi(b, quads):
                for q in quads:
                    n = 3 * b + q
                    act.wait_ge(ctxT_ps, n + 1)
                    act.activation(ctxT[:, 0, b, 4 * q:4 * q + 4, :].rearrange("p t n -> p (t n)"),
                                   praw[:, n % 2, 0:4 * KP], ACT.Copy).then_inc(ctxT_hi, 1)

            def stream_copy(n):
                for k in range(KK):
                    act.wait_ge(xnT_ps, KK * n + k + 1)
                    act.activation(xnT[:, k, :], bank[2 + k][:, 0:TOK], ACT.Copy).then_inc(xnT_ready, 1)
            stream_copy(0)

            def fold_hi_head(l, g, i):
                n = l * H + g * HU + i
                act.wait_ge(qk_ps, n + 1)
                act.activation(qk[:, :, g, 0, i * SQ:(i + 1) * SQ],
                               fold_bank(n).rearrange("p (b q) -> p b q", b=B), ACT.Copy).then_inc(qk_hi, 1)

            def fold_hi(l, g):
                for i in range(HU):
                    fold_hi_head(l, g, i)

            def q_square(i):
                act.wait_ge(q_ps, i + 1)
                wait(act, q_var, i)
                act.activation(qsq, pk[0:TP, i % 2, :], ACT.Square).then_inc(q_sq, 1)
            q_square(0)
            for i in range(2 * NT):
                j = i % NT
                context_hi(i, (0, 1))
                if i + 1 < 2 * NT:
                    q_square(i + 1)
                context_hi(i, (2,))
                if i == B - 1:
                    act.wait_ge(ctx_lo, i - 1)
                act.activation(ctx16[0:KP, i, 0], stage(i), ACT.Copy).then_inc(ctx_hi, 1)
                for n in range(2):
                    act.wait_ge(qT_ps, 2 * i + n + 1)
                    if i == NT and n == 0:
                        act.wait_ge(qk_ps, HU)
                    pt = pA if n == 0 else pB
                    act.activation(qT[0][:, 4 * n:4 * n + 4, j * TP:(j + 1) * TP],
                                   pt[:, 0:4 * TP].rearrange("p (h t) -> p h t", h=4),
                                   ACT.Copy).then_inc(qT_ready, 1)
                if i == NT - 1:
                    fold_hi(0, 0)

            def square(u, t):
                act.wait_ge(k_ps, u * KT + t + 1)
                wait(act, k_red, u * KT + t - 1)
                act.activation(sq[0:KP, t % 2, :], pk[0:KP, t % 2, :], ACT.Square).then_inc(k_sq, 1)

            def exponential(l, u, slot, c):
                if l == 0 and isinstance(u, int) and u == NU - 1:
                    act.wait_ge(last_sub, c + 1)
                else:
                    act.wait_ge(at[l].sub, u * NC + c + 1)
                act.activation(chunk(slot, c), chunk(slot, c), ACT.Exp, bias=shift[0:KP, :]).then_inc(at[l].exp, 1)

            def high_half(l, u, slot, c, first):
                a = at[l]
                if l == 0 and not first:
                    wait_used(act, 0, u - 1, c)
                if l == 1 and (c == NC - 1 or not first):
                    wait_used(act, 1, u if c == NC - 1 else u - 1, (c + 1) % NC)
                act.wait_ge(a.exp, u * NC + c + 1)
                act.activation(p_hi(l, slot, c), chunk(slot, c), ACT.Copy).then_inc(a.hi, 1)

            def exps(l, u, slot, c, first=False):
                exponential(l, u, slot, c)
                high_half(l, u, slot, c, first)

            def copy_max(u):
                act.wait_ge(at[0].mbc, u + 1)
                act.activation(msp[:, :], pA[0:KP, 0:QU], ACT.Copy).then_inc(at[0].msp, 1)

            def key_r0(u, r):
                i, ts = 2 * u + r, slice(r * KR, (r + 1) * KR)
                act.wait_ge(k_var, i + 1)
                act.activation(ktmp[:, ts, :], ssq[:, ts, :], ACT.Ln).then_inc(k_ln, 1)
                act.wait_ge(k_ln, i + 1)
                act.activation(krstd[:, ts, :], ktmp[:, ts, :], ACT.Exp, scale=-0.5).then_inc(k_r0, 1)

            act.preload_act_table_set("natural_log_exp_and_others")
            act.wait_ge(wkT_ps, 4)
            act.wait_ge(wk_lo, 1)
            for t in range(KT):
                if t == 2:
                    act.wait_ge(ctx_lo, B)
                if 2 <= t < 2 + HU:
                    fold_hi_head(0, 1, t - 2)
                square(0, t)
            key_r0(0, 0)
            key_r0(0, 1)

            def step0(b, g, n):
                u = 2 * b + g

                def exps0(c):
                    if n != 0:
                        exps(0, u - 1, slot_of(0, 1 - g), c, n == 1)
                if n != 0:
                    copy_max(u - 1)
                exps0(0)
                for t in range(KT):
                    if n != -1:
                        square(u + 1, t)
                    if t in (1, 6):
                        exps0((1, 6).index(t) + 1)
                    if t == KR + 2 and n != -1:
                        key_r0(u + 1, 0)
                if n != -1:
                    key_r0(u + 1, 1)
                exps0(NC - 1)
            for g in range(2):
                step0(0, g, g)
            with act.Fori(1, B - 1) as b:
                for g in range(2):
                    step0(b, g, None)
            step0(B - 1, 0, None)
            step0(B - 1, 1, -1)
            for c in range(NC):
                exps(0, NU - 1, slot_of(0, 1), c)

            def split_wo(l, q):
                if q == 0:
                    wait_used(act, l, NU - 2, NC - 1)
                    act.wait_ge(ld_wvo[l], 32)
                if q == HU // WQ:
                    act.wait_ge(ld_wo_hi[l], 16)
                act.activation(wo_h16[l][:, WQ * q:WQ * (q + 1), :], wo_part(l, q), ACT.Copy,
                               scale=WOS).then_inc(at[l].wo, 1)

            def project(l):
                a = at[l]
                split_wo(l, 0)
                split_wo(l, 1)
                for h in range(H):
                    act.wait_ge(a.oT_ps, h + 1)
                    act.activation(oT[l][:, 0, h % 2, :], praw[:, h % 2, 0:TOK], ACT.Copy).then_inc(a.oT, 1)
                    if h in (1, 3):
                        split_wo(l, 2 + h // 2)
                    if l == 1 and h in WSTEPS:
                        i = WSTEPS.index(h)
                        act.wait_ge(ld_moe, LD_MOE)
                        if i >= GUP:
                            act.wait_ge(ld_wd, 48)
                            act.wait_ge(w_lo, NWQ + GUP)
                        act.activation(pieces[i][1], pieces[i][0], ACT.Copy).then_inc(w_hi, 1)
                    if l == 0 and h in (3, 5):
                        i = (h - 3) // 2
                        act.wait_ge(ld_ffn, 32)
                        wait(act, wabs, i)
                        act.activation(wabs_out, (wfc_sb, wpj_sb)[i].rearrange("p o d -> p (o d)"), ACT.Abs,
                                       accum_out=wsum[:, i:i + 1]).then_inc(wabs, 1)
            project(0)

            for q in range(8):
                act.wait_ge(ternT_ps, q + 1)
                pt = (pA16 if q % 2 == 0 else pB16)[:, 0:512]
                if q < 4:
                    act.activation(fcT[:, q // 2, 512 * (q % 2):512 * (q % 2) + 512], pt, ACT.Copy).then_inc(ternT, 1)
                else:
                    act.activation(pjT[:, 2 * (q - 4):2 * (q - 4) + 2, :],
                                   pt.rearrange("p (o n) -> p o n", o=2), ACT.Copy).then_inc(ternT, 1)
            for k in range(KK):
                act.wait_ge(xnT_ps, KK + k + 1)
                act.activation(zT[:, 0, k, :], bank[2 + k][:, 0:TOK], ACT.Copy).then_inc(zT_hi, 1)
            act.wait_ge(gam_ready, 1)
            for j in range(NT):
                act.wait_ge(h_ps, j + 1)
                act.activation(hbuf[:, j, :], pk[0:TP, j % 2, :], ACT.Gelu, scale=gam[0:TP, 0:1]).then_inc(h_act, 1)
            for j in range(NT):
                for q in ((0, 1), (2, 3), (), ())[j]:
                    act.wait_ge(ld_wq1, 16)
                    act.activation(wq_h16[:, QW * q:QW * (q + 1)], wq_quarter[q], ACT.Copy).then_inc(w_hi, 1)
                for r in range(2):
                    act.wait_ge(hT_ps, 2 * j + r + 1)
                    act.activation(hT16[:, 0, 4 * r:4 * r + 4, j * TP:(j + 1) * TP],
                                   praw[:, r, 0:TOK].rearrange("p (o t) -> p o t", o=4), ACT.Copy).then_inc(hT_hi, 1)

            for q in range(2):
                act.wait_ge(wkT_ps, 5 + q)
                act.activation(wkT[1][:, 4 * q:4 * q + 4, :],
                               (pA if q == 0 else pB)[:, :].rearrange("p (h c) -> p h c", h=4),
                               ACT.Copy).then_inc(wkT_ready, 1)
            for k in range(KK):
                act.wait_ge(xnT_ps, 2 * KK + k + 1)
                act.activation(xq16[:, 0, k, :], bank[2 + k][:, 0:TOK], ACT.Copy).then_inc(xnT_ready, 1)
            for m in range(H + 2):
                if m < H:
                    act.wait_ge(qT_ps, 16 + m + 1)
                    if m >= HU:
                        act.wait_ge(qk_ps, H + m - HU + 1)
                    act.activation(qT[1][:, m % HU, :], bank[m % 2][:, 0:TOK], ACT.Copy).then_inc(qT_ready, 1)
                if m >= 2:
                    fold_hi_head(1, (m - 2) // HU, (m - 2) % HU)

            def step1(b, g, mb, slot, n):
                a, u = at[1], 2 * b + g
                if g == 0:
                    act.wait_ge(mbias_ready, b + 1)
                for t in range(KT):
                    if n >= 3 and t % EXPG == 0:
                        wait_used(act, 1, u - 3, t // EXPG)
                    act.wait_ge(a.raw, u * KT + t + 1)
                    act.activation(tiles(slot)[:, t, :], raw_bank(1, t), ACT.Identity,
                                   bias=mbias[:, mb, t:t + 1], scale=float(HD) ** -0.5).then_inc(a.score, 1)
                    c = (t // EXPG + 2) % NC
                    v, sv, nv = (u - 2, (slot + 1) % 3, n - 2) if t // EXPG < 2 else (u - 1, (slot + 2) % 3, n - 1)
                    if nv >= 0:
                        if t % EXPG == 0:
                            exponential(1, v, sv, c)
                        if t % EXPG == 1:
                            high_half(1, v, sv, c, nv == 0)
            for u in range(4):
                step1(u // 2, u % 2, u // 2, slot_of(1, u), u)
            with act.Fori(0, 2) as i:
                for k in range(6):
                    step1(3 * i + 2 + k // 2, k % 2, (2 + k // 2) % 3, slot_of(1, 4 + k), 9)
            for c in range(2, NC):
                exps(1, NU - 2, slot_of(1, NU - 2), c)
            for c in range(NC):
                exps(1, NU - 1, slot_of(1, NU - 1), c)
            project(1)

            for k in range(KK):
                act.wait_ge(xnT_ps, 3 * KK + k + 1)
                act.activation(xnT[:, k, :], bank[2 + k][:, 0:TOK], ACT.Copy).then_inc(xnT_ready, 1)
            for k in range(KK):
                act.activation(xnT16[:, 0, k, :], bank[2 + k][:, 0:TOK], ACT.Copy).then_inc(xn_hi, 1)
            act.wait_ge(lg_sub, 1)
            act.activation(ex, lg, ACT.Exp).then_inc(lg_exp, 1)

            def hidden_hi(s):
                n, rows = CHUNKS[s], chunk_rows(CHUNKS[s])
                act.wait_ge(moeh, s + 1)
                act.activation(h16[0:rows, 0, n, :], hprod[0:rows, s % 2, :], ACT.Copy).then_inc(moeh_hi, 1)
            for s, n in enumerate(CHUNKS):
                rows = chunk_rows(n)
                act.wait_ge(gu_ps, s + 1)
                wait(act, moeh, s - 1)
                act.activation(sil[0:rows, s % 2, :], bank[2 * (s % 2)][0:rows, 0:TOK], ACT.Silu).then_inc(silu, 1)
                if s == 1:
                    act.wait_ge(combT_ps, 1)
                    act.activation(combT16[:, 0, :], praw[0:E, 0, 0:TOK], ACT.Copy, scale=HSCALE).then_inc(combT_hi, 1)
                if s > 0:
                    hidden_hi(s - 1)
            hidden_hi(NHC - 1)

        @block.vector
        def _(dve):
            links = [0]

            def link(ins):
                links[0] += 1
                ins.then_inc(chain, 1)
                dve.wait_ge(chain, links[0])

            def normalise(n, src, dst, eps, ready, extremes=False, find=False):
                for j in range(NT):
                    s = dve.bn_stats(stats[:, j, 0, :], src[:, j, :])
                link(s)
                for j in range(NT):
                    s = dve.bn_aggr(mv[:, j, :], stats[:, j, 0, :])
                link(s)
                dve.tensor_scalar(lnv[:, :], mv[:, :, 1], eps, None, ALU.add).then_inc(ln_var, 1)
                if find:
                    for j in range(NT):
                        s = row_extremes(src, j)
                    link(s)
                dve.wait_ge(ln_rstd, n + 1)
                for j in range(NT):
                    s = dve.tensor_scalar(dst[:, j, :], src[:, j, :], mv[:, j, 0:1], lnr[:, j:j + 1],
                                          ALU.subtract, ALU.mult)
                    if ready is not None:
                        s.then_inc(ready, 1)
                if extremes:
                    for j in range(NT):
                        s = dve.tensor_scalar(ext[:, j, :], ext[:, j, :], mv[:, j, 0:1], lnr[:, j:j + 1],
                                              ALU.subtract, ALU.mult)
                if ready is None:
                    link(s)

            def row_extremes(src, j):
                dve.tensor_reduce(ext[:, j, 0:1], src[:, j, :], AX.X, ALU.max)
                return dve.tensor_reduce(ext[:, j, 1:2], src[:, j, :], AX.X, ALU.min)

            dve.wait_ge(ld_x, 16)
            normalise(0, x_sb, xn, 1e-5, xn_ready)
            dve.wait_ge(ld_g, 32)
            dve.tensor_tensor(g2[:, 2:3], g2[:, 0:1], g2[:, 1:2], ALU.mult).then_inc(g_ready, 1)
            dve.wait_ge(g_ready, 1)
            for q in range(4):
                dve.wait_ge(wkT_ps, q + 1)
                dve.tensor_scalar(wkT[0][:, 4 * q:4 * q + 4, :], bank[q % 2].rearrange("p (h c) -> p h c", h=4),
                                  g2[:, 2:3], None, ALU.mult).then_inc(wkT_ready, 1)
            dve.wait_ge(wk_hi, 1)
            dve.scalar_tensor_tensor(out=wk16[:, 1, :], in0=wk_sb, scalar=16.0, in1=wk16[:, 0, :],
                                     op0=ALU.mult, op1=ALU.subtract).then_inc(wk_lo, 1)
            def context_lo(b, quads):
                for q in quads:
                    n = 3 * b + q
                    dve.wait_ge(ctxT_hi, n + 1)
                    dve.tensor_tensor(ctxT[:, 1, b, 4 * q:4 * q + 4, :].rearrange("p t n -> p (t n)"),
                                      praw[:, n % 2, 0:4 * KP],
                                      ctxT[:, 0, b, 4 * q:4 * q + 4, :].rearrange("p t n -> p (t n)"),
                                      ALU.subtract).then_inc(ctxT_lo, 1)

            def fold_lo_head(l, g, i):
                n = l * H + g * HU + i
                dve.wait_ge(qk_hi, n + 1)
                dve.tensor_tensor(qk[:, :, g, 1, i * SQ:(i + 1) * SQ],
                                  fold_bank(n).rearrange("p (b q) -> p b q", b=B),
                                  qk[:, :, g, 0, i * SQ:(i + 1) * SQ], ALU.subtract).then_inc(qk_lo, 1)

            def fold_lo(l, g):
                for i in range(HU):
                    fold_lo_head(l, g, i)

            def q_stats(i):
                dve.wait_ge(q_sq, i + 1)
                link(dve.tensor_reduce(qss[:, :], qsq.rearrange("p (h d) -> p h d", h=HU), AX.X, ALU.add))
                dve.tensor_scalar(qvar[:, :], qss[:, :], 1.0 / HD, 1e-5, ALU.mult, ALU.add).then_inc(q_var, 1)
            q_stats(0)
            for i in range(2 * NT):
                dve.wait_ge(q_rstd, i + 1)
                wait(dve, qT_ps, 2 * i)
                dve.tensor_tensor(qn.rearrange("p (h d) -> p h d", h=HU),
                                  pk[0:TP, i % 2, :].rearrange("p (h d) -> p h d", h=HU),
                                  qrstd[:, :].unsqueeze(2).broadcast_to([TP, HU, HD]),
                                  ALU.mult).then_inc(qn_ready, 1)
                context_lo(i, (0, 1))
                if i + 1 < 2 * NT:
                    q_stats(i + 1)
                context_lo(i, (2,))
                if i == NT - 1:
                    fold_lo(0, 0)
            dve.wait_ge(ld_mask, 16)
            dve.tensor_copy(mask_f[:, :, :], mask_u8[:, :, :]).then_inc(mask_ready, 1)
            dve.wait_ge(mask_ready, 1)
            dve.tensor_scalar(half_bias[:, 0:B, :], mask_f[:, :, :], -NEG / 2, NEG / 2, ALU.mult,
                              ALU.add).then_inc(mask_ready, 1)

            def key_sum(u, t):
                dve.wait_ge(k_sq, u * KT + t + 1)
                dve.tensor_reduce(ssq[:, t, :], sq[0:KP, t % 2, :].rearrange("p (h d) -> p h d", h=HU),
                                  AX.X, ALU.add).then_inc(k_red, 1)

            def key_var(u, r):
                v = ssq[:, r * KR:(r + 1) * KR, :]
                dve.wait_ge(k_red, KT * u + KR * (r + 1))
                dve.tensor_scalar(v, v, 1.0 / 256.0, HD * 1e-5, ALU.mult, ALU.add).then_inc(k_var, 1)

            def max_step(l, u, slot, t):
                a = at[l]
                s = tiles(slot)
                dve.wait_ge(a.score, u * KT + t + 1)
                if t > 1:
                    dve.wait_ge(a.mstep, u * (KT - 1) + t - 1)
                else:
                    wait(dve, a.maccT, u)
                dve.tensor_tensor(macc[:, :], s[:, 0, :] if t == 1 else macc[:, :], s[:, t, :],
                                  ALU.max).then_inc(a.mstep, 1)

            def max_col(l, u):
                a = at[l]
                dve.wait_ge(a.maccT, u + 1)
                dve.tensor_reduce(mcol[:, :], pA[0:TP, 0:QJ * KP].rearrange("p (j s) -> p j s", j=QJ), AX.X,
                                  ALU.max).then_inc(a.mcol, 1)

            def subtract(l, u, slot, c):
                a = at[l]
                if c == 0:
                    dve.wait_ge(a.mbc, u + 1)
                s = chunk(slot, c)
                dve.tensor_tensor(s, s, pB[0:KP, 0:QU].unsqueeze(1).broadcast_to([KP, EXPG, QU]),
                                  ALU.subtract).then_inc(a.sub, 1)

            def finish(l, b, g, pv, den):
                a, u = at[l], 2 * b + g
                dve.wait_ge(a.den, (NC - NSC) * (u + 1))
                if isinstance(u, int):
                    wait(dve, a.ac, u)
                dve.reciprocal(rden, den).then_inc(a.rden, 1)
                dve.wait_ge(a.rden, u + 1)
                dve.tensor_tensor(acT[:, b, g, :], pv, rden, ALU.mult).then_inc(a.ac, 1)

            def key_newton(u, r):
                i, ts = 2 * u + r, slice(r * KR, (r + 1) * KR)
                r0, t, v = krstd[:, ts, :], ktmp[:, ts, :], ssq[:, ts, :]
                dve.wait_ge(k_r0, i + 1)
                dve.scalar_tensor_tensor(out=t, in0=r0, scalar=-0.5, in1=r0, op0=ALU.mult,
                                         op1=ALU.mult).then_inc(k_newton, 1)
                dve.wait_ge(k_newton, 2 * i + 1)
                dve.tensor_tensor(t, t, v, ALU.mult).then_inc(k_newton, 1)
                dve.wait_ge(k_newton, 2 * i + 2)
                dve.scalar_tensor_tensor(out=r0, in0=t, scalar=1.5, in1=r0, op0=ALU.add,
                                         op1=ALU.mult).then_inc(k_rstd, 1)

            for t in range(KT):
                if 2 <= t < 2 + HU:
                    fold_lo_head(0, 1, t - 2)
                key_sum(0, t)
            for r in range(2):
                key_var(0, r)
            key_newton(0, 0)

            def step0(b, g, n):
                a, u = at[0], 2 * b + g
                s = tiles(slot_of(0, g)).rearrange("p t (h q) -> p t h q", h=HU)
                if n == 0:
                    dve.wait_ge(qT_ps, 4 * NT)
                    dve.wait_ge(qk_ps, H)
                for t in range(KT):
                    if t == 0:
                        dve.wait_ge(k_rstd, 2 * u + 1)
                    if t == KR:
                        key_newton(u, 1)
                        dve.wait_ge(k_rstd, 2 * u + 2)
                    if n not in (0, 1) and t % EXPG == 0:
                        wait_used(dve, 0, u - 2, t // EXPG)
                    dve.wait_ge(a.raw, u * KT + t + 1)
                    dve.tensor_tensor(s[:, t, :, :], raw_bank(0, t).rearrange("p (h q) -> p h q", h=HU),
                                      krstd[:, t, :].unsqueeze(2).broadcast_to([KP, HU, SQ]),
                                      ALU.mult).then_inc(a.score, 1)
                    if n != 0 and t == 0:
                        max_col(0, u - 1)
                if n not in (0, 1):
                    finish(0, b - 1, g, PV0, DEN0)
                    dve.wait_ge(a.ac, u - 1)
                for t in range(KT):
                    if n != -1:
                        key_sum(u + 1, t)
                        if t == KR - 1:
                            key_var(u + 1, 0)
                    if 0 < t < KT - LATE:
                        max_step(0, u, slot_of(0, g), t)
                if n != -1:
                    key_var(u + 1, 1)
                for t in range(KT - LATE, KT):
                    max_step(0, u, slot_of(0, g), t)
                if n != -1:
                    key_newton(u + 1, 0)
            for g in range(2):
                step0(0, g, g)
            with dve.Fori(1, B - 1) as b:
                for g in range(2):
                    step0(b, g, None)
            step0(B - 1, 0, None)
            step0(B - 1, 1, -1)
            max_col(0, NU - 1)
            last = slot_of(0, 1)
            dve.wait_ge(at[0].mbc, NU)
            for c in range(NC):
                dve.tensor_tensor(chunk(last, c), chunk(last, c),
                                  pA[0:KP, 0:QU].unsqueeze(1).broadcast_to([KP, EXPG, QU]),
                                  ALU.subtract).then_inc(last_sub, 1)
            for c in range(NC):
                dve.wait_ge(at[0].hi, NC * (NU - 1) + c + 1)
                if c < NSC:
                    dve.wait_ge(at[0].dsum, (NSC * EXPG - 1) * (NU - 1) + c * EXPG + EXPG - 1)
                dve.tensor_tensor(p_lo(last, c), chunk(last, c), p_hi(0, last, c), ALU.subtract).then_inc(last_lo, 1)

            def wo_lows(l, q):
                dve.wait_ge(at[l].wo, q + 1)
                dve.scalar_tensor_tensor(out=wo_l16(l, q), in0=wo_part(l, q), scalar=WOS,
                                         in1=wo_h16[l][:, WQ * q:WQ * (q + 1), :],
                                         op0=ALU.mult, op1=ALU.subtract).then_inc(at[l].wo_l, 1)
            finish(0, B - 1, 0, PV0, DEN0)
            finish(0, B - 1, 1, PV_LAST, DEN_LAST)
            wo_lows(0, 0)
            wo_lows(0, 1)

            def values_lo(l, h):
                dve.wait_ge(at[l].oT, h + 1)
                dve.tensor_tensor(oT[l][:, 1, h % 2, :], praw[:, h % 2, 0:TOK], oT[l][:, 0, h % 2, :],
                                  ALU.subtract).then_inc(at[l].oT_lo, 1)
                if h in (1, 3):
                    wo_lows(l, 2 + h // 2)

            def residual(l):
                dve.wait_ge(at[l].y, 1)
                for j in range(NT):
                    dve.scalar_tensor_tensor(out=x_sb[:, j, :], in0=bank[j][0:TP, 0:DM], scalar=1.0 / WOS,
                                             in1=x_sb[:, j, :], op0=ALU.mult, op1=ALU.add).then_inc(at[l].x, 1)
                dve.wait_ge(at[l].x, NT)
            for h in range(HU + 1):
                values_lo(0, h)
            dve.wait_ge(wsum_ps, 1)
            inv = 1.0 / float(FF * DM)
            dve.tensor_scalar(gam[:, :], pA[:, 0:2], inv, None, ALU.mult).then_inc(gam_ready, 1)
            dve.wait_ge(gam_ready, 1)
            dve.tensor_scalar(thr[:, 0, :], gam[:, :], 1e-6, 0.5, ALU.add, ALU.mult)
            link(dve.tensor_scalar(thr[:, 1, :], gam[:, :], 1e-6, -0.5, ALU.add, ALU.mult))
            for i, (w, tt) in enumerate(((wfc_sb, t_fc), (wpj_sb, t_pj))):
                w2, t2 = w.rearrange("p o d -> p (o d)"), tt.rearrange("p o d -> p (o d)")
                wait(dve, tern, i)
                link(dve.tensor_scalar(tneg, w2, thr[:, 1, i:i + 1], None, ALU.is_lt))
                values_lo(0, HU + 1 + 3 * i)
                dve.scalar_tensor_tensor(out=t2, in0=w2, scalar=thr[:, 0, i:i + 1], in1=tneg,
                                         op0=ALU.is_gt, op1=ALU.subtract).then_inc(tern, 1)
                values_lo(0, HU + 2 + 3 * i)
                values_lo(0, HU + 3 + 3 * i)
            values_lo(0, H - 1)
            residual(0)


            def clip_absmax(src, j, ready):
                dve.tensor_scalar(src[:, j, :], src[:, j, :], amx[:, j:j + 1], namx[:, j:j + 1],
                                  ALU.min, ALU.max).then_inc(ready, 1)

            def absmax(js):
                link(dve.scalar_tensor_tensor(out=amx[:, js], in0=ext[:, js, 1], scalar=-1.0, in1=ext[:, js, 0],
                                              op0=ALU.mult, op1=ALU.max))
                link(dve.tensor_scalar(namx[:, js], amx[:, js], -1.0, None, ALU.mult))

            normalise(1, x_sb, xn, 1e-5, None, extremes=True, find=True)
            normalise(2, xn, xn, 1e-6, None, extremes=True)
            absmax(slice(0, NT))
            for j in range(NT):
                clip_absmax(xn, j, z_ready)
            for k in range(KK):
                dve.wait_ge(zT_hi, k + 1)
                dve.tensor_tensor(zT[:, 1, k, :], bank[2 + k][:, 0:TOK], zT[:, 0, k, :],
                                  ALU.subtract).then_inc(zT_lo, 1)
            def hidden_stats(j):
                dve.wait_ge(h_act, j + 1)
                for n in range(2):
                    s = dve.bn_stats(stats[:, j, n, :], hbuf[:, j, n * 512:(n + 1) * 512])
                link(s)
                row_extremes(hbuf, j)
                link(dve.bn_aggr(mv[:, j, :], stats[:, j, :, :]))
                dve.tensor_scalar(lnv[:, j:j + 1], mv[:, j, 1:2], 1e-6, None, ALU.add).then_inc(h_var, 1)

            def hidden_lo(j):
                for r in range(2):
                    dve.wait_ge(hT_hi, 2 * j + r + 1)
                    o = slice(4 * r, 4 * r + 4)
                    dve.tensor_tensor(hT16[:, 1, o, j * TP:(j + 1) * TP],
                                      praw[:, r, 0:TOK].rearrange("p (o t) -> p o t", o=4),
                                      hT16[:, 0, o, j * TP:(j + 1) * TP], ALU.subtract).then_inc(hT_lo, 1)
            hidden_stats(0)
            for j in range(NT):
                if j + 1 < NT:
                    hidden_stats(j + 1)
                dve.wait_ge(h_rstd, j + 1)
                dve.tensor_scalar(hbuf[:, j, :], hbuf[:, j, :], mv[:, j, 0:1], lnr[:, j:j + 1],
                                  ALU.subtract, ALU.mult)
                link(dve.tensor_scalar(ext[:, j, :], ext[:, j, :], mv[:, j, 0:1], lnr[:, j:j + 1],
                                       ALU.subtract, ALU.mult))
                absmax(slice(j, j + 1))
                clip_absmax(hbuf, j, h_ready)
                if j > 0:
                    hidden_lo(j - 1)
            hidden_lo(NT - 1)
            for j in range(NT):
                dve.wait_ge(f_ps, j + 1)
                dve.scalar_tensor_tensor(out=x_sb[:, j, :], in0=bank[j][0:TP, 0:DM], scalar=gam[0:TP, 1:2],
                                         in1=x_sb[:, j, :], op0=ALU.mult, op1=ALU.add).then_inc(f_done, 1)
            dve.wait_ge(f_done, NT)

            normalise(3, x_sb, xn, 1e-5, xn_ready)
            for k in range(KK):
                dve.wait_ge(xnT_ready, KK + k + 1)
                dve.tensor_tensor(xq16[:, 1, k, :], bank[2 + k][:, 0:TOK], xq16[:, 0, k, :],
                                  ALU.subtract).then_inc(xn_lo, 1)
            for g in range(2):
                fold_lo(1, g)

            def step1(b, g, slot, n):
                u = 2 * b + g
                if n >= 2:
                    subtract(1, u - 2, (slot + 1) % 3, NC - 1)
                if n >= 1:
                    max_col(1, u - 1)
                if n >= 3:
                    bf, gf = (b - 1, 0) if g == 1 else (b - 2, 1)
                    finish(1, bf, gf, bank[gf][:, 0:QU], DEN1)
                    dve.wait_ge(at[1].ac, u - 2)
                for t in range(1, KT):
                    max_step(1, u, slot, t)
                    if t in (2, 5, 8) and n >= 1:
                        subtract(1, u - 1, (slot + 2) % 3, t // EXPG)
            for u in range(4):
                step1(u // 2, u % 2, slot_of(1, u), u)
            with dve.Fori(0, 2) as i:
                for k in range(6):
                    step1(3 * i + 2 + k // 2, k % 2, slot_of(1, 4 + k), 9)
            subtract(1, NU - 2, slot_of(1, NU - 2), NC - 1)
            max_col(1, NU - 1)
            finish(1, B - 2, 1, bank[1][:, 0:QU], DEN1)
            for c in range(NC):
                subtract(1, NU - 1, slot_of(1, NU - 1), c)
            finish(1, B - 1, 0, bank[0][:, 0:QU], DEN1)
            wo_lows(1, 0)
            wo_lows(1, 1)
            finish(1, B - 1, 1, bank[1][:, 0:QU], DEN1)
            for h in range(H):
                values_lo(1, h)
                if h in WSTEPS:
                    i = WSTEPS.index(h)
                    w, hi, lo = pieces[i]
                    dve.wait_ge(w_hi, NWQ + i + 1)
                    dve.tensor_tensor(lo, w, hi, ALU.subtract).then_inc(w_lo, 1)
            residual(1)

            normalise(4, x_sb, xn, 1e-5, xn_ready)
            dve.wait_ge(gwT_ps, 1)
            dve.tensor_copy(gwT, pA[:, 0:KK * E].rearrange("p (k e) -> p k e", k=KK)).then_inc(gwT_ready, 1)
            for k in range(KK):
                dve.wait_ge(xn_hi, k + 1)
                dve.tensor_tensor(xnT16[:, 1, k, :], bank[2 + k][:, 0:TOK], xnT16[:, 0, k, :],
                                  ALU.subtract).then_inc(xn_lo, 1)
            dve.wait_ge(lg_ps, 1)
            pl = pB[0:TP, 0:NT * E].rearrange("p (j e) -> p j e", j=NT)
            link(dve.tensor_reduce(rmx, pl, AX.X, ALU.max))
            dve.tensor_tensor(lg, pl, rmx.unsqueeze(2).broadcast_to([TP, NT, E]), ALU.subtract).then_inc(lg_sub, 1)
            dve.wait_ge(lg_exp, 1)
            link(dve.tensor_reduce(rsm, ex, AX.X, ALU.add))
            link(dve.reciprocal(rsm, rsm))
            link(dve.tensor_tensor(lg, ex, rsm.unsqueeze(2).broadcast_to([TP, NT, E]), ALU.mult))
            other = lg.unsqueeze(2).broadcast_to([TP, NT, E, E])
            own = lg.unsqueeze(3).broadcast_to([TP, NT, E, E])
            dve.tensor_tensor(gt, other, own, ALU.is_gt)
            link(dve.tensor_tensor(eq, other, own, ALU.is_equal))
            dve.wait_ge(tri_ready, 1)
            link(dve.tensor_tensor(eq, eq, tri.unsqueeze(1).broadcast_to([TP, NT, E, E]), ALU.mult))
            link(dve.tensor_tensor(gt, gt, eq, ALU.add))
            link(dve.tensor_reduce(rank, gt, AX.X, ALU.add))
            dve.scalar_tensor_tensor(out=comb, in0=rank, scalar=1.5, in1=lg, op0=ALU.is_lt,
                                     op1=ALU.mult).then_inc(comb_ready, 1)
            for s, n in enumerate(CHUNKS):
                rows = chunk_rows(n)
                dve.wait_ge(silu, s + 1)
                wait(dve, moeh_lo, s - 1)
                hp = hprod[0:rows, s % 2, :]
                dve.tensor_tensor(hp, sil[0:rows, s % 2, :], bank[2 * (s % 2) + 1][0:rows, 0:TOK],
                                  ALU.mult).then_inc(moeh if s < NSH else glu, 1)
                if s >= NSH:
                    dve.wait_ge(wt_ps, s - NSH + 1)
                    dve.wait_ge(glu, s - NSH + 1)
                    dve.tensor_tensor(hp, hp, praw[:, s % 2, 0:TOK], ALU.mult).then_inc(moeh, 1)
                if s == 1:
                    dve.wait_ge(combT_hi, 1)
                    dve.scalar_tensor_tensor(out=combT16[:, 1, :], in0=praw[0:E, 0, 0:TOK], scalar=HSCALE,
                                             in1=combT16[:, 0, :], op0=ALU.mult, op1=ALU.subtract).then_inc(combT_lo, 1)
            for j in range(NT):
                dve.wait_ge(ye_ps, j // 2 + 1)
                dve.tensor_tensor(x_sb[:, j, :], ye[j], x_sb[:, j, :], ALU.add).then_inc(ye_used, 1)


_INS = ['x', 'ctx_1024', 'mask_BxS2_bf1', 'L0_xattn_Wq', 'L0_xattn_Wk', 'L0_xattn_Wv', 'L0_xattn_Wo',
        'L0_xattn_gq', 'L0_xattn_gk', 'L0_ffn_w_fc', 'L0_ffn_w_proj', 'L1_xattn_Wq', 'L1_xattn_Wk',
        'L1_xattn_Wv', 'L1_xattn_Wo', 'L1_ffn_gate_w', 'L1_ffn_w_gate', 'L1_ffn_w_up', 'L1_ffn_w_down',
        'L1_ffn_sw_gate', 'L1_ffn_sw_up', 'L1_ffn_sw_down']


def kernel(**inputs):
    import numpy as _np
    import concourse.bacc as _bacc
    from concourse import mybir as _mybir
    from concourse.bass_utils import run_bass_kernel_spmd as _run

    nc = _bacc.Bacc("TRN2", target_bir_lowering=False, num_devices=1)
    arrays, args = {}, []
    for name in _INS:
        a = _np.ascontiguousarray(inputs[name])
        if a.dtype == _np.bool_:
            a = a.view(_np.uint8)
        arrays[f"in_{name}_dram"] = a
        args.append(nc.dram_tensor(f"in_{name}_dram", a.shape, _mybir.dt.from_np(a.dtype), kind="ExternalInput").ap())
    out = nc.dram_tensor("out_dram", (B, SQ, DM), F32, kind="ExternalOutput").ap()
    build(nc, *args, out)
    r = _run(nc, [arrays], core_ids=[0])
    return r.results[0]["out_dram"]
```
